# Optimizing a Trainium2 kernel written in Bass

```python
import numpy as np
import jax
import jax.numpy as jnp

def _softmax(x, axis=-1):
    return jax.nn.softmax(x, axis=axis)

def _gelu(x):
    return jax.nn.gelu(x, approximate=True)

def _silu(x):
    return jax.nn.silu(x)

def _sigmoid(x):
    return jax.nn.sigmoid(x)

def _layernorm(x, axis=-1, eps=1e-05):
    m = jnp.mean(x, axis=axis, keepdims=True)
    v = jnp.var(x, axis=axis, keepdims=True)
    return (x - m) / jnp.sqrt(v + eps)

def _scatter_add(tgt, idx, src, axis=0):
    return tgt.at[idx].add(src)

def _segment_sum(src, seg, n):
    return jax.ops.segment_sum(src, seg, n)
kernel_name = 'mk_seq_postln_d2_jaxref_r4_ad9d0a'

def setup_inputs(seed: int=0):
    np.random.seed(seed)
    _w = jnp.asarray

    def _L0_attn_setup():
        import jax, jax.numpy as jnp
        import numpy as np
        EPS = 1e-05
        N_HEADS, KV_HEADS = (16, 4)

        def layernorm(x, g, b):
            m = jnp.mean(x, -1, keepdims=True)
            v = jnp.var(x, -1, keepdims=True)
            return (x - m) / jnp.sqrt(v + EPS) * g + b

        def mamba_block(x, ln_g, ln_b, in_w, conv_w, conv_b, xp_w, dt_w, dt_b, A_log, D_skip, out_w):
            Bsz, L, _ = x.shape
            d_inner = D_skip.shape[0]
            d_conv = conv_w.shape[-1]
            res = x
            h = layernorm(x, ln_g, ln_b)
            xs, gate = jnp.split(h @ in_w, 2, axis=-1)
            xc = jnp.pad(xs.transpose(0, 2, 1), ((0, 0), (0, 0), (d_conv - 1, 0)))
            xc = jax.lax.conv_general_dilated(xc, conv_w, (1,), 'VALID', dimension_numbers=('NCH', 'OIH', 'NCH'), feature_group_count=d_inner)
            xs = jax.nn.silu(xc.transpose(0, 2, 1) + conv_b)
            Bm, Cm = jnp.split(xs @ xp_w, 2, axis=-1)
            dt = jax.nn.softplus(Bm @ dt_w + dt_b)
            A = -jnp.exp(A_log)

            def step(hst, inp):
                xt, dtt, Bt, Ct = inp
                dA = jnp.exp(dtt[..., None] * A)
                hst = hst * dA + dtt[..., None] * Bt[:, None, :] * xt[..., None]
                yt = jnp.sum(hst * Ct[:, None, :], -1)
                return (hst, yt)
            h0 = jnp.zeros((Bsz, d_inner, A.shape[-1]), xs.dtype)
            _, y = jax.lax.scan(step, h0, (xs.transpose(1, 0, 2), dt.transpose(1, 0, 2), Bm.transpose(1, 0, 2), Cm.transpose(1, 0, 2)))
            y = y.transpose(1, 0, 2)
            y = (y + D_skip * xs) * jax.nn.silu(gate)
            return y @ out_w + res

        def attn_block(x, ln_g, ln_b, q_w, k_w, v_w, o_w):
            Bsz, L, D = x.shape
            H, KV = (N_HEADS, KV_HEADS)
            dh = D // H
            res = x
            h = layernorm(x, ln_g, ln_b)
            q = (h @ q_w).reshape(Bsz, L, H, dh).transpose(0, 2, 1, 3)
            k = (h @ k_w).reshape(Bsz, L, KV, dh).transpose(0, 2, 1, 3)
            v = (h @ v_w).reshape(Bsz, L, KV, dh).transpose(0, 2, 1, 3)
            inv = 1.0 / 10000.0 ** (jnp.arange(0, dh, 2, dtype=jnp.float32) / dh)
            fr = jnp.arange(L, dtype=jnp.float32)[:, None] * inv
            emb = jnp.concatenate([fr, fr], -1)
            cos, sin = (jnp.cos(emb), jnp.sin(emb))

            def rot(t):
                t1, t2 = jnp.split(t, 2, -1)
                return jnp.concatenate([-t2, t1], -1)
            q = q * cos + rot(q) * sin
            k = k * cos + rot(k) * sin
            g = H // KV
            k = jnp.repeat(k, g, axis=1)
            v = jnp.repeat(v, g, axis=1)
            sc = jnp.einsum('bhqd,bhkd->bhqk', q, k) / jnp.sqrt(jnp.float32(dh))
            mask = jnp.where(jnp.tril(jnp.ones((L, L), bool)), 0.0, -1000000000.0)
            p = jax.nn.softmax((sc + mask).astype(jnp.float32), -1).astype(q.dtype)
            o = jnp.einsum('bhqk,bhkd->bhqd', p, v).transpose(0, 2, 1, 3).reshape(Bsz, L, D)
            return o @ o_w + res
        key = jax.random.key(seed)
        B, L, D = (4, 256, 256)
        d_inner, d_state, d_conv = (512, 16, 4)
        H, KV, dh = (N_HEADS, KV_HEADS, D // N_HEADS)
        dff = 1024
        ks = jax.random.split(key, 16)
        w = lambda k, shape: jax.random.normal(k, shape, jnp.float32) * 0.02
        return {'x': jax.random.normal(ks[0], (B, L, D), jnp.float32), 'ln1_g': jnp.ones(D), 'ln1_b': jnp.zeros(D), 'in_proj_w': w(ks[1], (D, 2 * d_inner)), 'conv_w': w(ks[2], (d_inner, 1, d_conv)), 'conv_b': jnp.zeros(d_inner), 'x_proj_w': w(ks[3], (d_inner, 2 * d_state)), 'dt_proj_w': w(ks[4], (d_state, d_inner)), 'dt_proj_b': jnp.zeros(d_inner), 'A_log': jnp.log(jnp.tile(jnp.arange(1, d_state + 1, dtype=jnp.float32), (d_inner, 1))), 'D_skip': jnp.ones(d_inner), 'out_proj_w': w(ks[5], (d_inner, D)), 'ln2_g': jnp.ones(D), 'ln2_b': jnp.zeros(D), 'q_w': w(ks[6], (D, H * dh)), 'k_w': w(ks[7], (D, KV * dh)), 'v_w': w(ks[8], (D, KV * dh)), 'o_w': w(ks[9], (H * dh, D)), 'ln3_g': jnp.ones(D), 'ln3_b': jnp.zeros(D), 'w1': w(ks[10], (D, dff)), 'w2': w(ks[11], (dff, D)), 'w3': w(ks[12], (D, dff))}
    _L0_attn_in = _L0_attn_setup()

    def _L0_ffn_setup():
        import jax, jax.numpy as jnp
        import numpy as np
        LN_EPS = 1e-05

        def layer_norm(x, g, b):
            mu = jnp.mean(x, axis=-1, keepdims=True)
            var = jnp.var(x, axis=-1, keepdims=True)
            return (x - mu) / jnp.sqrt(var + LN_EPS) * g + b

        def balanced_assignment(scores):
            T, E = scores.shape
            C = T // E
            taken = jnp.zeros((T,), dtype=bool)
            parts = []
            for e in range(E):
                s = jnp.where(taken, -jnp.inf, scores[:, e])
                _, idx = jax.lax.top_k(s, C)
                parts.append(idx)
                taken = taken.at[idx].set(True)
            return jnp.concatenate(parts)
        key = jax.random.key(seed)
        ks = jax.random.split(key, 4)
        B, S, D, F, E = (4, 512, 256, 1024, 8)
        return {'x': jax.random.normal(ks[0], (B, S, D), dtype=jnp.float32), 'centroids': jax.random.normal(ks[1], (E, D), dtype=jnp.float32) * 0.1, 'ln_g': jnp.ones((D,), dtype=jnp.float32), 'ln_b': jnp.zeros((D,), dtype=jnp.float32), 'w1': jax.random.normal(ks[2], (E, D, F), dtype=jnp.float32) * 0.02, 'b1': jnp.zeros((E, F), dtype=jnp.float32), 'w2': jax.random.normal(ks[3], (E, F, D), dtype=jnp.float32) * 0.02, 'b2': jnp.zeros((E, D), dtype=jnp.float32)}
    _L0_ffn_in = _L0_ffn_setup()

    def _L1_attn_setup():
        import jax, jax.numpy as jnp
        import numpy as np
        MAX_W, MIN_W = (120, 24)
        key = jax.random.key(seed)
        ks = jax.random.split(key, 11)
        B, S, D, H = (2, 512, 256, 16)
        hd = D // H
        s = 1.0 / float(np.sqrt(D))
        return {'x': jax.random.normal(ks[0], (B, S, D), jnp.float32), 'alpha': jnp.float32(0.1), 'Wq': jax.random.normal(ks[1], (D, D), jnp.float32) * s, 'bq': jnp.zeros((D,), jnp.float32), 'Wk': jax.random.normal(ks[2], (D, D), jnp.float32) * s, 'bk': jnp.zeros((D,), jnp.float32), 'Wv': jax.random.normal(ks[3], (D, D), jnp.float32) * s, 'bv': jnp.zeros((D,), jnp.float32), 'W_o': jax.random.normal(ks[4], (H, hd, hd), jnp.float32), 'Wfc': jax.random.normal(ks[5], (D, D), jnp.float32) * s, 'bfc': jnp.zeros((D,), jnp.float32)}
    _L1_attn_in = _L1_attn_setup()

    def _L1_ffn_setup():
        import jax, jax.numpy as jnp
        import numpy as np
        N_EMBD = 256
        N_STATE = 1024
        key = jax.random.key(seed)
        k_x, k_w1, k_b1, k_w2, k_b2 = jax.random.split(key, 5)
        x = jax.random.normal(k_x, (4, 512, N_EMBD), dtype=jnp.float32)
        w1 = jax.random.normal(k_w1, (N_EMBD, N_STATE), dtype=jnp.float32) * (1.0 / np.sqrt(N_EMBD))
        b1 = jax.random.normal(k_b1, (N_STATE,), dtype=jnp.float32) * 0.02
        w2 = jax.random.normal(k_w2, (N_STATE, N_EMBD), dtype=jnp.float32) * (1.0 / np.sqrt(N_STATE))
        b2 = jax.random.normal(k_b2, (N_EMBD,), dtype=jnp.float32) * 0.02
        return {'x': x, 'w1': w1, 'b1': b1, 'w2': w2, 'b2': b2}
    _L1_ffn_in = _L1_ffn_setup()
    _d = {'L0_attn_x': _L0_attn_in['x'], 'L0_attn_ln1_g': _L0_attn_in['ln1_g'], 'L0_attn_ln1_b': _L0_attn_in['ln1_b'], 'L0_attn_in_proj_w': _L0_attn_in['in_proj_w'], 'L0_attn_conv_w': _L0_attn_in['conv_w'], 'L0_attn_conv_b': _L0_attn_in['conv_b'], 'L0_attn_x_proj_w': _L0_attn_in['x_proj_w'], 'L0_attn_dt_proj_w': _L0_attn_in['dt_proj_w'], 'L0_attn_dt_proj_b': _L0_attn_in['dt_proj_b'], 'L0_attn_A_log': _L0_attn_in['A_log'], 'L0_attn_D_skip': _L0_attn_in['D_skip'], 'L0_attn_out_proj_w': _L0_attn_in['out_proj_w'], 'L0_attn_ln2_g': _L0_attn_in['ln2_g'], 'L0_attn_ln2_b': _L0_attn_in['ln2_b'], 'L0_attn_q_w': _L0_attn_in['q_w'], 'L0_attn_k_w': _L0_attn_in['k_w'], 'L0_attn_v_w': _L0_attn_in['v_w'], 'L0_attn_o_w': _L0_attn_in['o_w'], 'L0_attn_ln3_g': _L0_attn_in['ln3_g'], 'L0_attn_ln3_b': _L0_attn_in['ln3_b'], 'L0_attn_w1': _L0_attn_in['w1'], 'L0_attn_w2': _L0_attn_in['w2'], 'L0_attn_w3': _L0_attn_in['w3'], 'L0_ffn_centroids': _L0_ffn_in['centroids'], 'L0_ffn_ln_g': _L0_ffn_in['ln_g'], 'L0_ffn_ln_b': _L0_ffn_in['ln_b'], 'L0_ffn_w1': _L0_ffn_in['w1'], 'L0_ffn_b1': _L0_ffn_in['b1'], 'L0_ffn_w2': _L0_ffn_in['w2'], 'L0_ffn_b2': _L0_ffn_in['b2'], 'L1_attn_alpha': _L1_attn_in['alpha'], 'L1_attn_Wq': _L1_attn_in['Wq'], 'L1_attn_bq': _L1_attn_in['bq'], 'L1_attn_Wk': _L1_attn_in['Wk'], 'L1_attn_bk': _L1_attn_in['bk'], 'L1_attn_Wv': _L1_attn_in['Wv'], 'L1_attn_bv': _L1_attn_in['bv'], 'L1_attn_W_o': _L1_attn_in['W_o'], 'L1_attn_Wfc': _L1_attn_in['Wfc'], 'L1_attn_bfc': _L1_attn_in['bfc'], 'L1_ffn_w1': _L1_ffn_in['w1'], 'L1_ffn_b1': _L1_ffn_in['b1'], 'L1_ffn_w2': _L1_ffn_in['w2'], 'L1_ffn_b2': _L1_ffn_in['b2']}
    _x0 = _d['L0_attn_x']
    _d['L0_attn_x'] = jax.random.normal(jax.random.fold_in(jax.random.key(seed), 1), (2, 2048, 256), dtype=_x0.dtype)
    del _x0
    return _d

def reference(L0_attn_x, L0_attn_ln1_g, L0_attn_ln1_b, L0_attn_in_proj_w, L0_attn_conv_w, L0_attn_conv_b, L0_attn_x_proj_w, L0_attn_dt_proj_w, L0_attn_dt_proj_b, L0_attn_A_log, L0_attn_D_skip, L0_attn_out_proj_w, L0_attn_ln2_g, L0_attn_ln2_b, L0_attn_q_w, L0_attn_k_w, L0_attn_v_w, L0_attn_o_w, L0_attn_ln3_g, L0_attn_ln3_b, L0_attn_w1, L0_attn_w2, L0_attn_w3, L0_ffn_centroids, L0_ffn_ln_g, L0_ffn_ln_b, L0_ffn_w1, L0_ffn_b1, L0_ffn_w2, L0_ffn_b2, L1_attn_alpha, L1_attn_Wq, L1_attn_bq, L1_attn_Wk, L1_attn_bk, L1_attn_Wv, L1_attn_bv, L1_attn_W_o, L1_attn_Wfc, L1_attn_bfc, L1_ffn_w1, L1_ffn_b1, L1_ffn_w2, L1_ffn_b2):

    def _L0_attn_ref(x, ln1_g, ln1_b, in_proj_w, conv_w, conv_b, x_proj_w, dt_proj_w, dt_proj_b, A_log, D_skip, out_proj_w, ln2_g, ln2_b, q_w, k_w, v_w, o_w, ln3_g, ln3_b, w1, w2, w3):
        import jax, jax.numpy as jnp
        import numpy as np
        EPS = 1e-05
        N_HEADS, KV_HEADS = (16, 4)

        def layernorm(x, g, b):
            m = jnp.mean(x, -1, keepdims=True)
            v = jnp.var(x, -1, keepdims=True)
            return (x - m) / jnp.sqrt(v + EPS) * g + b

        def mamba_block(x, ln_g, ln_b, in_w, conv_w, conv_b, xp_w, dt_w, dt_b, A_log, D_skip, out_w):
            Bsz, L, _ = x.shape
            d_inner = D_skip.shape[0]
            d_conv = conv_w.shape[-1]
            res = x
            h = layernorm(x, ln_g, ln_b)
            xs, gate = jnp.split(h @ in_w, 2, axis=-1)
            xc = jnp.pad(xs.transpose(0, 2, 1), ((0, 0), (0, 0), (d_conv - 1, 0)))
            xc = jax.lax.conv_general_dilated(xc, conv_w, (1,), 'VALID', dimension_numbers=('NCH', 'OIH', 'NCH'), feature_group_count=d_inner)
            xs = jax.nn.silu(xc.transpose(0, 2, 1) + conv_b)
            Bm, Cm = jnp.split(xs @ xp_w, 2, axis=-1)
            dt = jax.nn.softplus(Bm @ dt_w + dt_b)
            A = -jnp.exp(A_log)

            def step(hst, inp):
                xt, dtt, Bt, Ct = inp
                dA = jnp.exp(dtt[..., None] * A)
                hst = hst * dA + dtt[..., None] * Bt[:, None, :] * xt[..., None]
                yt = jnp.sum(hst * Ct[:, None, :], -1)
                return (hst, yt)
            h0 = jnp.zeros((Bsz, d_inner, A.shape[-1]), xs.dtype)
            _, y = jax.lax.scan(step, h0, (xs.transpose(1, 0, 2), dt.transpose(1, 0, 2), Bm.transpose(1, 0, 2), Cm.transpose(1, 0, 2)))
            y = y.transpose(1, 0, 2)
            y = (y + D_skip * xs) * jax.nn.silu(gate)
            return y @ out_w + res

        def attn_block(x, ln_g, ln_b, q_w, k_w, v_w, o_w):
            Bsz, L, D = x.shape
            H, KV = (N_HEADS, KV_HEADS)
            dh = D // H
            res = x
            h = layernorm(x, ln_g, ln_b)
            q = (h @ q_w).reshape(Bsz, L, H, dh).transpose(0, 2, 1, 3)
            k = (h @ k_w).reshape(Bsz, L, KV, dh).transpose(0, 2, 1, 3)
            v = (h @ v_w).reshape(Bsz, L, KV, dh).transpose(0, 2, 1, 3)
            inv = 1.0 / 10000.0 ** (jnp.arange(0, dh, 2, dtype=jnp.float32) / dh)
            fr = jnp.arange(L, dtype=jnp.float32)[:, None] * inv
            emb = jnp.concatenate([fr, fr], -1)
            cos, sin = (jnp.cos(emb), jnp.sin(emb))

            def rot(t):
                t1, t2 = jnp.split(t, 2, -1)
                return jnp.concatenate([-t2, t1], -1)
            q = q * cos + rot(q) * sin
            k = k * cos + rot(k) * sin
            g = H // KV
            k = jnp.repeat(k, g, axis=1)
            v = jnp.repeat(v, g, axis=1)
            sc = jnp.einsum('bhqd,bhkd->bhqk', q, k) / jnp.sqrt(jnp.float32(dh))
            mask = jnp.where(jnp.tril(jnp.ones((L, L), bool)), 0.0, -1000000000.0)
            p = jax.nn.softmax((sc + mask).astype(jnp.float32), -1).astype(q.dtype)
            o = jnp.einsum('bhqk,bhkd->bhqd', p, v).transpose(0, 2, 1, 3).reshape(Bsz, L, D)
            return o @ o_w + res
        x = mamba_block(x, ln1_g, ln1_b, in_proj_w, conv_w, conv_b, x_proj_w, dt_proj_w, dt_proj_b, A_log, D_skip, out_proj_w)
        x = attn_block(x, ln2_g, ln2_b, q_w, k_w, v_w, o_w)
        h = layernorm(x, ln3_g, ln3_b)
        return x + jax.nn.silu(h @ w1) * (h @ w3) @ w2

    def _L0_ffn_ref(x, centroids, ln_g, ln_b, w1, b1, w2, b2):
        import jax, jax.numpy as jnp
        import numpy as np
        LN_EPS = 1e-05

        def layer_norm(x, g, b):
            mu = jnp.mean(x, axis=-1, keepdims=True)
            var = jnp.var(x, axis=-1, keepdims=True)
            return (x - mu) / jnp.sqrt(var + LN_EPS) * g + b

        def balanced_assignment(scores):
            T, E = scores.shape
            C = T // E
            taken = jnp.zeros((T,), dtype=bool)
            parts = []
            for e in range(E):
                s = jnp.where(taken, -jnp.inf, scores[:, e])
                _, idx = jax.lax.top_k(s, C)
                parts.append(idx)
                taken = taken.at[idx].set(True)
            return jnp.concatenate(parts)
        D = x.shape[-1]
        feat = x.reshape(-1, D)
        T = feat.shape[0]
        E = centroids.shape[0]
        C = T // E
        norm = layer_norm(feat, ln_g, ln_b)
        scores = jax.lax.stop_gradient(norm @ centroids.T)
        sort_by_expert = balanced_assignment(scores)
        routed = feat[sort_by_expert].reshape(E, C, D)
        h = layer_norm(routed, ln_g, ln_b)
        h = jax.nn.gelu(jnp.einsum('ecd,edf->ecf', h, w1) + b1[:, None, :])
        h = jnp.einsum('ecf,efd->ecd', h, w2) + b2[:, None, :]
        out = routed + h
        inv = jnp.zeros((T,), dtype=jnp.int32).at[sort_by_expert].set(jnp.arange(T, dtype=jnp.int32))
        return out.reshape(T, D)[inv].reshape(x.shape)

    def _L1_attn_ref(x, alpha, Wq, bq, Wk, bk, Wv, bv, W_o, Wfc, bfc):
        import jax, jax.numpy as jnp
        import numpy as np
        MAX_W, MIN_W = (120, 24)
        B, S, D = x.shape
        H, hd, _ = W_o.shape
        fluct = jnp.abs(x[:, -1] - x[:, -2])
        a = jax.nn.sigmoid(alpha)
        ewma_prev = fluct[0, 0]
        signal = a * fluct.mean() + (1.0 - a) * ewma_prev
        scale = jax.nn.sigmoid(signal)
        w = jnp.floor(MIN_W + (MAX_W - MIN_W) * scale).astype(jnp.int32)
        half = w // 2
        q = (x @ Wq + bq).reshape(B, S, H, hd).transpose(0, 2, 1, 3)
        k = (x @ Wk + bk).reshape(B, S, H, hd).transpose(0, 2, 1, 3)
        v = (x @ Wv + bv).reshape(B, S, H, hd).transpose(0, 2, 1, 3)
        inv_sqrt = 1.0 / float(np.sqrt(hd))
        scores = jnp.einsum('bhqd,bhkd->bhqk', q, k) * inv_sqrt
        idx = jnp.arange(S)
        band = jnp.abs(idx[:, None] - idx[None, :]) <= half
        scores = jnp.where(band[None, None], scores, -1e+30)
        attn = jax.nn.softmax(scores, axis=-1)
        out = jnp.einsum('bhqk,bhkd->bhqd', attn, v)
        out = jnp.einsum('bhqd,hdk->bhqk', out, W_o)
        out = out.transpose(0, 2, 1, 3).reshape(B, S, D)
        return out @ Wfc + bfc

    def _L1_ffn_ref(x, w1, b1, w2, b2):
        import jax, jax.numpy as jnp
        import numpy as np
        N_EMBD = 256
        N_STATE = 1024
        h = jax.nn.gelu(jnp.einsum('bse,eh->bsh', x, w1) + b1, approximate=False)
        return jnp.einsum('bsh,he->bse', h, w2) + b2
    x = L0_attn_x
    x = _layernorm(x + _L0_attn_ref(x, L0_attn_ln1_g, L0_attn_ln1_b, L0_attn_in_proj_w, L0_attn_conv_w, L0_attn_conv_b, L0_attn_x_proj_w, L0_attn_dt_proj_w, L0_attn_dt_proj_b, L0_attn_A_log, L0_attn_D_skip, L0_attn_out_proj_w, L0_attn_ln2_g, L0_attn_ln2_b, L0_attn_q_w, L0_attn_k_w, L0_attn_v_w, L0_attn_o_w, L0_attn_ln3_g, L0_attn_ln3_b, L0_attn_w1, L0_attn_w2, L0_attn_w3), axis=-1)
    x = _layernorm(x + _L0_ffn_ref(x, L0_ffn_centroids, L0_ffn_ln_g, L0_ffn_ln_b, L0_ffn_w1, L0_ffn_b1, L0_ffn_w2, L0_ffn_b2), axis=-1)
    x = _layernorm(x + _L1_attn_ref(x, L1_attn_alpha, L1_attn_Wq, L1_attn_bq, L1_attn_Wk, L1_attn_bk, L1_attn_Wv, L1_attn_bv, L1_attn_W_o, L1_attn_Wfc, L1_attn_bfc), axis=-1)
    x = _layernorm(x + _L1_ffn_ref(x, L1_ffn_w1, L1_ffn_b1, L1_ffn_w2, L1_ffn_b2), axis=-1)
    return x

_drawn_inputs = setup_inputs


def setup_inputs(seed=0):
    import zlib

    import numpy as np

    out = dict(_drawn_inputs(seed))
    spreads = {'L0_attn_ln1_g': (1.0, 0.6),
     'L0_attn_ln1_b': (0.0, 0.8),
     'L0_attn_conv_b': (0.0, 0.8),
     'L0_attn_dt_proj_b': (0.0, 0.8),
     'L0_attn_D_skip': (1.0, 0.6),
     'L0_attn_ln2_g': (1.0, 0.6),
     'L0_attn_ln2_b': (0.0, 2.0),
     'L0_attn_ln3_g': (1.0, 0.6),
     'L0_attn_ln3_b': (0.0, 2.0),
     'L0_ffn_ln_g': (1.0, 0.2),
     'L0_ffn_ln_b': (0.0, 0.8),
     'L0_ffn_b1': (0.0, 0.278),
     'L0_ffn_b2': (0.0, 0.1),
     'L1_attn_bq': (0.0, 0.1),
     'L1_attn_bk': (0.0, 2.0),
     'L1_attn_bv': (0.0, 0.1),
     'L1_attn_bfc': (0.0, 0.1)}
    factors = {'L0_attn_in_proj_w': 8.0,
     'L0_attn_conv_w': 8.0,
     'L0_attn_x_proj_w': 8.0,
     'L0_attn_dt_proj_w': 8.0,
     'L0_attn_A_log': 8.0,
     'L0_attn_out_proj_w': 8.0,
     'L0_attn_q_w': 63.69,
     'L0_attn_k_w': 62.888,
     'L0_attn_v_w': 26.122,
     'L1_ffn_b1': 5.151,
     'L1_ffn_b2': 3.466,
     'L0_attn_o_w': 8.0,
     'L0_attn_w1': 8.0,
     'L0_attn_w2': 8.0,
     'L0_attn_w3': 8.0}
    for name, (base, spread) in spreads.items():
        noise = np.random.default_rng([zlib.crc32(name.encode()), seed]).standard_normal(out[name].shape)
        drawn = base * np.exp(spread * noise) if base else spread * noise
        out[name] = jnp.asarray(drawn.astype(out[name].dtype))
    for name, factor in factors.items():
        out[name] = (out[name] * factor).astype(out[name].dtype)
    return out
```

```python
from contextlib import ExitStack

import numpy as np

import concourse.bass as bass
from concourse import mybir

F32 = mybir.dt.float32
BF16 = mybir.dt.bfloat16
I32 = mybir.dt.int32
U32 = mybir.dt.uint32
ALU = mybir.AluOpType
ACT = mybir.ActivationFunctionType
AX = mybir.AxisListType

P = 128
B, L, D = 2, 2048, 256
T = B * L
NT = T // P
TPB = L // P
KD = D // P
CH = 512
TPC = CH // P
NC = T // CH
EPS = 1e-5

DI, DS, DC = 512, 16, 4
ND = DI // P

H, DH = 16, 16
KV = 4
PAIRS = ((0, 0), (0, 1), (0, 2), (1, 0), (1, 1), (2, 0))
KS = len(PAIRS) * DH
KM = KS + 3
MASKED = -1e30

FF = 1024
NF = FF // P
E = 8
CAP = T // E

WA_COLS, WB_COLS = 6144, 8192


class Chain:

    def __init__(self, eng, sem):
        self.eng, self.sem, self.n = eng, sem, 0

    def restart(self):
        self.eng.sem_clear(self.sem)
        self.n = 0

    def post(self, ins):
        ins.then_inc(self.sem, 1)
        self.n += 1

    def join(self):
        self.eng.wait_ge(self.sem, self.n)

    def __call__(self, ins):
        self.post(ins)
        self.join()


class Core:

    def __init__(self, nc, ctx, args, out):
        self.nc, self.ctx, self.a, self.out = nc, ctx, args, out
        sb = self.sb(ctx)
        self.X = sb("X", [P, NT, D], F32)
        self.WA = sb("WA", [P, WA_COLS], F32)
        self.WB = sb("WB", [P, WB_COLS], F32)
        self.ident = sb("ident", [P, P], F32)
        self.identb = sb("identb", [P, P], BF16)
        self.stats = sb("stats", [P, NT, 6], F32)
        self.mean = sb("mean", [P, NT], F32)
        self.rstd = sb("rstd", [P, NT], F32)
        self.lnt = sb("lnt", [P, 3, NT], F32)
        self.slots = sb("slots", [P, NT], U32)
        self.sorted = nc.dram_tensor("sorted", (T, D), F32, kind="Internal").ap()
        self.hidden = nc.dram_tensor("hidden", (T, D), F32, kind="Internal").ap()
        self.PS = ctx.enter_context(nc.psum_tensor("PS", [P, 8, CH], F32))
        self.chain_v = nc.alloc_semaphore("chain_v")
        self.chain_a = nc.alloc_semaphore("chain_a")
        self.first_sem = self.chain_a.num + 1
        self.stage_sems = []
        self.pool_sems = 0

    def sb(self, ctx):
        return lambda name, shape, dt: ctx.enter_context(self.nc.sbuf_tensor(name, shape, dt))

    def sem(self, name):
        self.stage_sems.append(
            self.nc.alloc_semaphore(name, num=self.first_sem + len(self.stage_sems)))
        return self.stage_sems[-1]

    def pool_dma_sem(self, name):
        self.pool_sems += 1
        return self.nc.alloc_semaphore(name, num=256 - self.pool_sems)

    def end_stage(self):
        end = self.first_sem + len(self.stage_sems)
        self.nc.all_engine_barrier(sems_to_clear=range(self.first_sem, end))
        for s in self.stage_sems:
            self.nc.release_semaphore(s)
        self.stage_sems = []

    def sems(self, stage, names):
        return [self.sem(f"{stage}_{n}") for n in names.split()]


def row_stats(dve, k, tile):
    return dve.bn_stats(k.stats[:, tile, :], k.X[:, tile, :])


def finish_norm_dve(dve, k, chain, var_ready, std_ready, turn=1):
    s, d, v = k.lnt[:, 0, :], k.lnt[:, 1, :], k.lnt[:, 2, :]
    even, odd = k.stats[:, :, 1], k.stats[:, :, 4]
    chain.post(dve.tensor_tensor(s, even, odd, ALU.add))
    chain.post(dve.tensor_tensor(d, even, odd, ALU.subtract))
    chain(dve.tensor_tensor(v, k.stats[:, :, 2], k.stats[:, :, 5], ALU.add))
    chain.post(dve.tensor_scalar(k.mean[:, :], s, 0.5, None, ALU.mult))
    chain.post(dve.tensor_tensor(d, d, d, ALU.mult))
    chain(dve.tensor_scalar(v, v, 1.0 / D, EPS, ALU.mult, ALU.add))
    dve.scalar_tensor_tensor(out=v, in0=d, scalar=0.25, in1=v, op0=ALU.mult,
                             op1=ALU.add).then_inc(var_ready, 1)
    dve.wait_ge(std_ready, turn)
    chain(dve.reciprocal(k.rstd[:, :], s))


def finish_norm_act(act, k, var_ready, std_ready, turn=1):
    act.wait_ge(var_ready, turn)
    act.activation(k.lnt[:, 0, :], k.lnt[:, 2, :], ACT.Sqrt).then_inc(std_ready, 1)


def normalised(dve, k, out, tile):
    return dve.tensor_scalar(out, k.X[:, tile, :], k.mean[:, tile:tile + 1] if isinstance(tile, int)
                             else k.mean[:, bass.ds(tile, 1)],
                             k.rstd[:, tile:tile + 1] if isinstance(tile, int)
                             else k.rstd[:, bass.ds(tile, 1)], ALU.subtract, ALU.mult)


def load_weight(eng, dst, src, sem):
    eng.dma_start(dst, src.rearrange("(c p) n -> p c n", p=P)).then_inc(sem, 16)


def load_columns(eng, dst, src, sem):
    eng.dma_start(dst, src.rearrange("(c p) -> p c", p=P), allow_slow_non_contiguous=True)\
        .then_inc(sem, 16)


RING = 4


def stage_mamba(k):
    nc, a, X, PS = k.nc, k.a, k.X, k.PS
    with ExitStack() as ctx:
        sb = k.sb(ctx)
        in_w = k.WA[:, 0:2048].rearrange("p (c n) -> p c n", c=KD)
        out_w = k.WA[:, 2048:3072].rearrange("p (c n) -> p c n", c=ND)
        xp_w = k.WA[:, 3072:3200].rearrange("p (c n) -> p c n", c=ND)
        dt_w = k.WA[0:DS, 3200:3200 + DI]
        gb = sb("m_gb", [P, 2, KD], F32)
        convw = sb("m_convw", [P, ND, DC], F32)
        cols = sb("m_cols", [P, 3, ND], F32)
        Aneg = sb("m_A", [P, DS, ND], F32)
        Alog = sb("m_Alog", [P, ND, DS], F32)
        diagD = sb("m_diagD", [P, ND, P], F32)
        sel = sb("m_sel", [96, 2 * DS, P], BF16)
        xs = sb("m_xs", [P, ND, DC - 1 + CH], F32)
        xc = sb("m_xc", [P, ND, CH], F32)
        sg = sb("m_sg", [P, ND, CH], F32)
        dt = sb("m_dt", [P, ND, CH], F32)
        tmp = sb("m_tmp", [P, ND, CH], F32)
        dtx = sb("m_dtx", [P, ND, CH], F32)
        hn = dtx[:, 0:2, :].rearrange("p a (b d) -> p (a b) d", d=D)
        hT = dtx[:, 2:4, :]
        bc = sb("m_bc", [2 * DS, CH], F32)
        bc3 = sb("m_bc3", [96, CH], BF16)
        bcb = sb("m_bcb", [2 * DS, CH], BF16)
        Bs = sb("m_Bs", [P, 2, CH], F32)
        dA = sb("m_dA", [P, 2, ND, CH], F32)
        hh = k.WB[:, :].rearrange("p (u m n) -> p u m n", u=RING, m=ND)
        hC = sb("m_hC", [P, 2, ND, CH], F32)
        bcr = hC[0:2 * DS, 0, 0:2, :]
        state = sb("m_state", [P, DS, ND], F32)
        (x_in, w_in, sel_zero, sel_ready, var_ready, std_ready, A_ready, D_ready, hn_ready, hnT_done,
         hT_ready, proj_done, proj_out, conv_done, carried, xc_ready, bc_mm, bc_ready, bc3_ready,
         dt_mm, dt_out, sp_ready, dtx_ready, b_spread, c_spread, bs_ready, dA_ready, dbx, scanned, hc, yacc,
         gated, out_mm, x_out) = k.sems(
            "m", "x_in w_in sel_zero sel_ready var std A_ready D_ready hn_ready hnT_done "
            "hT_ready proj_done proj_out conv_done carried xc_ready bc_mm bc_ready bc3_ready "
            "dt_mm dt_out sp_ready dtx_ready b_spread c_spread bs_ready dA_ready dbx scanned hc yacc "
            "gated out_mm x_out")
        N_SMALL = 8

        with nc.Block() as block:
            @block.sync
            def _(sp):
                sp.dma_start(X[:, :, :], a["L0_attn_x"].rearrange("b (t p) d -> p (b t) d", p=P))\
                    .then_inc(x_in, 16)
                for dst, src in ((in_w, "L0_attn_in_proj_w"), (out_w, "L0_attn_out_proj_w"),
                                 (xp_w, "L0_attn_x_proj_w")):
                    load_weight(sp, dst, a[src], w_in)
                sp.dma_start(dt_w, a["L0_attn_dt_proj_w"]).then_inc(w_in, 16)
                sp.dma_start(convw[:, :, :], a["L0_attn_conv_w"].rearrange(
                    "(c p) one j -> p c (one j)", p=P)).then_inc(w_in, 16)
                sp.dma_start(Alog[:, :, :], a["L0_attn_A_log"].rearrange("(c p) n -> p c n", p=P))\
                    .then_inc(w_in, 16)
                sp.dma_start(k.ident[:, :], a["c_ident"]).then_inc(w_in, 16)
                sp.dma_start(k.identb[:, :], a["c_identb"]).then_inc(w_in, 16)
                for i, name in enumerate(("L0_attn_ln1_g", "L0_attn_ln1_b")):
                    load_columns(sp, gb[:, i, :], a[name], w_in)
                for i, name in enumerate(("L0_attn_conv_b", "L0_attn_dt_proj_b", "L0_attn_D_skip")):
                    load_columns(sp, cols[:, i, :], a[name], w_in)

            @block.gpsimd
            def _(pool):
                pool.memset(sel[:, :, :], 0.0).then_inc(sel_zero, 1)
                pool.wait_ge(sel_zero, 1)
                for part in range(3):
                    rows = sel[32 * part:32 * part + 32, :, :]
                    pool.affine_select(out=rows, in_=rows, pattern=[[-1, 2 * DS], [0, P]],
                                       compare_op=ALU.not_equal, fill=1.0, base=0,
                                       channel_multiplier=1).then_inc(sel_ready, 1)
                pool.sem_inc(dbx, 2)
                with pool.Fori(0, NC) as c:
                    with pool.Fori(0, DS // RING) as it:
                        for u in range(RING):
                            n = DS * c + RING * it + u
                            pool.wait_ge(dtx_ready, c + 1)
                            pool.wait_ge(bs_ready, n + 1)
                            pool.wait_ge(hc, n + 1)
                            pool.tensor_tensor(hh[:, u, :, :], dtx[:, :, :],
                                               Bs[:, u % 2, :].unsqueeze(1).broadcast_to([P, ND, CH]),
                                               ALU.mult).then_inc(dbx, 1)

            @block.scalar
            def _(act):
                finish_norm_act(act, k, var_ready, std_ready)
                act.wait_ge(w_in, 16 * (N_SMALL + 5))
                act.activation(Aneg[:, :, :], Alog[:, :, :].rearrange("p m n -> p n m"), ACT.Exp)\
                    .then_inc(A_ready, 1)

                def chunk(c):
                    for kd in range(KD):
                        act.wait_ge(hnT_done, KD * c + kd + 1)
                        act.activation(hT[:, kd, :], PS[:, kd, :], ACT.Identity,
                                       scale=gb[:, 0, kd:kd + 1], bias=gb[:, 1, kd:kd + 1])\
                            .then_inc(hT_ready, 1)
                    act.wait_ge(carried, c + 1)
                    act.wait_ge(gated, c + 1)
                    for m in range(2 * ND):
                        act.wait_ge(proj_done, 2 * ND * c + m + 1)
                        if m < ND:
                            act.activation(xs[:, m, DC - 1:], PS[:, 2 + m % 2, :], ACT.Copy)\
                                .then_inc(proj_out, 1)
                        else:
                            act.activation(sg[:, m - ND, :], PS[:, 2 + m % 2, :], ACT.Silu)\
                                .then_inc(proj_out, 1)
                    for m in range(ND):
                        act.wait_ge(conv_done, ND * c + m + 1)
                        act.activation(xc[:, m, :], tmp[:, m, :], ACT.Silu, bias=cols[:, 0, m:m + 1])\
                            .then_inc(xc_ready, 1)
                    chain = Chain(act, k.chain_a)
                    chain.restart()
                    for m in range(ND):
                        act.wait_ge(dt_mm, ND * c + m + 1)
                        act.activation(dt[:, m, :], PS[:, (m + 1) % 4, :], ACT.Identity,
                                       bias=cols[:, 1, m:m + 1]).then_inc(dt_out, 1)
                    act.wait_ge(dt_out, ND * c + ND)
                    chain(act.activation(tmp[:, :, :], dt[:, :, :], ACT.Abs))
                    chain(act.activation(tmp[:, :, :], tmp[:, :, :], ACT.Exp, scale=-1.0))
                    act.activation(tmp[:, :, :], tmp[:, :, :], ACT.Ln, bias=1.0)\
                        .then_inc(sp_ready, 1)
                    act.preload_act_table(ACT.Exp)
                    act.wait_ge(dtx_ready, c + 1)
                    with act.Fori(0, DS // 2) as it:
                        for u in range(2):
                            n = 2 * it + u
                            g = DS * c + n
                            act.wait_ge(b_spread, g + 1)
                            act.wait_ge(dbx, g + 1)
                            act.activation(Bs[:, u, :], PS[:, 2 * u, :], ACT.Copy)\
                                .then_inc(bs_ready, 1)
                            act.wait_ge(scanned, g + 1)
                            for m in range(ND):
                                e = act.activation(dA[:, u, m, :], dt[:, m, :], ACT.Exp,
                                                   scale=Aneg[:, n, m:m + 1])
                            e.then_inc(dA_ready, 1)

                act.wait_ge(A_ready, 2)
                with act.Fori(0, NC) as c:
                    chunk(c)

            @block.vector
            def _(dve):
                chain = Chain(dve, k.chain_v)
                chain.restart()
                dve.sem_inc(scanned, 2)
                dve.sem_inc(hc, RING)
                dve.sem_inc(carried, 1)
                dve.sem_inc(gated, 1)
                dve.wait_ge(x_in, 16)
                with dve.Fori(0, NT) as t:
                    row_stats(dve, k, t).then_inc(x_out, 1)
                dve.wait_ge(x_out, NT)
                finish_norm_dve(dve, k, chain, var_ready, std_ready)
                dve.wait_ge(A_ready, 1)
                dve.tensor_scalar(Aneg[:, :, :], Aneg[:, :, :], -1.0, None, ALU.mult)\
                    .then_inc(A_ready, 1)
                for m in range(ND):
                    chain.post(dve.tensor_scalar(diagD[:, m, :], k.ident[:, :], cols[:, 2, m:m + 1],
                                                 None, ALU.mult))
                chain.join()
                dve.sem_inc(D_ready, 1)

                def chunk(c):
                    chain.restart()
                    for j in range(TPC):
                        normalised(dve, k, hn[:, j, :], TPC * c + j).then_inc(hn_ready, 1)
                    for j in range(DC):
                        for m in range(ND):
                            if j == 0:
                                dve.wait_ge(proj_out, 2 * ND * c + m + 1)
                                chain.post(dve.tensor_scalar(tmp[:, m, :], xs[:, m, 0:CH],
                                                             convw[:, m, 0:1], None, ALU.mult))
                            else:
                                ins = dve.scalar_tensor_tensor(
                                    out=tmp[:, m, :], in0=xs[:, m, j:j + CH],
                                    scalar=convw[:, m, j:j + 1], in1=tmp[:, m, :],
                                    op0=ALU.mult, op1=ALU.add)
                                if j < DC - 1:
                                    chain.post(ins)
                                else:
                                    ins.then_inc(conv_done, 1)
                        if j < DC - 1:
                            chain.join()
                    dve.wait_ge(conv_done, ND * c + ND)
                    dve.tensor_copy(xs[:, :, 0:DC - 1], xs[:, :, CH:CH + DC - 1])\
                        .then_inc(carried, 1)
                    dve.wait_ge(bc_mm, c + 1)
                    dve.tensor_copy(bc[:, :], PS[0:2 * DS, 0, :]).then_inc(bc_ready, 1)
                    dve.wait_ge(bc_ready, c + 1)
                    chain(dve.tensor_copy(bc3[0:32, :], bc[:, :]))
                    chain(dve.tensor_tensor(bcr[:, 0, :], bc[:, :], bc3[0:32, :], ALU.subtract))
                    chain(dve.tensor_copy(bcb[:, :], bcr[:, 0, :]))
                    chain.post(dve.tensor_copy(bc3[32:64, :], bcb[:, :]))
                    chain(dve.tensor_tensor(bcr[:, 1, :], bcr[:, 0, :], bcb[:, :], ALU.subtract))
                    dve.tensor_copy(bc3[64:96, :], bcr[:, 1, :]).then_inc(bc3_ready, 1)
                    dve.wait_ge(sp_ready, c + 1)
                    chain(dve.scalar_tensor_tensor(out=dt[:, :, :], in0=dt[:, :, :], scalar=0.0,
                                                   in1=tmp[:, :, :], op0=ALU.max, op1=ALU.add))
                    dve.wait_ge(xc_ready, ND * c + ND)
                    dve.tensor_tensor(dtx[:, :, :], dt[:, :, :], xc[:, :, :], ALU.mult)\
                        .then_inc(dtx_ready, 1)
                    with dve.Fori(0, DS // RING) as it:
                        for u in range(RING):
                            n = RING * it + u
                            g = DS * c + n
                            dve.wait_ge(dA_ready, g + 1)
                            dve.wait_ge(dbx, g + 3)
                            for m in range(ND):
                                s = dve.tensor_tensor_scan(hh[:, u, m, :], dA[:, u % 2, m, :],
                                                           hh[:, u, m, :], state[:, n, m:m + 1],
                                                           ALU.mult, ALU.add)
                            s.then_inc(scanned, 1)
                            dve.wait_ge(scanned, g + 3)
                            dve.wait_ge(c_spread, g + 1)
                            dve.wait_ge(yacc, g + 1)
                            dve.tensor_scalar(state[:, n, :], hh[:, u, :, CH - 1], 1.0, None,
                                              ALU.mult)
                            dve.tensor_tensor(hC[:, u % 2, :, :], hh[:, u, :, :],
                                              PS[:, 2 * (u % 2) + 1, :].unsqueeze(1)
                                              .broadcast_to([P, ND, CH]), ALU.mult).then_inc(hc, 1)
                    dve.wait_ge(yacc, DS * c + DS + 2)
                    dve.tensor_tensor(tmp[:, :, :], PS[:, 4:8, :], sg[:, :, :], ALU.mult)\
                        .then_inc(gated, 1)
                    for j in range(TPC):
                        dve.wait_ge(out_mm, TPC * c + j + 1)
                        at = TPC * c + j
                        dve.tensor_tensor(X[:, at, :], X[:, at, :],
                                          PS[:, j, 0:D], ALU.add)\
                            .then_inc(x_out, 1)
                    dve.wait_ge(x_out, NT + TPC * c + TPC)
                    for j in range(TPC):
                        row_stats(dve, k, TPC * c + j)

                with dve.Fori(0, B) as b:
                    chain.restart()
                    chain.post(dve.memset(xs[:, :, 0:DC - 1], 0.0))
                    chain(dve.memset(state[:, :, :], 0.0))
                    with dve.Fori(0, NC // B) as i:
                        chunk(NC // B * b + i)

            @block.tensor
            def _(pe):
                pe.sem_inc(yacc, 2)
                pe.wait_ge(w_in, 16 * (N_SMALL + 5))
                pe.wait_ge(sel_ready, 3)
                pe.wait_ge(D_ready, 1)

                def spread_b(c, n, u):
                    pe.matmul(PS[:, 2 * u, :], sel[:, n, :], bc3[:, :], start=True, stop=True)\
                        .then_inc(b_spread, 1)

                def spread_c(c, n, u):
                    pe.matmul(PS[:, 2 * u + 1, :], sel[:, n + DS, :], bc3[:, :], start=True,
                              stop=True).then_inc(c_spread, 1)

                def accumulate(c, n, u):
                    for m in range(ND):
                        mm = pe.matmul(PS[:, 4 + m, :], k.ident[:, :], hC[:, u, m, :], start=False,
                                       stop=False, skip_group_check=True)
                    mm.then_inc(yacc, 1)

                def chunk(c):
                    for kd in range(KD):
                        for j in range(TPC):
                            pe.wait_ge(hn_ready, TPC * c + j + 1)
                            mm = pe.transpose(PS[:, kd, P * j:P * j + P],
                                              hn[:, j, P * kd:P * kd + P], k.ident[:, :])
                        mm.then_inc(hnT_done, 1)
                    pe.wait_ge(hT_ready, KD * c + KD)
                    for m in range(2 * ND):
                        if m >= 2:
                            pe.wait_ge(proj_out, 2 * ND * c + m - 1)
                        for kd in range(KD):
                            mm = pe.matmul(PS[:, 2 + m % 2, :], in_w[:, kd, P * m:P * m + P],
                                           hT[:, kd, :], start=(kd == 0), stop=(kd == KD - 1))
                        mm.then_inc(proj_done, 1)
                    for m in range(ND):
                        pe.wait_ge(xc_ready, ND * c + m + 1)
                        mm = pe.matmul(PS[0:2 * DS, 0, :], xp_w[:, m, :], xc[:, m, :],
                                       start=(m == 0), stop=(m == ND - 1))
                    mm.then_inc(bc_mm, 1)
                    pe.wait_ge(bc_ready, c + 1)
                    pe.wait_ge(proj_out, 2 * ND * c + 2 * ND)
                    for m in range(ND):
                        pe.matmul(PS[:, (m + 1) % 4, :], dt_w[:, P * m:P * m + P], bc[0:DS, :],
                                  start=True, stop=True).then_inc(dt_mm, 1)
                    for m in range(ND):
                        pe.matmul(PS[:, 4 + m, :], diagD[:, m, :], xc[:, m, :], start=True,
                                  stop=True, skip_group_check=True)
                    pe.wait_ge(bc3_ready, c + 1)
                    pe.wait_ge(dt_out, ND * c + ND)
                    for n in range(2):
                        spread_b(c, n, n)
                        spread_c(c, n, n)
                    pe.wait_ge(bs_ready, DS * c + 1)
                    spread_b(c, 2, 0)

                    def state_sum(n, u, left):
                        if left > 3:
                            pe.wait_ge(bs_ready, DS * c + n + 2)
                            spread_b(c, n + 3, (u + 1) % 2)
                        pe.wait_ge(hc, DS * c + n + 1 + RING)
                        if left > 2:
                            spread_c(c, n + 2, u % 2)
                        accumulate(c, n, u % 2)

                    with pe.Fori(0, DS // RING - 1) as it:
                        for u in range(RING):
                            state_sum(RING * it + u, u, DS)
                    for u in range(RING):
                        state_sum(DS - RING + u, u, RING - u)
                    pe.wait_ge(gated, c + 2)
                    for j in range(TPC):
                        for m in range(ND):
                            mm = pe.matmul(PS[:, j, 0:D],
                                           tmp[:, m, P * j:P * j + P], out_w[:, m, :],
                                           start=(m == 0), stop=(m == ND - 1))
                        mm.then_inc(out_mm, 1)

                with pe.Fori(0, NC) as c:
                    chunk(c)


NHP = H // 2
QB = 4
NJ = TPB // QB


def causal_windows():
    scores = [[(i, c * QB, min(QB, i + 1 - c * QB), i if c == J else None)
               for i in range(QB * J, QB * J + QB) for c in range(J + 1)] for J in range(NJ)]
    turned = [[(j, max(j - QB * J, 0), QB - max(j - QB * J, 0), 0, int(j >= QB * J))
               for j in [*range(QB * J, QB * J + QB), *range(QB * J)]] for J in range(NJ)]
    return scores, turned


def band_windows():
    scores = [[(i, max(i - 1, 0), min(i + 1, TPB - 1) - max(i - 1, 0) + 1, max(i - 1, 0))
               for i in range(QB * J, QB * J + QB)] for J in range(NJ)]
    turned = []
    for J in range(NJ):
        rows = []
        for j in range(max(QB * J - 1, 0), min(QB * J + QB, TPB - 1) + 1):
            lo, hi = max(j - 1, QB * J), min(j + 1, QB * J + QB - 1)
            rows.append((j, lo - QB * J, hi - lo + 1, lo - j + 1, hi - lo + 1))
        turned.append(rows)
    return scores, turned


GAPS = ((0,), (1,), (2, 3))


LEAD = (7, 4, 2)


def plan_attention(scores, turned, mixes):
    blocks = [(g, J) for J in range(NJ) for g in range(2)]
    order, uses, maxes, turns = [], 0, 0, 0

    def put(action):
        nonlocal uses, maxes
        if action[0] == "max":
            order.append(("max", maxes, *action[1:]))
            maxes += 1
        elif action[0] == "parts":
            order.append(action)
        elif action[0] == "inv":
            order.append(("inv", uses - 1, *action[1:]))
        else:
            order.append((action[0], uses, *action[1:]))
            uses += 1

    def spread_out(actions, slots, lo, hi):
        for i, action in enumerate(actions):
            slots[lo + (hi - lo) * i // len(actions)].append(action)

    def maxima(q):
        return [("max", q, hh, w) for w in scores[blocks[q][1]] for hh in range(4)]

    def tail(q):
        return [("den", q)] + [("inv", q, i) for i in range(QB)] + [("mix", q)] * mixes + \
            [("out", q, 0), ("out", q, 1)]

    for action in maxima(0) + [("parts", 0), ("rows", 0, 0), ("rows", 0, 1)]:
        put(action)
    for q in range(len(blocks)):
        windows = turned[blocks[q][1]]
        slots = [[] for _ in range(4 * len(windows))]
        end = len(slots)
        if q:
            spread_out(tail(q - 1), slots, 1, end - 2)
        if q + 1 < len(blocks):
            spread_out(maxima(q + 1), slots, 0, end - LEAD[0])
            slots[end - LEAD[0]].append(("parts", q + 1))
            slots[end - LEAD[1]].append(("rows", q + 1, 0))
            slots[end - LEAD[2]].append(("rows", q + 1, 1))
        for n, w in enumerate(windows):
            for gap in range(3):
                if gap < 2:
                    order.append(("turn", turns + n, q, w, gap))
                elif n:
                    order.append(("pv", turns + n - 1, q, windows[n - 1], n == 1, False))
                for slot in GAPS[gap]:
                    for action in slots[4 * n + slot]:
                        put(action)
        order.append(("pv", turns + len(windows) - 1, q, windows[-1], len(windows) == 1, True))
        turns += len(windows)
    for action in tail(len(blocks) - 1):
        put(action)
    return blocks, order, uses, maxes, turns


def two_ahead(eng, front, back):
    front(0, 0)
    front(1, 1)
    with eng.Fori(0, TPB // 2 - 1) as it:
        for u in range(2):
            front(2 * it + u + 2, u)
            back(2 * it + u, u)
    back(TPB - 2, 0)
    back(TPB - 1, 1)


def stage_attention(k, causal):
    nc, a, X, PS = k.nc, k.a, k.X, k.PS
    nk = KV // 2 if causal else NHP
    tag = "g" if causal else "w"
    nq_w, nk_w = NHP * DH, nk * DH
    qk_w, all_w = nq_w + nk_w, nq_w + 2 * nk_w
    nh = NHP + nk
    scores, turned = causal_windows() if causal else band_windows()
    blocks, order, USES, MAXES, TURNS = plan_attention(scores, turned, mixes=not causal)
    NB = len(blocks)
    wide = CH if causal else 3 * P
    chunks_of = len(scores[NJ - 1]) // QB

    with ExitStack() as ctx:
        sb = k.sb(ctx)
        W, V_ = (k.WB, k.WA) if causal else (k.WA, k.WB)
        qkv_w = W[:, 0:KD * 2 * all_w].rearrange("p (c s n) -> p c s n", c=KD, s=2)
        at = KD * 2 * all_w
        o_w = W[:, at:at + 4 * D].rearrange("p (g n) -> p g n", g=4)
        at += 4 * D
        if causal:
            Y = sb(tag + "_Y", [P, TPB, D], F32)
            small = sb(tag + "_small", [P, 4, CH], F32)
            rope = sb(tag + "_rope", [P, TPB, 2, DH], F32)
            gb = sb(tag + "_gb", [P, 2, KD], F32)
            qkv = sb(tag + "_qkv", [P, 2, all_w], F32)
            mask_q = sb(tag + "_mq", [P, P], BF16)
            mask_k = sb(tag + "_mk", [P, P], BF16)
        else:
            mix_w = W[:, at:at + 4 * P].rearrange("p (g n) -> p g n", g=4)
            at += 4 * P
            small = W[:, at:at + 4 * CH].rearrange("p (i n) -> p i n", i=4)
            at += 4 * CH
            qkv = W[:, at:at + 2 * all_w].rearrange("p (u n) -> p u n", u=2)
            at += 2 * all_w
            mix_now = W[:, at:at + 2 * P].rearrange("p (g n) -> p g n", g=2)
            Y = V_[:, WB_COLS - TPB * D:].rearrange("p (t d) -> p t d", t=TPB)
            bias = sb(tag + "_bias", [1, 2, all_w], F32)
            ones_row = sb(tag + "_ones", [1, P], F32)
            bfc = sb(tag + "_bfc", [P, D], F32)
            dist = sb(tag + "_dist", [P, 3, P], BF16)
            band = sb(tag + "_band", [P, 3, P], BF16)
            edge = sb(tag + "_edge", [P, 1], F32)
            sig = sb(tag + "_sig", [1, 16], F32)
            last = sb(tag + "_last", [1, B, D], F32)
            last_two = sb(tag + "_last_two", [P, 1], F32)
        Ot, rden, On, Om = (small[:, i, :] for i in range(4))
        spread = sb(tag + "_spread", [P, P], F32)
        hn = sb(tag + "_hn", [P, 2, D], F32)
        hT = sb(tag + "_hT", [P, 2, KD, P], F32)
        turned_qk = sb(tag + "_rot", [P, 2, nh, DH], F32)
        parts = sb(tag + "_parts", [P, 3, nh, DH], BF16)
        Qs = sb(tag + "_Qs", [P, 2, NHP, len(PAIRS), DH], BF16)
        Ks = sb(tag + "_Ks", [P, 2, nk, len(PAIRS), DH], BF16)
        QT = sb(tag + "_QT", [KM, NHP, TPB, P], BF16)
        KT = sb(tag + "_KT", [KM, nk, TPB, P], BF16)
        Vt = sb(tag + "_V", [P, TPB, nk, 32], F32)
        pT = sb(tag + "_pT", [P, 2, 4, wide], F32)
        mxp = sb(tag + "_mxp", [P, QB, 4, chunks_of], F32)
        negm = sb(tag + "_negm", [P, 2, QB * 4], F32)
        stg = sb(tag + "_stg", [P, QB * 4, KM], BF16)
        (w_in, init, zeroed, norm_ready, centred, y_init, hn_ready, hnT, hT_ready, qkv_mm, qkv_out, parts_ready, qkT,
         q_out, k_out, mx, mx_read, m_parts, used, read, st, ex, pv, o_out, normed,
         x_out, stat, var_ready, std_ready, edge_mm, edge_v, edge_a) = k.sems(
            tag, "w_in init zeroed norm_ready centred y_init hn_ready hnT hT_ready qkv_mm qkv_out parts_ready "
            "qkT q_out k_out mx mx_read m_parts used read st ex pv o_out normed "
            "x_out stat var std edge_mm edge_v edge_a")
        n_in = [0]

        def kmap(h):
            return h // 4 if causal else h

        with nc.Block() as block:
            @block.sync
            def _(sp):
                def load(dst, src, **kw):
                    sp.dma_start(dst, src, **kw).then_inc(w_in, 16)
                    n_in[0] += 1

                pre = "L0_attn_" if causal else "L1_attn_"
                names = ("q_w", "k_w", "v_w") if causal else ("Wq", "Wk", "Wv")
                lo = 0
                for name, w in zip(names, (nq_w, nk_w, nk_w)):
                    for s in range(2):
                        load(qkv_w[:, :, s, lo:lo + w],
                             a[pre + name][:, w * s:w * s + w].rearrange("(c p) n -> p c n", p=P))
                    lo += w
                load(spread[:, :], a["c_spread"])
                sp.wait_ge(init, 1)
                wo = a[pre + ("o_w" if causal else "Wfc")].rearrange("(g h d) n -> h d g n", h=4, d=DH)
                for h in range(4):
                    load(o_w[32 * h:32 * h + DH, :, :], wo[h])
                if causal:
                    load(rope[:, :, :, :], a["c_rope"])
                    for i, name in enumerate(("ln2_g", "ln2_b")):
                        load(gb[:, i, :], a[pre + name].rearrange("(c p) -> p c", p=P),
                             allow_slow_non_contiguous=True)
                    load(mask_q[:, :], a["c_mask_q"])
                    load(mask_k[:, :], a["c_mask_k"])
                else:
                    for h in range(4):
                        load(mix_w[32 * h:32 * h + DH, :, 32 * h:32 * h + DH],
                             a["L1_attn_W_o"].rearrange("(g h) d n -> h d g n", h=4)[h])
                    lo = 0
                    for name, w in zip(("bq", "bk", "bv"), (nq_w, nk_w, nk_w)):
                        load(bias[:, :, lo:lo + w],
                             a[pre + name].rearrange("(one s n) -> one s n", one=1, s=2))
                        lo += w
                    load(bfc[:, :], a["L1_attn_bfc"].rearrange("(one n) -> one n", one=1)
                         .broadcast_to([P, D]))
                    load(dist[:, :, :], a["c_dist"])
                    load(last_two[:, :], a["c_last_two"])
                    load(sig[:, 0:1], a["L1_attn_alpha"].rearrange("(one n) -> one n", one=1))

            N_IN = n_in[0]

            @block.gpsimd
            def _(pool):
                pool.memset(o_w, 0.0).then_inc(zeroed, 1)
                if not causal:
                    pool.memset(mix_w, 0.0).then_inc(zeroed, 1)
                    pool.memset(ones_row[:, :], 1.0).then_inc(zeroed, 1)
                pool.memset(Vt[:, :, :, :], 0.0).then_inc(zeroed, 1)
                pool.memset(stg[:, :, :], 0.0).then_inc(zeroed, 1)
                pool.wait_ge(zeroed, 3 if causal else 5)
                pool.memset(Vt[:, :, :, DH:DH + 1], 1.0).then_inc(zeroed, 1)
                pool.wait_ge(zeroed, 4 if causal else 6)
                pool.memset(KT[KS:KM, :, :, :], 1.0).then_inc(zeroed, 1)
                pool.wait_ge(zeroed, 5 if causal else 7)
                pool.sem_inc(init, 1)
                pool.sem_inc(normed, 1)
                pool.wait_ge(norm_ready, 1)

                def rows(s, b):
                    with pool.Fori(0, TPB // 2) as it:
                        for u in range(2):
                            t = 2 * it + u
                            pool.wait_ge(hnT, TPB * s + t + 1)
                            tile = TPB * b + t
                            if causal:
                                mean, rstd = (x[:, bass.ds(tile, 1)].broadcast_to([P, D])
                                              for x in (k.mean, k.rstd))
                                pool.tensor_tensor(hn[:, u, :], X[:, tile, :], mean, ALU.subtract)\
                                    .then_inc(centred, 1)
                                pool.wait_ge(centred, TPB * s + t + 1)
                                pool.tensor_tensor(hn[:, u, :], hn[:, u, :], rstd, ALU.mult)\
                                    .then_inc(hn_ready, 1)
                            else:
                                pool.tensor_copy(hn[:, u, :], X[:, tile, :]).then_inc(hn_ready, 1)

                dens = [x[1] for x in order if x[0] == "den"]

                def divide(s):
                    for use in dens:
                        pool.wait_ge(read, USES * s + use + 2)
                        pool.tensor_tensor(On, Ot, rden, ALU.mult).then_inc(normed, 1)

                with pool.Fori(0, B) as b:
                    rows(2 * b, b)
                    with pool.Fori(0, TPB) as t:
                        pool.wait_ge(x_out, TPB * b + 1)
                        pool.tensor_copy(Y[:, t, :], X[:, TPB * b + t, :]).then_inc(y_init, 1)
                    divide(2 * b)
                    rows(2 * b + 1, b)
                    divide(2 * b + 1)

            @block.scalar
            def _(act):
                act.sem_inc(hT_ready, 2)
                act.sem_inc(qkv_out, 2)
                act.sem_inc(q_out, 2)
                act.sem_inc(ex, 2)
                act.sem_inc(o_out, 1)
                if causal:
                    finish_norm_act(act, k, var_ready, std_ready)
                else:
                    act.wait_ge(edge_v, 1)
                    act.activation(sig[:, 1:2], sig[:, 0:1], ACT.Exp, scale=-1.0)\
                        .then_inc(edge_a, 1)
                    act.wait_ge(edge_v, 2)
                    act.activation(sig[:, 8:9], sig[:, 7:8], ACT.Exp, scale=-1.0)\
                        .then_inc(edge_a, 1)
                act.wait_ge(w_in, 16 * N_IN)
                act.wait_ge(init, 1)

                def front(s, t, u):
                    g = TPB * s + t
                    act.wait_ge(hnT, g + 3)
                    act.wait_ge(qkv_mm, g + 1)
                    if causal:
                        for kd in range(KD):
                            e = act.activation(hT[:, u, kd, :], PS[:, u, P * kd:P * kd + P],
                                               ACT.Identity, scale=gb[:, 0, kd:kd + 1],
                                               bias=gb[:, 1, kd:kd + 1])
                    else:
                        e = act.activation(hT[:, u, :, :].rearrange("p c n -> p (c n)"),
                                           PS[:, u, 0:D], ACT.Copy)
                    e.then_inc(hT_ready, 1)
                    act.wait_ge(qkv_mm, g + 3)
                    act.wait_ge(parts_ready, g + 1)
                    act.activation(Vt[:, t, :, 0:DH],
                                   PS[:, 2 + u, qk_w:all_w].rearrange("p (h d) -> p h d", d=DH),
                                   ACT.Copy)
                    act.activation(qkv[:, u, 0:qk_w], PS[:, 2 + u, 0:qk_w], ACT.Copy)\
                        .then_inc(qkv_out, 1)

                def back(s, t, u):
                    act.wait_ge(qkT, TPB * s + t + 3)
                    act.activation(QT[0:KS, :, t, :],
                                   PS[0:KS, 4 + 2 * u, :].bitcast(BF16)
                                   .rearrange("p (h n) -> p h n", h=NHP), ACT.Copy)\
                        .then_inc(q_out, 1)

                def attend(s):
                    for what, *x in order:
                        if what == "turn":
                            n, q, (j, first, tiles, _, _), pair = x
                            act.wait_ge(st, 2 * TURNS * s + 2 * n + pair + 1)
                            if pair == 0:
                                act.wait_ge(pv, TURNS * s + n + 1)
                            act.activation(
                                pT[:, n % 2, 2 * pair:2 * pair + 2, 0:P * tiles],
                                PS[:, 2 * pair:2 * pair + 2, P * first:P * (first + tiles)],
                                ACT.Exp, scale=DH ** -0.5).then_inc(ex, 1)
                        elif what == "rows":
                            use, q, r = x
                            g, J = blocks[q]
                            act.wait_ge(used, USES * s + use + 1)
                            act.activation(
                                QT[KS:KM, 4 * g:4 * g + 4, QB * J + 2 * r:QB * J + 2 * r + 2, :],
                                PS[KS:KM, 7, :].bitcast(BF16)
                                .rearrange("p (i h n) -> p h i n", i=2, h=4), ACT.Copy)\
                                .then_inc(read, 1)
                        elif what == "pv" and x[-1]:
                            q = x[1]
                            act.wait_ge(pv, TURNS * s + x[0] + 3)
                            act.wait_ge(normed, NB * s + q + 1)
                            act.activation(Ot, PS[:, 6, :], ACT.Copy).then_inc(o_out, 1)
                        elif what == "mix":
                            use, q = x
                            act.wait_ge(used, USES * s + use + 1)
                            act.activation(Om, PS[:, 7, :], ACT.Copy).then_inc(read, 1)

                act.preload_act_table(ACT.Exp)
                with act.Fori(0, 2 * B) as s:
                    two_ahead(act, lambda t, u: front(s, t, u), lambda t, u: back(s, t, u))
                    attend(s)
                if not causal:
                    finish_norm_act(act, k, var_ready, std_ready)

            def band_edge(dve, chain):
                dve.sem_inc(edge_v, 1)
                dve.wait_ge(edge_a, 1)
                one = sig[:, 2:3]
                chain(dve.tensor_scalar(one, sig[:, 1:2], 1.0, None, ALU.add))
                chain(dve.reciprocal(sig[:, 3:4], one))
                dve.wait_ge(edge_mm, 1)
                flat = last[:, :, :].rearrange("p b d -> p (b d)")
                chain(dve.tensor_copy(flat, PS[0:1, 0, :]))
                chain(dve.scalar_tensor_tensor(out=flat, in0=flat, scalar=-1.0, in1=flat,
                                               op0=ALU.mult, op1=ALU.max))
                chain(dve.tensor_reduce(sig[:, 4:5], flat, AX.X, ALU.add))
                chain(dve.tensor_scalar(sig[:, 5:6], sig[:, 4:5], 1.0 / (B * D), flat[:, 0:1],
                                        ALU.mult, ALU.subtract))
                chain(dve.tensor_scalar(sig[:, 6:7], sig[:, 5:6], sig[:, 3:4], flat[:, 0:1],
                                        ALU.mult, ALU.add))
                chain(dve.tensor_copy(sig[:, 7:8], sig[:, 6:7]))
                dve.sem_inc(edge_v, 1)
                dve.wait_ge(edge_a, 2)
                chain(dve.tensor_scalar(sig[:, 9:10], sig[:, 8:9], 1.0, None, ALU.add))
                chain(dve.reciprocal(sig[:, 10:11], sig[:, 9:10]))
                chain(dve.tensor_scalar(sig[:, 11:12], sig[:, 10:11], 96.0, 24.0, ALU.mult, ALU.add))
                dve.sem_inc(edge_v, 1)
                dve.wait_ge(edge_mm, 2)
                chain(dve.tensor_copy(edge[:, :], PS[:, 1, 0:1]))
                chain(dve.tensor_scalar(band[:, :, :], dist[:, :, :], edge[:, 0:1], MASKED,
                                        ALU.is_gt, ALU.mult))
                dve.sem_inc(edge_v, 1)

            @block.vector
            def _(dve):
                chain = Chain(dve, k.chain_v)
                chain.restart()
                dve.sem_inc(parts_ready, 2)
                dve.sem_inc(k_out, 2)
                dve.sem_inc(mx_read, 2)
                dve.sem_inc(read, 1)
                dve.sem_inc(x_out, 1)
                if causal:
                    finish_norm_dve(dve, k, chain, var_ready, std_ready)
                dve.wait_ge(w_in, 16 * N_IN)
                dve.wait_ge(init, 1)
                dve.sem_inc(norm_ready, 1)
                if not causal:
                    band_edge(dve, chain)

                def parts_of(s, t, u):
                    g = TPB * s + t
                    chain.restart()
                    dve.wait_ge(parts_ready, g + 2)
                    dve.wait_ge(qkv_out, g + 3)
                    src = qkv[:, u, 0:qk_w].rearrange("p (h d) -> p h d", d=DH)
                    if causal:
                        half = DH // 2
                        cos, sin = (rope[:, t, i, :].unsqueeze(1) for i in range(2))
                        rot, out = turned_qk[:, 0], turned_qk[:, 1]
                        chain.post(dve.tensor_tensor(rot[:, :, 0:half], src[:, :, half:DH],
                                                     sin[:, :, 0:half].broadcast_to([P, nh, half]),
                                                     ALU.mult))
                        chain.post(dve.tensor_tensor(rot[:, :, half:DH], src[:, :, 0:half],
                                                     sin[:, :, half:DH].broadcast_to([P, nh, half]),
                                                     ALU.mult))
                        chain(dve.tensor_tensor(out, src, cos.broadcast_to([P, nh, DH]), ALU.mult))
                        chain(dve.tensor_tensor(out, out, rot, ALU.add))
                    else:
                        rot, out = turned_qk[:, 0], src
                    chain(dve.tensor_copy(parts[:, 0], out))
                    chain(dve.tensor_tensor(rot, out, parts[:, 0], ALU.subtract))
                    chain(dve.tensor_copy(parts[:, 1], rot))
                    chain(dve.tensor_tensor(parts[:, 2], rot, parts[:, 1], ALU.subtract))
                    dve.wait_ge(qkT, g + 1)
                    slot = 0
                    for part, n in ((0, 3), (1, 2), (2, 1)):
                        chain.post(dve.tensor_copy(
                            Qs[:, u, :, slot:slot + n, :],
                            parts[:, part, 0:NHP, :].unsqueeze(2)
                            .broadcast_to([P, NHP, n, DH])))
                        slot += n
                    for part, slots in ((0, slice(0, 4, 3)), (1, slice(1, 5, 3)),
                                        (2, slice(2, 3, 1)), (0, slice(5, 6, 1))):
                        n = len(range(*slots.indices(6)))
                        ins = dve.tensor_copy(Ks[:, u, :, slots, :],
                                              parts[:, part, NHP:nh, :].unsqueeze(2)
                                              .broadcast_to([P, nk, n, DH]))
                        if slots.start < 5:
                            chain.post(ins)
                    chain.join()
                    ins.then_inc(parts_ready, 1)

                def keys_out(s, t, u):
                    dve.wait_ge(qkT, TPB * s + t + 3)
                    dve.tensor_scalar(KT[0:KS, :, t, :],
                                      PS[0:KS, 5 + 2 * u, 0:nk * P // 2].bitcast(BF16)
                                      .rearrange("p (h n) -> p h n", h=nk), 1.0, None, ALU.mult)\
                        .then_inc(k_out, 1)

                def attend(s, b, half):
                    chain.restart()
                    if not causal:
                        chain(dve.tensor_scalar(mix_now, mix_w[:, bass.ds(2 * half, 2), :], 1.0,
                                                None, ALU.mult))
                    dve.wait_ge(y_init, TPB * b + TPB)
                    for what, *x in order:
                        if what == "max":
                            n, q, hh, (i, k0, tiles, _) = x
                            J = blocks[q][1]
                            c = k0 // QB if causal else 0
                            dve.wait_ge(mx, MAXES * s + n + 1)
                            dve.tensor_reduce(mxp[:, i % QB, hh, c:c + 1],
                                              PS[:, 4 + n % 2, 0:P * tiles], AX.X, ALU.max)\
                                .then_inc(mx_read, 1)
                            done = n
                        elif what == "parts":
                            q, = x
                            J = blocks[q][1]
                            width = J + 1 if causal else 1
                            dve.wait_ge(mx_read, MAXES * s + done + 3)
                            m, r = negm[:, 0, :], negm[:, 1, :]
                            chain(dve.tensor_reduce(
                                m, mxp[:, :, :, 0:width].rearrange("p i h c -> p (i h) c"),
                                AX.X, ALU.max, negate=True))
                            chain(dve.tensor_copy(stg[:, :, KS], m))
                            chain(dve.tensor_tensor(r, m, stg[:, :, KS], ALU.subtract))
                            chain(dve.tensor_copy(stg[:, :, KS + 1], r))
                            dve.tensor_tensor(stg[:, :, KS + 2], r, stg[:, :, KS + 1],
                                              ALU.subtract).then_inc(m_parts, 1)
                        elif what == "inv":
                            use, q, i = x
                            if i == 0:
                                dve.wait_ge(used, USES * s + use + 1)
                            part = slice(P * i, P * i + P)
                            ins = dve.reciprocal(rden[:, part], PS[:, 7, part])
                            if i == QB - 1:
                                ins.then_inc(read, 1)
                        elif what == "out":
                            use, q, r = x
                            J = blocks[q][1]
                            dve.wait_ge(used, USES * s + use + 1)
                            dst = Y[:, QB * J + 2 * r:QB * J + 2 * r + 2, :]
                            dve.tensor_tensor(dst, dst, PS[:, 7, :]
                                              .rearrange("p (t d) -> p t d", t=2), ALU.add)\
                                .then_inc(read, 1)
                    dve.wait_ge(read, USES * s + USES + 1)

                with dve.Fori(0, B) as b:
                    with dve.Fori(0, 2) as half:
                        s = 2 * b + half
                        parts_of(s, 0, 0)
                        with dve.Fori(0, TPB // 2 - 1) as it:
                            for u in range(2):
                                parts_of(s, 2 * it + u + 1, 1 - u)
                                keys_out(s, 2 * it + u, u)
                        parts_of(s, TPB - 1, 1)
                        keys_out(s, TPB - 2, 0)
                        keys_out(s, TPB - 1, 1)
                        attend(s, b, half)
                    chain.restart()
                    with dve.Fori(0, TPB) as t:
                        tile = TPB * b + t
                        if causal:
                            dve.tensor_scalar(X[:, tile, :], Y[:, t, :], 1.0, None, ALU.mult)\
                                .then_inc(x_out, 1)
                        else:
                            dve.tensor_tensor(X[:, tile, :], Y[:, t, :], bfc[:, :], ALU.add)\
                                .then_inc(x_out, 1)
                        dve.wait_ge(x_out, tile + 2)
                        row_stats(dve, k, tile).then_inc(stat, 1)
                if not causal:
                    dve.wait_ge(stat, NT)
                    finish_norm_dve(dve, k, chain, var_ready, std_ready)
                    with dve.Fori(0, NT) as t:
                        normalised(dve, k, X[:, t, :], t)

            @block.tensor
            def _(pe):
                pe.sem_inc(hnT, 2)
                pe.sem_inc(qkv_mm, 2)
                pe.sem_inc(qkT, 2)
                pe.sem_inc(pv, 2)
                pe.wait_ge(w_in, 16 * N_IN)
                pe.wait_ge(init, 1)
                if not causal:
                    for b in range(B):
                        mm = pe.matmul(PS[0:1, 0, D * b:D * b + D], last_two[:, :], X[:, TPB * b + TPB - 1, :],
                                       start=(b == 0), stop=True, skip_group_check=True)
                    mm.then_inc(edge_mm, 1)
                    pe.wait_ge(edge_v, 3)
                    pe.matmul(PS[:, 1, 0:1], ones_row[:, :], sig[:, 11:12], start=True, stop=True)\
                        .then_inc(edge_mm, 1)
                    pe.wait_ge(edge_v, 4)

                def front(s, half, t, u):
                    g = TPB * s + t
                    pe.wait_ge(hn_ready, g + 1)
                    pe.wait_ge(hT_ready, g + 1)
                    for kd in range(KD):
                        mm = pe.transpose(PS[:, u, P * kd:P * kd + P], hn[:, u, P * kd:P * kd + P],
                                          k.ident[:, :])
                    mm.then_inc(hnT, 1)
                    pe.wait_ge(hT_ready, g + 3)
                    pe.wait_ge(qkv_out, g + 1)
                    for kd in range(KD):
                        mm = pe.matmul(PS[:, 2 + u, 0:all_w], hT[:, u, kd, :], qkv_w[:, kd, half, :],
                                       start=(kd == 0), stop=(kd == KD - 1) and causal)
                    if not causal:
                        mm = pe.matmul(PS[:, 2 + u, 0:all_w], ones_row[:, :], bias[:, half, :],
                                       start=False, stop=True)
                    mm.then_inc(qkv_mm, 1)

                def back(s, t, u):
                    g = TPB * s + t
                    pe.wait_ge(parts_ready, g + 3)
                    pe.wait_ge(q_out, g + 1)
                    pe.wait_ge(k_out, g + 1)
                    for h in range(NHP):
                        pe.transpose(PS[0:KS, 4 + 2 * u, P // 2 * h:P // 2 * (h + 1)].bitcast(BF16),
                                     Qs[:, u, h, :, :].rearrange("p s d -> p (s d)"),
                                     k.identb[:, :])
                    for h in range(nk):
                        mm = pe.transpose(
                            PS[0:KS, 5 + 2 * u, P // 2 * h:P // 2 * (h + 1)].bitcast(BF16),
                            Ks[:, u, h, :, :].rearrange("p s d -> p (s d)"), k.identb[:, :])
                    mm.then_inc(qkT, 1)

                def attend(s, half):
                    pe.wait_ge(q_out, TPB * s + TPB + 2)
                    pe.wait_ge(k_out, TPB * s + TPB + 2)
                    for what, *x in order:
                        if what == "max":
                            n, q, hh, (i, k0, tiles, masked) = x
                            h = 4 * blocks[q][0] + hh
                            bank = PS[:, 4 + n % 2, :]
                            pe.wait_ge(mx_read, MAXES * s + n + 1)
                            mm = pe.matmul(bank[:, 0:P * tiles], QT[0:KS, h, i, :],
                                           KT[0:KS, kmap(h), k0:k0 + tiles, :],
                                           start=True, stop=masked is None)
                            if masked is not None:
                                m0 = masked - k0
                                what_mask = mask_q[:, :] if causal else \
                                    band[:, k0 - i + 1:k0 - i + 1 + tiles, :]
                                mm = pe.matmul(bank[:, P * m0:P * tiles], k.identb[:, :], what_mask,
                                               start=False, stop=True)
                            mm.then_inc(mx, 1)
                        elif what == "turn":
                            n, q, (j, first, tiles, m_at, m_tiles), pair = x
                            g, J = blocks[q]
                            if j == turned[J][0][0] and pair == 0:
                                rows = [y[1] for y in order if y[0] == "rows" and y[2] == q]
                                pe.wait_ge(read, USES * s + rows[-1] + 2)
                            cols = slice(P * first, P * (first + tiles))
                            pe.wait_ge(ex, 2 * TURNS * s + 2 * n + pair + 1)
                            for h2 in range(2):
                                h = 4 * g + 2 * pair + h2
                                bank = PS[:, 2 * pair + h2, :]
                                mm = pe.matmul(bank[:, cols], KT[:, kmap(h), j, :],
                                               QT[:, h, QB * J + first:QB * J + first + tiles, :],
                                               start=True, stop=not m_tiles)
                                if m_tiles:
                                    what_mask = mask_k[:, :] if causal else \
                                        band[:, m_at:m_at + m_tiles, :]
                                    mm = pe.matmul(bank[:, P * first:P * (first + m_tiles)],
                                                   k.identb[:, :], what_mask, start=False,
                                                   stop=True)
                            mm.then_inc(st, 1)
                        elif what == "pv":
                            n, q, (j, first, tiles, _, _), opens, closes = x
                            g = blocks[q][0]
                            pe.wait_ge(ex, 2 * TURNS * s + 2 * n + 4)
                            if opens:
                                pe.wait_ge(o_out, NB * s + q + 1)
                            for hh in range(4):
                                mm = pe.matmul(PS[32 * hh:32 * hh + 32, 6, P * first:P * (first + tiles)],
                                               Vt[:, j, kmap(4 * g + hh), :],
                                               pT[:, n % 2, hh, 0:P * tiles], start=opens,
                                               stop=closes, skip_group_check=True)
                            mm.then_inc(pv, 1)
                        elif what == "rows":
                            use, q, r = x
                            pe.wait_ge(m_parts, NB * s + q + 1)
                            pe.wait_ge(read, USES * s + use + 1)
                            for i in range(8):
                                mm = pe.transpose(
                                    PS[0:KM, 7, P // 2 * i:P // 2 * (i + 1)].bitcast(BF16),
                                    stg[:, 8 * r + i, :], k.identb[:, :])
                            mm.then_inc(used, 1)
                        elif what == "den":
                            use, q = x
                            pe.wait_ge(o_out, NB * s + q + 2)
                            pe.wait_ge(read, USES * s + use + 1)
                            pe.matmul(PS[:, 7, :], spread[:, :], Ot, start=True, stop=True)\
                                .then_inc(used, 1)
                        elif what == "mix":
                            use, q = x
                            pe.wait_ge(normed, NB * s + q + 2)
                            pe.wait_ge(read, USES * s + use + 1)
                            pe.matmul(PS[:, 7, :], mix_now[:, blocks[q][0], :], On, start=True,
                                      stop=True).then_inc(used, 1)
                        elif what == "out":
                            use, q, r = x
                            pe.wait_ge(normed, NB * s + q + 2)
                            pe.wait_ge(read, USES * s + use + 1)
                            src = On if causal else Om
                            for t in range(2):
                                mm = pe.matmul(PS[:, 7, D * t:D * t + D],
                                               src[:, P * (2 * r + t):P * (2 * r + t + 1)],
                                               o_w[:, 2 * half + blocks[q][0], :], start=(t == 0), stop=(t == 1),
                                               skip_group_check=True)
                            mm.then_inc(used, 1)
                    pe.wait_ge(read, USES * s + USES + 1)

                with pe.Fori(0, B) as b:
                    with pe.Fori(0, 2) as half:
                        s = 2 * b + half
                        two_ahead(pe, lambda t, u: front(s, half, t, u),
                                  lambda t, u: back(s, t, u))
                        attend(s, half)


def stage_causal_attention(k):
    stage_attention(k, True)


def stage_band_attention(k):
    stage_attention(k, False)


def stage_mlp(k, kind):
    nc, a, X, PS = k.nc, k.a, k.X, k.PS
    swiglu, expert, gelu = (kind == x for x in ("swiglu", "expert", "gelu"))
    tag = "f" if gelu else kind[0]
    with ExitStack() as ctx:
        sb = k.sb(ctx)

        def weights(arena, at, c):
            return arena[:, at:at + 2048].rearrange("p (c n) -> p c n", c=c)

        if swiglu:
            w1, w3, w2 = [weights(k.WA, 0, KD)] * 2, weights(k.WA, 2048, KD), \
                [weights(k.WA, 4096, NF)] * 2
        elif expert:
            w1, w2 = ([weights(k.WB, 4096 * u + at, c) for u in range(2)]
                      for at, c in ((0, KD), (2048, NF)))
        else:
            w1, w2 = [weights(k.WB, 0, KD)] * 2, [weights(k.WB, 2048, NF)] * 2
        if not swiglu:
            nb = E if expert else 1
            b1r = sb(tag + "_b1r", [nb * NF, P], F32)
            b1 = sb(tag + "_b1", [P, nb * NF], F32)
            b2 = sb(tag + "_b2", [1, nb, D], F32)
            ones_row = sb(tag + "_ones", [1, P], F32)
        if not gelu:
            gb = sb(tag + "_gb", [P, 2, KD], F32)
        hn = sb(tag + "_hn", [P, 2, TPC, D], F32)
        hT = sb(tag + "_hT", [P, 2, KD, CH], F32)
        G = sb(tag + "_G", [P, NF, CH], F32)
        sa = sb(tag + "_sa", [P, 2, CH], F32)
        io = sb(tag + "_io", [P, 2, TPC, D], F32)
        (w_in, b_in, b_T, ones_set, hn_ready, hnT, hT_ready, up, silu, G_ready, down, x_sum, x_out,
         var_ready, std_ready, renorm, freed, combined, stat) = k.sems(
            tag, "w_in b_in b_T ones hn_ready hnT hT_ready up silu G_ready down x_sum x_out "
            "var std renorm freed combined stat")
        w_e, rows_in = ([k.sem(f"{tag}_{n}{u}") for u in range(2)] for n in ("w_e", "rows"))
        stored = k.pool_dma_sem(tag + "_stored") if expert else k.sem(tag + "_stored")
        gathered = [k.pool_dma_sem(f"{tag}_gathered{u}") for u in range(NT // TPC)] \
            if expert else []

        def chunks(eng, body):
            with eng.Fori(0, NC // 2 - 1) as it:
                for u in range(2):
                    body(2 * it + u, it, u, False)
            for u in range(2):
                body(NC - 2 + u, NC // 2 - 1, u, u == 1)

        with nc.Block() as block:
            @block.sync
            def _(sp):
                if swiglu:
                    for dst, src in ((w1[0], "L0_attn_w1"), (w3, "L0_attn_w3"),
                                     (w2[0], "L0_attn_w2")):
                        load_weight(sp, dst, a[src], w_in)
                if gelu:
                    load_weight(sp, w1[0], a["L1_ffn_w1"], w_in)
                    load_weight(sp, w2[0], a["L1_ffn_w2"], w_in)
                else:
                    for i, name in enumerate(("L0_attn_ln3_g", "L0_attn_ln3_b") if swiglu else
                                             ("L0_ffn_ln_g", "L0_ffn_ln_b")):
                        load_columns(sp, gb[:, i, :], a[name], b_in)
                if expert:
                    sp.dma_start(b1r[:, :], a["L0_ffn_b1"].rearrange("e (f p) -> (e f) p", p=P))\
                        .then_inc(b_in, 16)
                    sp.dma_start(b2[:, :, :], a["L0_ffn_b2"].rearrange("(one e) d -> one e d", one=1))\
                        .then_inc(b_in, 16)
                    w1x = a["L0_ffn_w1"].rearrange("e (c p) n -> e p c n", p=P)
                    w2x = a["L0_ffn_w2"].rearrange("e (c p) n -> e p c n", p=P)
                    rows = k.sorted.rearrange("(c j p) d -> c p j d", p=P, j=TPC)
                    with sp.Fori(0, NC // 2) as it:
                        for u in range(2):
                            c = 2 * it + u
                            sp.wait_ge(down, TPC * c + TPC)
                            sp.dma_start(w1[u], w1x[c]).then_inc(w_e[u], 16)
                            sp.dma_start(w2[u], w2x[c]).then_inc(w_e[u], 16)
                            sp.dma_start(hn[:, u, :, :], rows[c]).then_inc(rows_in[u], 16)
                if gelu:
                    sp.dma_start(b1r[:, :], a["L1_ffn_b1"].rearrange("(f p) -> f p", p=P))\
                        .then_inc(b_in, 16)
                    sp.dma_start(b2[:, 0, :], a["L1_ffn_b2"].rearrange("(one d) -> one d", one=1))\
                        .then_inc(b_in, 16)
                    o = k.out.rearrange("(c j p) d -> c p j d", p=P, j=TPC)
                    sp.sem_inc(freed, 2)
                    with sp.Fori(0, NC // 2) as it:
                        for u in range(2):
                            c = 2 * it + u
                            sp.wait_ge(renorm, TPC * c + TPC)
                            sp.dma_start(o[c], io[:, u, :, :]).then_inc(stored, 16)
                            sp.wait_ge(stored, 16 * c + 16)
                            sp.sem_inc(freed, 1)
                if swiglu:
                    x = a["L0_attn_x"].rearrange("b (c j p) d -> (b c) p j d", p=P, j=TPC)
                    with sp.Fori(0, NC // 2) as it:
                        for u in range(2):
                            c = 2 * it + u
                            sp.wait_ge(x_out, TPC * c + TPC)
                            sp.dma_start(io[:, u, :, :], x[c]).then_inc(rows_in[u], 16)

            @block.gpsimd
            def _(pool):
                if not swiglu:
                    pool.memset(ones_row[:, :], 1.0).then_inc(ones_set, 1)
                if swiglu:
                    with pool.Fori(0, NC // 2) as it:
                        for u in range(2):
                            c = 2 * it + u
                            for j in range(TPC):
                                pool.wait_ge(rows_in[u], 16 * it + 16)
                                pool.tensor_tensor(io[:, u, j, :], io[:, u, j, :],
                                                   X[:, TPC * c + j, :], ALU.add)\
                                    .then_inc(x_sum, 1)
                if expert:
                    outs = k.hidden.rearrange("(c j p) d -> c p j d", p=P, j=TPC)
                    pool.sem_inc(freed, 2)
                    with pool.Fori(0, NC // 2) as it:
                        for u in range(2):
                            c = 2 * it + u
                            pool.wait_ge(x_out, TPC * c + TPC + 8)
                            pool.dma_start(outs[c], io[:, u, :, :]).then_inc(stored, 16)
                            pool.wait_ge(stored, 16 * c + 16)
                            pool.sem_inc(freed, 1)
                    for t in range(NT):
                        if t == 0:
                            pool.wait_ge(down, TPC * NC + 8)
                            pool.wait_ge(stored, 16 * NC)
                        if t >= NT // 2:
                            pool.wait_ge(combined, t - NT // 2 + 1)
                        pool.indirect_dma_start(
                            G[:, t % 16 // 2, D * (t % 2):D * (t % 2) + D], None, k.hidden,
                            bass.IndirectOffsetOnAxis(ap=k.slots[:, t:t + 1], axis=0))\
                            .then_inc(gathered[t // TPC], 16)

            @block.scalar
            def _(act):
                act.sem_inc(silu, 2)
                if not swiglu:
                    act.sem_inc(G_ready, 2)
                if swiglu:
                    finish_norm_act(act, k, var_ready, std_ready)
                if not gelu:
                    act.wait_ge(b_in, 16 * (4 if expert else 2))
                if not swiglu:
                    act.wait_ge(b_T, 2)

                def transposed(c, u):
                    for kd in range(KD):
                        act.wait_ge(hnT, KD * c + kd + 1)
                        if gelu:
                            e = act.activation(hT[:, u, kd, :], PS[:, 4 + kd, :], ACT.Copy)
                        else:
                            e = act.activation(hT[:, u, kd, :], PS[:, 4 + kd, :], ACT.Identity,
                                               scale=gb[:, 0, kd:kd + 1], bias=gb[:, 1, kd:kd + 1])
                        e.then_inc(hT_ready, 1)

                def body(c, it, u, last):
                    for f in range(NF):
                        act.wait_ge(up, NF * c + f + 1)
                        if swiglu:
                            act.wait_ge(G_ready, NF * c + f + 1)
                            act.activation(sa[:, f % 2, :], PS[:, f % 2, :], ACT.Silu)\
                                .then_inc(silu, 1)
                        else:
                            at = NF * c + f if expert else f
                            act.activation(G[:, f, :], PS[:, f % 2, :],
                                           ACT.Gelu_apprx_tanh if expert else ACT.Gelu,
                                           bias=b1[:, bass.ds(at, 1)]).then_inc(G_ready, 1)
                    if not last:
                        transposed(c + 1, 1 - u)

                transposed(0, 0)
                chunks(act, body)
                finish_norm_act(act, k, var_ready, std_ready, 2 if swiglu else 1)

            @block.vector
            def _(dve):
                chain = Chain(dve, k.chain_v)
                chain.restart()
                dve.sem_inc(x_out, 8)
                if swiglu:
                    dve.sem_inc(G_ready, 2)
                    finish_norm_dve(dve, k, chain, var_ready, std_ready)
                else:
                    dve.wait_ge(b_T, 1)
                    dve.tensor_copy(b1[:, :], PS[:, 7, 0:nb * NF]).then_inc(b_T, 1)

                def rows(c, u):
                    for j in range(TPC):
                        tile = TPC * c + j
                        if swiglu:
                            ins = normalised(dve, k, hn[:, u, j, :], tile)
                        else:
                            ins = dve.tensor_scalar(hn[:, u, j, :], X[:, tile, :], 1.0, None,
                                                    ALU.mult)
                        ins.then_inc(hn_ready, 1)

                def body(c, it, u, last):
                    for f in range(NF):
                        if swiglu:
                            dve.wait_ge(silu, NF * c + f + 3)
                            dve.tensor_tensor(G[:, f, :], sa[:, f % 2, :], PS[:, 2 + f % 2, :],
                                              ALU.mult).then_inc(G_ready, 1)
                        if f == 3 and not last and not expert:
                            rows(c + 1, 1 - u)
                    for j in range(TPC):
                        tile = TPC * c + j
                        src = PS[:, 6 + j % 2, 0:D]
                        dve.wait_ge(down, TPC * c + j + 9)
                        if swiglu:
                            dve.wait_ge(x_sum, TPC * c + j + 1)
                            ins = dve.tensor_tensor(X[:, tile, :], src, io[:, u, j, :], ALU.add)
                        elif expert:
                            dve.wait_ge(freed, c + 1)
                            ins = dve.tensor_copy(io[:, u, j, :], src)
                        else:
                            ins = dve.tensor_tensor(X[:, tile, :], src, X[:, tile, :], ALU.add)
                        ins.then_inc(x_out, 1)
                    if not expert:
                        dve.wait_ge(x_out, TPC * c + TPC + 8)
                        for j in range(TPC):
                            row_stats(dve, k, TPC * c + j).then_inc(stat, 1)

                if not expert:
                    rows(0, 0)
                chunks(dve, body)
                if expert:
                    for t in range(NT):
                        dve.wait_ge(gathered[t // TPC], 16 * TPC)
                        dve.scalar_tensor_tensor(
                            out=X[:, t, :], in0=X[:, t, :], scalar=2.0,
                            in1=G[:, t % 16 // 2, D * (t % 2):D * (t % 2) + D],
                            op0=ALU.mult, op1=ALU.add).then_inc(combined, 1)
                        if t:
                            dve.wait_ge(combined, t)
                            row_stats(dve, k, t - 1).then_inc(stat, 1)
                    dve.wait_ge(combined, NT)
                    row_stats(dve, k, NT - 1).then_inc(stat, 1)
                chain.restart()
                dve.wait_ge(stat, NT)
                finish_norm_dve(dve, k, chain, var_ready, std_ready, 2 if swiglu else 1)
                with dve.Fori(0, NC // 2) as it:
                    for u in range(2):
                        for j in range(TPC):
                            c = 2 * it + u
                            tile = TPC * c + j
                            if gelu:
                                dve.wait_ge(freed, c + 1)
                                normalised(dve, k, io[:, u, j, :], tile).then_inc(renorm, 1)
                            else:
                                normalised(dve, k, X[:, tile, :], tile).then_inc(renorm, 1)
                if swiglu:
                    with dve.Fori(0, NT) as t:
                        dve.wait_ge(renorm, t + 1)
                        row_stats(dve, k, t).then_inc(stat, 1)
                if gelu:
                    dve.wait_ge(stored, 16 * NC)

            @block.tensor
            def _(pe):
                pe.sem_inc(down, 8)
                if not swiglu:
                    pe.wait_ge(b_in, 16 * (4 if expert else 2))
                    pe.wait_ge(ones_set, 1)
                    pe.transpose(PS[:, 7, 0:nb * NF], b1r[:, :], k.ident[0:nb * NF, 0:nb * NF])\
                        .then_inc(b_T, 1)
                    pe.wait_ge(b_T, 2)
                if not expert:
                    pe.wait_ge(w_in, 16 * (3 if swiglu else 2))

                def transpose(c, it, u):
                    if expert:
                        pe.wait_ge(rows_in[u], 16 * it + 16)
                    else:
                        pe.wait_ge(hn_ready, TPC * c + TPC)
                    for kd in range(KD):
                        for j in range(TPC):
                            mm = pe.transpose(PS[:, 4 + kd, P * j:P * j + P],
                                              hn[:, u, j, P * kd:P * kd + P], k.ident[:, :])
                        mm.then_inc(hnT, 1)

                def body(c, it, u, last):
                    if expert:
                        pe.wait_ge(w_e[u], 32 * it + 32)
                    pe.wait_ge(hT_ready, KD * c + KD)
                    for f in range(NF):
                        pe.wait_ge(G_ready, NF * c + f + 1)
                        if swiglu:
                            pe.wait_ge(silu, NF * c + f + 1)
                        for w, bank in ((w1[u], f % 2), (w3, 2 + f % 2)) if swiglu else \
                                ((w1[u], f % 2),):
                            for kd in range(KD):
                                mm = pe.matmul(PS[:, bank, :], w[:, kd, P * f:P * f + P],
                                               hT[:, u, kd, :], start=(kd == 0),
                                               stop=(kd == KD - 1))
                        mm.then_inc(up, 1)
                    if not last:
                        transpose(c + 1, it if u == 0 else it + 1, 1 - u)
                    pe.wait_ge(G_ready, NF * c + NF + 2)
                    for j in range(TPC):
                        pe.wait_ge(x_out, TPC * c + j + 7)
                        dst = PS[:, 6 + j % 2, 0:D]
                        for f in range(NF):
                            mm = pe.matmul(dst, G[:, f, P * j:P * j + P], w2[u][:, f, :],
                                           start=(f == 0), stop=(f == NF - 1 and swiglu))
                        if not swiglu:
                            mm = pe.matmul(dst, ones_row[:, :], b2[:, c if expert else 0, :],
                                           start=False, stop=True)
                        mm.then_inc(down, 1)

                transpose(0, 0, 0)
                chunks(pe, body)


def stage_swiglu(k):
    stage_mlp(k, "swiglu")


def stage_experts(k):
    stage_mlp(k, "expert")


def stage_final(k):
    stage_mlp(k, "gelu")


FAN = 15


def stage_route(k):
    nc, a, X, PS = k.nc, k.a, k.X, k.PS
    with ExitStack() as ctx:
        sb = k.sb(ctx)
        gb = sb("r_gb", [P, 2, KD], F32)
        cent = sb("r_cent", [E, D], F32)
        centT = sb("r_centT", [P, KD, E], F32)
        hn = sb("r_hn", [P, 2, D], F32)
        hT = sb("r_hT", [P, 2, KD, P], F32)
        XN = sb("r_XN", [P, NT, D], F32)
        score = sb("r_score", [P, E, NT], F32)
        bits = sb("r_bits", [P, E, NT], U32)
        high = sb("r_high", [P, E, NT], F32)
        low = sb("r_low", [P, E, NT], F32)
        neg = sb("r_neg", [P, E, NT], F32)
        fold = sb("r_fold", [P, E, NT], F32)
        grid = sb("r_grid", [P, FAN], F32)
        before = sb("r_before", [P, P], F32)
        onesb = sb("r_onesb", [P, P], BF16)
        ones = sb("r_ones", [P, NT], F32)
        left = sb("r_left", [P, NT], F32)
        slot = sb("r_slot", [P, NT], F32)
        base = sb("r_base", [P, 1], F32)
        key = sb("r_key", [P, NT], F32)
        tie = sb("r_tie", [P, NT], F32)
        sel = sb("r_sel", [P, NT], F32)
        pick = sb("r_pick", [P, NT], BF16)
        run = sb("r_run", [P, NT], F32)
        reach = sb("r_reach", [P, FAN, NT], BF16)
        thr = sb("r_thr", [P, FAN], F32)
        count = sb("r_count", [P, FAN], F32)
        hit = sb("r_hit", [P, FAN], F32)
        one = sb("r_one", [P, 8], F32)
        need, found, n_hit, total = (one[:, i:i + 1] for i in range(4))
        (w_in, var_ready, std_ready, c_T, hn_ready, hnT, hT_ready, sc_mm, asked, told,
         summed, ranked, slots_ready) = k.sems(
            "r", "w_in var std c_T hn_ready hnT hT_ready sc_mm asked told summed ranked slots")
        scattered = k.pool_dma_sem("r_scattered")
        STEPS = (4096, 256, 16, 1)
        ASKS = 2 * (len(STEPS) + 1) + 1

        with nc.Block() as block:
            @block.sync
            def _(sp):
                for i, name in enumerate(("L0_ffn_ln_g", "L0_ffn_ln_b")):
                    load_columns(sp, gb[:, i, :], a[name], w_in)
                for dst, src in ((cent, "L0_ffn_centroids"), (grid, "c_grid"),
                                 (before, "c_before")):
                    sp.dma_start(dst[:, :], a[src]).then_inc(w_in, 16)

            @block.gpsimd
            def _(pool):
                for t in range(NT):
                    if t == 0:
                        pool.wait_ge(slots_ready, 1)
                    pool.indirect_dma_start(
                        k.sorted, bass.IndirectOffsetOnAxis(ap=k.slots[:, t:t + 1], axis=0),
                        XN[:, t, :], None).then_inc(scattered, 16)
                pool.wait_ge(scattered, 16 * NT)

            @block.scalar
            def _(act):
                act.sem_inc(hT_ready, 2)
                finish_norm_act(act, k, var_ready, std_ready)
                act.wait_ge(w_in, 16 * 5)
                with act.Fori(0, NT // 2) as it:
                    for u in range(2):
                        t = 2 * it + u
                        act.wait_ge(hnT, t + 3)
                        act.wait_ge(sc_mm, t + 1)
                        for kd in range(KD):
                            e = act.activation(hT[:, u, kd, :], PS[:, u, P * kd:P * kd + P],
                                               ACT.Identity, scale=gb[:, 0, kd:kd + 1],
                                               bias=gb[:, 1, kd:kd + 1])
                        e.then_inc(hT_ready, 1)

            @block.vector
            def _(dve):
                chain = Chain(dve, k.chain_v)
                chain.restart()
                finish_norm_dve(dve, k, chain, var_ready, std_ready)
                dve.wait_ge(w_in, 16 * 5)
                dve.wait_ge(c_T, 1)
                dve.tensor_copy(centT[:, :, :], PS[:, 6, 0:KD * E].rearrange("p (c e) -> p c e", c=KD))\
                    .then_inc(c_T, 1)
                with dve.Fori(0, NT // 2) as it:
                    for u in range(2):
                        t = 2 * it + u
                        dve.wait_ge(hnT, t + 1)
                        normalised(dve, k, hn[:, u, :], t).then_inc(hn_ready, 1)
                        normalised(dve, k, XN[:, t, :], t)
                dve.wait_ge(sc_mm, NT + 2)
                every = (slice(None),) * 3
                chain.restart()
                chain(dve.tensor_copy(score[every],
                                      PS[:, 2, 0:E * NT].rearrange("p (t e) -> p e t", e=E)))
                raw = score[:, :, :].bitcast(U32)
                chain(dve.tensor_scalar(bits[every], raw, 16, None, ALU.logical_shift_right))
                chain(dve.tensor_copy(high[every], bits[every]))
                chain(dve.tensor_scalar(bits[every], raw, 0xFFFF, None, ALU.bitwise_and))
                chain.post(dve.tensor_copy(low[every], bits[every]))
                chain.post(dve.tensor_scalar(neg[every], high[every], 32768.0, None, ALU.is_ge))
                chain.post(dve.tensor_scalar(fold[every], high[every], -2.0, 32767.0, ALU.mult,
                                             ALU.add))
                chain.join()
                chain(dve.tensor_tensor(fold[every], fold[every], neg[every], ALU.mult))
                chain(dve.scalar_tensor_tensor(out=high[every], in0=high[every], scalar=32769.0,
                                               in1=fold[every], op0=ALU.add, op1=ALU.add))
                chain(dve.tensor_scalar(fold[every], low[every], -2.0, 65535.0, ALU.mult, ALU.add))
                chain(dve.tensor_tensor(fold[every], fold[every], neg[every], ALU.mult))
                chain(dve.scalar_tensor_tensor(out=low[every], in0=low[every], scalar=1.0,
                                               in1=fold[every], op0=ALU.add, op1=ALU.add))
                chain.post(dve.memset(ones[:, :], 1.0))
                chain.post(dve.memset(onesb[:, :], 1.0))
                chain.post(dve.memset(left[:, :], 1.0))
                chain.post(dve.memset(slot[:, :], 0.0))
                chain.post(dve.memset(base[:, :], -1.0))
                chain.join()

                def give_slots(turn):
                    chain(dve.tensor_tensor_scan(run[:, :], ones[:, :], sel[:, :], 0.0, ALU.mult,
                                                 ALU.add))
                    dve.tensor_copy(total, run[:, NT - 1:NT]).then_inc(summed, 1)
                    dve.wait_ge(ranked, turn)
                    chain(dve.tensor_copy(n_hit, PS[:, 4, 0:1]))
                    chain(dve.tensor_scalar(run[:, :], run[:, :], n_hit, base[:, :], ALU.add,
                                            ALU.add))
                    chain(dve.tensor_tensor(run[:, :], run[:, :], sel[:, :], ALU.mult))
                    chain.post(dve.tensor_tensor(slot[:, :], slot[:, :], run[:, :], ALU.add))
                    chain.post(dve.tensor_tensor(left[:, :], left[:, :], sel[:, :], ALU.subtract))
                    chain.post(dve.tensor_scalar(base[:, :], base[:, :], float(CAP), None, ALU.add))
                    chain.join()

                with dve.Fori(0, E - 1) as e:
                    chain.restart()
                    asks = [0]

                    def ask(ins):
                        ins.then_inc(asked, 1)
                        asks[0] += 1
                        dve.wait_ge(told, ASKS * e + asks[0])

                    def search(keys, steps):
                        chain(dve.memset(found, 1.0))
                        for step in steps:
                            chain(dve.tensor_scalar(thr[:, :], grid[:, :], float(step), found,
                                                    ALU.mult, ALU.add))
                            ask(dve.tensor_tensor(
                                reach[:, :, :], keys.unsqueeze(1).broadcast_to([P, FAN, NT]),
                                thr[:, :].unsqueeze(2).broadcast_to([P, FAN, NT]), ALU.is_ge))
                            chain(dve.tensor_reduce(
                                count[:, :], PS[:, 0, 0:FAN * NT].rearrange("p (f t) -> p f t", f=FAN),
                                AX.X, ALU.add))
                            chain(dve.tensor_scalar(hit[:, :], count[:, :], need, None, ALU.is_ge))
                            chain(dve.tensor_reduce(n_hit, hit[:, :], AX.X, ALU.add))
                            chain(dve.scalar_tensor_tensor(
                                out=found, in0=n_hit, scalar=float(step), in1=found,
                                op0=ALU.mult, op1=ALU.add))

                    def take_above(keys):
                        chain(dve.tensor_scalar(run[:, :], keys, found, None, ALU.is_gt))
                        chain.post(dve.tensor_tensor(sel[:, :], sel[:, :], run[:, :], ALU.add))
                        ask(dve.tensor_copy(pick[:, :], run[:, :]))
                        chain(dve.tensor_reduce(total, PS[:, 1, 0:NT], AX.X, ALU.add))
                        chain(dve.tensor_tensor(need, need, total, ALU.subtract))

                    chain.post(dve.memset(need, float(CAP)))
                    chain.post(dve.memset(sel[:, :], 0.0))
                    chain(dve.tensor_tensor(key[:, :], high[:, e, :], left[:, :], ALU.mult))
                    search(key[:, :], STEPS)
                    take_above(key[:, :])
                    chain(dve.tensor_scalar(tie[:, :], key[:, :], found, None, ALU.is_equal))
                    chain(dve.tensor_tensor(key[:, :], low[:, e, :], tie[:, :], ALU.mult))
                    search(key[:, :], STEPS)
                    take_above(key[:, :])
                    chain(dve.tensor_scalar(tie[:, :], key[:, :], found, None, ALU.is_equal))
                    ask(dve.tensor_copy(pick[:, :], tie[:, :]))
                    chain(dve.tensor_tensor_scan(run[:, :], ones[:, :], PS[:, 1, 0:NT], 0.0,
                                                 ALU.mult, ALU.add))
                    chain(dve.tensor_tensor(run[:, :], run[:, :], PS[:, 1, 0:NT], ALU.subtract))
                    chain(dve.tensor_tensor(run[:, :], run[:, :], PS[:, 3, 0:NT], ALU.add))
                    chain(dve.tensor_scalar(run[:, :], run[:, :], need, None, ALU.is_lt))
                    chain(dve.tensor_tensor(run[:, :], run[:, :], tie[:, :], ALU.mult))
                    chain(dve.tensor_tensor(sel[:, :], sel[:, :], run[:, :], ALU.add))
                    give_slots(e + 1)
                    assert asks[0] == ASKS, asks
                chain.restart()
                chain(dve.tensor_scalar(sel[:, :], left[:, :], 1.0, None, ALU.mult))
                give_slots(E)
                dve.tensor_copy(k.slots[:, :], slot[:, :]).then_inc(slots_ready, 1)

            @block.tensor
            def _(pe):
                pe.sem_inc(hnT, 2)
                pe.sem_inc(sc_mm, 2)
                pe.wait_ge(w_in, 16 * 5)
                for kd in range(KD):
                    mm = pe.transpose(PS[:, 6, E * kd:E * kd + E], cent[:, P * kd:P * kd + P],
                                      k.ident[0:E, 0:E])
                mm.then_inc(c_T, 1)
                pe.wait_ge(c_T, 2)

                def turn_rows(t, u):
                    pe.wait_ge(hn_ready, t + 1)
                    pe.wait_ge(hT_ready, t + 1)
                    for kd in range(KD):
                        mm = pe.transpose(PS[:, u, P * kd:P * kd + P],
                                          hn[:, u, P * kd:P * kd + P], k.ident[:, :])
                    mm.then_inc(hnT, 1)

                def scores(t, u):
                    pe.wait_ge(hT_ready, t + 3)
                    for kd in range(KD):
                        mm = pe.matmul(PS[:, 2, bass.ds(E * t, E)], hT[:, u, kd, :],
                                       centT[:, kd, :], start=(kd == 0), stop=(kd == KD - 1),
                                       skip_group_check=True)
                    mm.then_inc(sc_mm, 1)

                turn_rows(0, 0)
                with pe.Fori(0, NT // 2 - 1) as it:
                    for u in range(2):
                        turn_rows(2 * it + u + 1, 1 - u)
                        scores(2 * it + u, u)
                turn_rows(NT - 1, 1)
                scores(NT - 2, 0)
                scores(NT - 1, 1)

                def taken_before(turn):
                    pe.wait_ge(summed, turn)
                    pe.matmul(PS[:, 4, 0:1], before[:, :], total, start=True, stop=True)\
                        .then_inc(ranked, 1)

                with pe.Fori(0, E - 1) as e:
                    asks = [0]

                    def tell(bank, ones_or_before, what):
                        asks[0] += 1
                        pe.wait_ge(asked, ASKS * e + asks[0])
                        pe.matmul(bank, ones_or_before, what, start=True, stop=True)\
                            .then_inc(told, 1)

                    for _ in range(2):
                        for _ in STEPS:
                            tell(PS[:, 0, 0:FAN * NT], onesb[:, :],
                                 reach[:, :, :].rearrange("p f t -> p (f t)"))
                        tell(PS[:, 1, 0:NT], onesb[:, :], pick[:, :])
                    pe.wait_ge(asked, ASKS * e + ASKS)
                    pe.matmul(PS[:, 1, 0:NT], onesb[:, :], pick[:, :], start=True, stop=True)
                    pe.matmul(PS[:, 3, 0:NT], before[:, :], tie[:, :], start=True, stop=True)\
                        .then_inc(told, 1)
                    taken_before(e + 1)
                taken_before(E)


def program(nc, args, out, stages):
    with ExitStack() as ctx:
        core = Core(nc, ctx, args, out)
        for stage in stages:
            stage(core)
            core.end_stage()



def constants():
    p, q = np.arange(P)[:, None], np.arange(P)[None, :]
    f32 = np.float32
    rotation = f32(1.0) / np.power(f32(10000.0), np.arange(0, DH, 2, dtype=f32) / f32(DH))
    angle = np.arange(L, dtype=f32)[:, None] * rotation
    cos, sin = np.cos(angle), np.sin(angle)
    rope = np.stack([np.concatenate([cos, cos], 1), np.concatenate([-sin, sin], 1)], 1)
    last_two = np.zeros((P, 1), f32)
    last_two[P - 1], last_two[P - 2] = 1, -1
    tile = (np.arange(3) - 1)[None, :, None]
    wide = {
        "c_ident": np.eye(P),
        "c_spread": p == DH + 32 * (q // 32),
        "c_rope": rope.reshape(TPB, P, 2, DH).transpose(1, 0, 2, 3),
        "c_last_two": last_two,
        "c_grid": np.broadcast_to(np.arange(1, 16), (P, 15)),
        "c_before": p < q,
    }
    narrow = {
        "c_identb": np.eye(P),
        "c_mask_q": np.where(q > p, MASKED, 0),
        "c_mask_k": np.where(q < p, MASKED, 0),
        "c_dist": np.minimum(2 * np.abs(P * tile + q[:, None, :] - p[:, :, None]), 2 * P),
    }
    out = {n: np.ascontiguousarray(v, dtype=f32) for n, v in wide.items()}
    out.update((n, np.ascontiguousarray(v.astype(np.dtype("bfloat16")))) for n, v in narrow.items())
    return out


STAGES = (stage_mamba, stage_causal_attention, stage_swiglu, stage_route, stage_experts,
          stage_band_attention, stage_final)


def kernel(**inputs):
    import concourse.bacc as _bacc
    from concourse.bass_utils import run_bass_kernel_spmd as _run

    nc = _bacc.Bacc("TRN2", target_bir_lowering=False, num_devices=1)
    arrays, args = {}, {}
    for name, value in {**inputs, **constants()}.items():
        v = np.ascontiguousarray(value)
        v = v.reshape(v.shape or (1,))
        arrays[f"in_{name}"] = v
        args[name] = nc.dram_tensor(f"in_{name}", v.shape, mybir.dt.from_np(v.dtype),
                                    kind="ExternalInput").ap()
    out = nc.dram_tensor("out", (T, D), F32, kind="ExternalOutput").ap()
    program(nc, args, out, STAGES)
    r = _run(nc, [arrays], core_ids=[0])
    return r.results[0]["out"].reshape(B, L, D)
```

```python
from contextlib import ExitStack

import numpy as np

import concourse.bass as bass
from concourse import mybir

F32 = mybir.dt.float32
BF16 = mybir.dt.bfloat16
I32 = mybir.dt.int32
U32 = mybir.dt.uint32
ALU = mybir.AluOpType
ACT = mybir.ActivationFunctionType
AX = mybir.AxisListType

P = 128
B, L, D = 2, 2048, 256
T = B * L
NT = T // P
TPB = L // P
KD = D // P
CH = 512
TPC = CH // P
NC = T // CH
EPS = 1e-5

DI, DS, DC = 512, 16, 4
ND = DI // P

H, DH = 16, 16
KV = 4
PAIRS = ((0, 0), (0, 1), (0, 2), (1, 0), (1, 1), (2, 0))
KS = len(PAIRS) * DH
KM = KS + 3
MASKED = -1e30

FF = 1024
NF = FF // P
E = 8
CAP = T // E

WA_COLS, WB_COLS = 6144, 8192


class Chain:

    def __init__(self, eng, sem):
        self.eng, self.sem, self.n = eng, sem, 0

    def restart(self):
        self.eng.sem_clear(self.sem)
        self.n = 0

    def post(self, ins):
        ins.then_inc(self.sem, 1)
        self.n += 1

    def join(self):
        self.eng.wait_ge(self.sem, self.n)

    def __call__(self, ins):
        self.post(ins)
        self.join()


class Core:

    def __init__(self, nc, ctx, args, out):
        self.nc, self.ctx, self.a, self.out = nc, ctx, args, out
        sb = self.sb(ctx)
        self.X = sb("X", [P, NT, D], F32)
        self.WA = sb("WA", [P, WA_COLS], F32)
        self.WB = sb("WB", [P, WB_COLS], F32)
        self.ident = sb("ident", [P, P], F32)
        self.identb = sb("identb", [P, P], BF16)
        self.stats = sb("stats", [P, NT, 6], F32)
        self.mean = sb("mean", [P, NT], F32)
        self.rstd = sb("rstd", [P, NT], F32)
        self.lnt = sb("lnt", [P, 3, NT], F32)
        self.slots = sb("slots", [P, NT], U32)
        self.sorted = nc.dram_tensor("sorted", (T, D), F32, kind="Internal").ap()
        self.hidden = nc.dram_tensor("hidden", (T, D), F32, kind="Internal").ap()
        self.PS = ctx.enter_context(nc.psum_tensor("PS", [P, 8, CH], F32))
        self.chain_v = nc.alloc_semaphore("chain_v")
        self.chain_a = nc.alloc_semaphore("chain_a")
        self.first_sem = self.chain_a.num + 1
        self.stage_sems = []
        self.pool_sems = 0

    def sb(self, ctx):
        return lambda name, shape, dt: ctx.enter_context(self.nc.sbuf_tensor(name, shape, dt))

    def sem(self, name):
        self.stage_sems.append(
            self.nc.alloc_semaphore(name, num=self.first_sem + len(self.stage_sems)))
        return self.stage_sems[-1]

    def pool_dma_sem(self, name):
        self.pool_sems += 1
        return self.nc.alloc_semaphore(name, num=256 - self.pool_sems)

    def end_stage(self):
        end = self.first_sem + len(self.stage_sems)
        self.nc.all_engine_barrier(sems_to_clear=range(self.first_sem, end))
        for s in self.stage_sems:
            self.nc.release_semaphore(s)
        self.stage_sems = []

    def sems(self, stage, names):
        return [self.sem(f"{stage}_{n}") for n in names.split()]


def each_tile(eng, body, n=NT):
    with eng.Fori(0, n // 4) as i:
        for j in range(4):
            body(4 * i + j)


def row_stats(dve, k, tile, rows=None):
    return dve.bn_stats(k.stats[:, tile, :], k.X[:, tile, :] if rows is None else rows)


def tiles_of(first, n):
    return slice(first, first + n) if isinstance(first, int) else bass.ds(first, n)


def variances(dve, k, chain, var_ready, first=0, n=NT):
    tiles = tiles_of(first, n)
    s, d, v = (k.lnt[:, i, 0:n] for i in range(3))
    even, odd = k.stats[:, tiles, 1], k.stats[:, tiles, 4]
    chain.post(dve.tensor_tensor(s, even, odd, ALU.add))
    chain.post(dve.tensor_tensor(d, even, odd, ALU.subtract))
    chain(dve.tensor_tensor(v, k.stats[:, tiles, 2], k.stats[:, tiles, 5], ALU.add))
    chain.post(dve.tensor_scalar(k.mean[:, tiles], s, 0.5, None, ALU.mult))
    chain.post(dve.tensor_tensor(d, d, d, ALU.mult))
    chain(dve.tensor_scalar(v, v, 1.0 / D, EPS, ALU.mult, ALU.add))
    dve.scalar_tensor_tensor(out=v, in0=d, scalar=0.25, in1=v, op0=ALU.mult,
                             op1=ALU.add).then_inc(var_ready, 1)


def inverse_roots(dve, k, chain, std_ready, turn, first=0, n=NT):
    dve.wait_ge(std_ready, turn)
    chain(dve.reciprocal(k.rstd[:, tiles_of(first, n)], k.lnt[:, 0, 0:n]))


def finish_norm_dve(dve, k, chain, var_ready, std_ready, turn=1, first=0, n=NT):
    variances(dve, k, chain, var_ready, first, n)
    inverse_roots(dve, k, chain, std_ready, turn, first, n)


def finish_norm_act(act, k, var_ready, std_ready, turn=1, n=NT):
    act.wait_ge(var_ready, turn)
    act.activation(k.lnt[:, 0, 0:n], k.lnt[:, 2, 0:n], ACT.Sqrt).then_inc(std_ready, 1)


def normalised(dve, k, out, tile, rows=None):
    rows = k.X[:, tile, :] if rows is None else rows
    one = tiles_of(tile, 1)
    return dve.tensor_scalar(out, rows, k.mean[:, one], k.rstd[:, one], ALU.subtract, ALU.mult)


def load_weight(eng, dst, src, sem):
    eng.dma_start(dst, src.rearrange("(c p) n -> p c n", p=P)).then_inc(sem, 16)


def load_columns(eng, dst, src, sem):
    eng.dma_start(dst, src.rearrange("(c p) -> p c", p=P), allow_slow_non_contiguous=True)\
        .then_inc(sem, 16)


RING = 4


def chunk_of(b, i=0):
    return NC // B * b + i


def stage_mamba(k):
    nc, a, X, PS = k.nc, k.a, k.X, k.PS
    with ExitStack() as ctx:
        sb = k.sb(ctx)
        in_w = k.WA[:, 0:2048].rearrange("p (c n) -> p c n", c=KD)
        out_w = k.WA[:, 2048:3072].rearrange("p (c n) -> p c n", c=ND)
        xp_w = k.WA[:, 3072:3200].rearrange("p (c n) -> p c n", c=ND)
        dt_w = k.WA[0:DS, 3200:3200 + DI]
        gb = sb("m_gb", [P, 2, KD], F32)
        convw = sb("m_convw", [P, ND, DC], F32)
        cols = sb("m_cols", [P, 3, ND], F32)
        Aneg = sb("m_A", [P, DS, ND], F32)
        Alog = sb("m_Alog", [P, ND, DS], F32)
        diagD = sb("m_diagD", [P, ND, P], F32)
        sel = sb("m_sel", [96, 2 * DS, P], BF16)
        xs = sb("m_xs", [P, ND, DC - 1 + CH], F32)
        xc = sb("m_xc", [P, ND, CH], F32)
        sg = sb("m_sg", [P, ND, CH], F32)
        dt = sb("m_dt", [P, ND, CH], F32)
        tmp = sb("m_tmp", [P, ND, CH], F32)
        dtx = sb("m_dtx", [P, ND, CH], F32)
        hn = dtx[:, 0:2, :].rearrange("p a (b d) -> p (a b) d", d=D)
        hT = dtx[:, 2:4, :]
        bc = sb("m_bc", [2 * DS, CH], F32)
        bc3 = sb("m_bc3", [96, CH], BF16)
        bcb = sb("m_bcb", [2 * DS, CH], BF16)
        Bs = sb("m_Bs", [P, 2, CH], F32)
        dA = sb("m_dA", [P, 2, ND, CH], F32)
        hh = k.WB[:, :].rearrange("p (u m n) -> p u m n", u=RING, m=ND)
        hC = sb("m_hC", [P, 2, ND, CH], F32)
        gy = hC[:, 0, :, :]
        bcr = hC[0:2 * DS, 1, 0:2, :]
        state = sb("m_state", [P, DS, ND], F32)
        (w_in, sel_zero, sel_ready, var_ready, std_ready, A_ready, D_ready, hn_ready, hnT_done,
         hT_ready, proj_done, proj_out, conv_done, carried, xc_ready, bc_mm, bc_ready, bc3_ready,
         dt_mm, dt_out, sp_ready, dtx_ready, b_spread, c_spread, bs_ready, dA_ready,
         dbx, scanned, hc, yacc,
         gated, out_mm, x_out) = k.sems(
            "m", "w_in sel_zero sel_ready var std A_ready D_ready hn_ready hnT_done "
            "hT_ready proj_done proj_out conv_done carried xc_ready bc_mm bc_ready bc3_ready "
            "dt_mm dt_out sp_ready dtx_ready b_spread c_spread bs_ready dA_ready dbx scanned hc yacc "
            "gated out_mm x_out")
        x_in = [k.sem(f"m_x_in{i}") for i in range(4)]
        N_LOADS = 13

        with nc.Block() as block:
            @block.sync
            def _(sp):
                x = a["L0_attn_x"].rearrange("b (t p) d -> p (b t) d", p=P)
                for i, arrived in enumerate(x_in):
                    tiles = slice(NT // 4 * i, NT // 4 * (i + 1))
                    sp.dma_start(X[:, tiles, :], x[:, tiles, :]).then_inc(arrived, 16)
                for dst, src in ((in_w, "L0_attn_in_proj_w"), (out_w, "L0_attn_out_proj_w"),
                                 (xp_w, "L0_attn_x_proj_w")):
                    load_weight(sp, dst, a[src], w_in)
                sp.dma_start(dt_w, a["L0_attn_dt_proj_w"]).then_inc(w_in, 16)
                sp.dma_start(convw[:, :, :], a["L0_attn_conv_w"].rearrange(
                    "(c p) one j -> p c (one j)", p=P)).then_inc(w_in, 16)
                sp.dma_start(Alog[:, :, :], a["L0_attn_A_log"].rearrange("(c p) n -> p c n", p=P))\
                    .then_inc(w_in, 16)
                sp.dma_start(k.ident[:, :], a["c_ident"]).then_inc(w_in, 16)
                sp.dma_start(k.identb[:, :], a["c_identb"]).then_inc(w_in, 16)
                for i, name in enumerate(("L0_attn_ln1_g", "L0_attn_ln1_b")):
                    load_columns(sp, gb[:, i, :], a[name], w_in)
                for i, name in enumerate(("L0_attn_conv_b", "L0_attn_dt_proj_b", "L0_attn_D_skip")):
                    load_columns(sp, cols[:, i, :], a[name], w_in)

            @block.gpsimd
            def _(pool):
                pool.memset(sel[:, :, :], 0.0).then_inc(sel_zero, 1)
                pool.wait_ge(sel_zero, 1)
                for part in range(3):
                    rows = sel[32 * part:32 * part + 32, :, :]
                    pool.affine_select(out=rows, in_=rows, pattern=[[-1, 2 * DS], [0, P]],
                                       compare_op=ALU.not_equal, fill=1.0, base=0,
                                       channel_multiplier=1).then_inc(sel_ready, 1)
                pool.sem_inc(dbx, 2)
                with pool.Fori(0, NC) as c:
                    with pool.Fori(0, DS // RING) as it:
                        for u in range(RING):
                            n = DS * c + RING * it + u
                            pool.wait_ge(dtx_ready, c + 1)
                            pool.wait_ge(bs_ready, n + 1)
                            pool.wait_ge(hc, n + 1)
                            pool.tensor_tensor(hh[:, u, :, :], dtx[:, :, :],
                                               Bs[:, u % 2, :].unsqueeze(1).broadcast_to([P, ND, CH]),
                                               ALU.mult).then_inc(dbx, 1)

            @block.scalar
            def _(act):
                finish_norm_act(act, k, var_ready, std_ready)
                act.wait_ge(w_in, 16 * N_LOADS)
                act.activation(Aneg[:, :, :], Alog[:, :, :].rearrange("p m n -> p n m"), ACT.Exp)\
                    .then_inc(A_ready, 1)

                def project(c):
                    for kd in range(KD):
                        act.wait_ge(hnT_done, KD * c + kd + 1)
                        act.activation(hT[:, kd, :], PS[:, kd, :], ACT.Identity,
                                       scale=gb[:, 0, kd:kd + 1], bias=gb[:, 1, kd:kd + 1])\
                            .then_inc(hT_ready, 1)
                    act.wait_ge(carried, c + 1)
                    for m in range(2 * ND):
                        act.wait_ge(proj_done, 2 * ND * c + m + 1)
                        if m < ND:
                            act.activation(xs[:, m, DC - 1:], PS[:, 2 + m % 2, :], ACT.Copy)\
                                .then_inc(proj_out, 1)
                        else:
                            if m == ND:
                                act.wait_ge(gated, c + 1)
                            act.activation(sg[:, m - ND, :], PS[:, 2 + m % 2, :], ACT.Silu)\
                                .then_inc(proj_out, 1)

                def steps_and_decays(c):
                    for m in range(ND):
                        act.wait_ge(conv_done, ND * c + m + 1)
                        act.activation(xc[:, m, :], tmp[:, m, :], ACT.Silu, bias=cols[:, 0, m:m + 1])\
                            .then_inc(xc_ready, 1)
                    act.preload_act_table(ACT.Exp)
                    chain = Chain(act, k.chain_a)
                    chain.restart()
                    for m in range(ND):
                        act.wait_ge(dt_mm, ND * c + m + 1)
                        u = PS[:, (m + 1) % 4, :]
                        act.activation(dt[:, m, :], u, ACT.Identity, bias=cols[:, 1, m:m + 1])
                        act.activation(tmp[:, m, :], u, ACT.Abs, bias=cols[:, 1, m:m + 1])\
                            .then_inc(dt_out, 1)
                    act.wait_ge(dt_out, ND * c + ND)
                    chain(act.activation(tmp[:, :, :], tmp[:, :, :], ACT.Exp, scale=-1.0))
                    act.activation(tmp[:, :, :], tmp[:, :, :], ACT.Ln, bias=1.0)\
                        .then_inc(sp_ready, 1)
                    act.preload_act_table(ACT.Exp)
                    act.wait_ge(dtx_ready, c + 1)
                    with act.Fori(0, DS // 2) as it:
                        for u in range(2):
                            n = 2 * it + u
                            g = DS * c + n
                            act.wait_ge(b_spread, g + 1)
                            act.wait_ge(dbx, g + 1)
                            act.activation(Bs[:, u, :], PS[:, 2 * u, :], ACT.Copy)\
                                .then_inc(bs_ready, 1)
                            act.wait_ge(scanned, g + 1)
                            for m in range(ND):
                                e = act.activation(dA[:, u, m, :], dt[:, m, :], ACT.Exp,
                                                   scale=Aneg[:, n, m:m + 1])
                            e.then_inc(dA_ready, 1)

                act.wait_ge(A_ready, 2)
                with act.Fori(0, B) as b:
                    project(chunk_of(b))
                    with act.Fori(0, NC // B - 1) as i:
                        steps_and_decays(chunk_of(b, i))
                        project(chunk_of(b, i) + 1)
                    steps_and_decays(chunk_of(b, NC // B - 1))

            @block.vector
            def _(dve):
                chain = Chain(dve, k.chain_v)
                chain.restart()
                dve.sem_inc(scanned, 2)
                dve.sem_inc(hc, RING)
                dve.sem_inc(carried, 1)
                dve.sem_inc(gated, 1)
                for i, arrived in enumerate(x_in):
                    dve.wait_ge(arrived, 16)
                    for t in range(NT // 4 * i, NT // 4 * (i + 1)):
                        row_stats(dve, k, t).then_inc(x_out, 1)
                dve.wait_ge(x_out, NT)
                finish_norm_dve(dve, k, chain, var_ready, std_ready)
                dve.wait_ge(A_ready, 1)
                dve.tensor_scalar(Aneg[:, :, :], Aneg[:, :, :], -1.0, None, ALU.mult)\
                    .then_inc(A_ready, 1)
                for m in range(ND):
                    chain.post(dve.tensor_scalar(diagD[:, m, :], k.ident[:, :], cols[:, 2, m:m + 1],
                                                 None, ALU.mult))
                chain.join()
                dve.sem_inc(D_ready, 1)

                def rows(c):
                    for j in range(TPC):
                        normalised(dve, k, hn[:, j, :], TPC * c + j).then_inc(hn_ready, 1)

                def convolve(c):
                    chain.restart()
                    for j in range(DC):
                        for m in range(ND):
                            if j == 0:
                                dve.wait_ge(proj_out, 2 * ND * c + m + 1)
                                chain.post(dve.tensor_scalar(tmp[:, m, :], xs[:, m, 0:CH],
                                                             convw[:, m, 0:1], None, ALU.mult))
                            else:
                                ins = dve.scalar_tensor_tensor(
                                    out=tmp[:, m, :], in0=xs[:, m, j:j + CH],
                                    scalar=convw[:, m, j:j + 1], in1=tmp[:, m, :],
                                    op0=ALU.mult, op1=ALU.add)
                                if j < DC - 1:
                                    chain.post(ins)
                                else:
                                    ins.then_inc(conv_done, 1)
                        if j < DC - 1:
                            chain.join()
                    dve.wait_ge(conv_done, ND * c + ND)
                    dve.tensor_copy(xs[:, :, 0:DC - 1], xs[:, :, CH:CH + DC - 1])\
                        .then_inc(carried, 1)

                def scan_states(c):
                    chain.restart()
                    dve.wait_ge(bc_mm, c + 1)
                    dve.tensor_copy(bc[:, :], PS[0:2 * DS, 0, :]).then_inc(bc_ready, 1)
                    dve.wait_ge(bc_ready, c + 1)
                    chain(dve.tensor_copy(bc3[0:32, :], bc[:, :]))
                    chain(dve.tensor_tensor(bcr[:, 0, :], bc[:, :], bc3[0:32, :], ALU.subtract))
                    chain(dve.tensor_copy(bcb[:, :], bcr[:, 0, :]))
                    chain.post(dve.tensor_copy(bc3[32:64, :], bcb[:, :]))
                    chain(dve.tensor_tensor(bcr[:, 1, :], bcr[:, 0, :], bcb[:, :], ALU.subtract))
                    dve.tensor_copy(bc3[64:96, :], bcr[:, 1, :]).then_inc(bc3_ready, 1)
                    dve.wait_ge(sp_ready, c + 1)
                    chain(dve.scalar_tensor_tensor(out=dt[:, :, :], in0=dt[:, :, :], scalar=0.0,
                                                   in1=tmp[:, :, :], op0=ALU.max, op1=ALU.add))
                    dve.wait_ge(xc_ready, ND * c + ND)
                    dve.tensor_tensor(dtx[:, :, :], dt[:, :, :], xc[:, :, :], ALU.mult)\
                        .then_inc(dtx_ready, 1)
                    with dve.Fori(0, DS // RING) as it:
                        for u in range(RING):
                            n = RING * it + u
                            g = DS * c + n
                            dve.wait_ge(dA_ready, g + 1)
                            dve.wait_ge(dbx, g + 3)
                            for m in range(ND):
                                s = dve.tensor_tensor_scan(hh[:, u, m, :], dA[:, u % 2, m, :],
                                                           hh[:, u, m, :], state[:, n, m:m + 1],
                                                           ALU.mult, ALU.add)
                            s.then_inc(scanned, 1)
                            dve.wait_ge(scanned, g + 3)
                            dve.wait_ge(c_spread, g + 1)
                            dve.wait_ge(yacc, g + 1)
                            dve.tensor_scalar(state[:, n, :], hh[:, u, :, CH - 1], 1.0, None,
                                              ALU.mult)
                            dve.tensor_tensor(hC[:, u % 2, :, :], hh[:, u, :, :],
                                              PS[:, 2 * (u % 2) + 1, :].unsqueeze(1)
                                              .broadcast_to([P, ND, CH]), ALU.mult).then_inc(hc, 1)

                def gate(c):
                    dve.wait_ge(yacc, DS * c + DS + 2)
                    dve.tensor_tensor(gy, PS[:, 4:8, :], sg[:, :, :], ALU.mult)\
                        .then_inc(gated, 1)

                def add_output(c):
                    for j in range(TPC):
                        dve.wait_ge(out_mm, TPC * c + j + 1)
                        at = TPC * c + j
                        dve.tensor_tensor(X[:, at, :], X[:, at, :],
                                          PS[:, 4 + j, 0:D], ALU.add)\
                            .then_inc(x_out, 1)
                    dve.wait_ge(x_out, NT + TPC * c + TPC)
                    for j in range(TPC):
                        row_stats(dve, k, TPC * c + j)

                with dve.Fori(0, B) as b:
                    chain.restart()
                    chain.post(dve.memset(xs[:, :, 0:DC - 1], 0.0))
                    chain(dve.memset(state[:, :, :], 0.0))
                    rows(chunk_of(b))
                    convolve(chunk_of(b))
                    with dve.Fori(0, NC // B - 1) as i:
                        c = chunk_of(b, i)
                        scan_states(c)
                        rows(c + 1)
                        gate(c)
                        convolve(c + 1)
                        add_output(c)
                    c = chunk_of(b, NC // B - 1)
                    scan_states(c)
                    gate(c)
                    add_output(c)

            @block.tensor
            def _(pe):
                pe.sem_inc(yacc, 2)
                pe.wait_ge(w_in, 16 * N_LOADS)
                pe.wait_ge(sel_ready, 3)
                pe.wait_ge(D_ready, 1)

                def spread_b(c, n, u):
                    pe.matmul(PS[:, 2 * u, :], sel[:, n, :], bc3[:, :], start=True, stop=True)\
                        .then_inc(b_spread, 1)

                def spread_c(c, n, u):
                    pe.matmul(PS[:, 2 * u + 1, :], sel[:, n + DS, :], bc3[:, :], start=True,
                              stop=True).then_inc(c_spread, 1)

                def accumulate(c, n, u):
                    for m in range(ND):
                        mm = pe.matmul(PS[:, 4 + m, :], k.ident[:, :], hC[:, u, m, :], start=False,
                                       stop=False, skip_group_check=True)
                    mm.then_inc(yacc, 1)

                def project(c):
                    for kd in range(KD):
                        for j in range(TPC):
                            pe.wait_ge(hn_ready, TPC * c + j + 1)
                            mm = pe.transpose(PS[:, kd, P * j:P * j + P],
                                              hn[:, j, P * kd:P * kd + P], k.ident[:, :])
                        mm.then_inc(hnT_done, 1)
                    pe.wait_ge(hT_ready, KD * c + KD)
                    for m in range(2 * ND):
                        if m >= 2:
                            pe.wait_ge(proj_out, 2 * ND * c + m - 1)
                        for kd in range(KD):
                            mm = pe.matmul(PS[:, 2 + m % 2, :], in_w[:, kd, P * m:P * m + P],
                                           hT[:, kd, :], start=(kd == 0), stop=(kd == KD - 1))
                        mm.then_inc(proj_done, 1)

                def sum_states(c):
                    for m in range(ND):
                        pe.wait_ge(xc_ready, ND * c + m + 1)
                        mm = pe.matmul(PS[0:2 * DS, 0, :], xp_w[:, m, :], xc[:, m, :],
                                       start=(m == 0), stop=(m == ND - 1))
                    mm.then_inc(bc_mm, 1)
                    pe.wait_ge(bc_ready, c + 1)
                    pe.wait_ge(proj_out, 2 * ND * c + 2 * ND)
                    for m in range(ND):
                        pe.matmul(PS[:, (m + 1) % 4, :], dt_w[:, P * m:P * m + P], bc[0:DS, :],
                                  start=True, stop=True).then_inc(dt_mm, 1)
                    pe.wait_ge(x_out, TPC * c + NT)
                    for m in range(ND):
                        pe.matmul(PS[:, 4 + m, :], diagD[:, m, :], xc[:, m, :], start=True,
                                  stop=True, skip_group_check=True)
                    pe.wait_ge(bc3_ready, c + 1)
                    pe.wait_ge(dt_out, ND * c + ND)
                    for n in range(2):
                        spread_b(c, n, n)
                        spread_c(c, n, n)
                    pe.wait_ge(bs_ready, DS * c + 1)
                    spread_b(c, 2, 0)

                    def state_sum(n, u, left):
                        if left > 3:
                            pe.wait_ge(bs_ready, DS * c + n + 2)
                            spread_b(c, n + 3, (u + 1) % 2)
                        pe.wait_ge(hc, DS * c + n + 1 + RING)
                        if left > 2:
                            spread_c(c, n + 2, u % 2)
                        accumulate(c, n, u % 2)

                    with pe.Fori(0, DS // RING - 1) as it:
                        for u in range(RING):
                            state_sum(RING * it + u, u, DS)
                    for u in range(RING):
                        state_sum(DS - RING + u, u, RING - u)

                def output(c):
                    pe.wait_ge(gated, c + 2)
                    for j in range(TPC):
                        for m in range(ND):
                            mm = pe.matmul(PS[:, 4 + j, 0:D],
                                           gy[:, m, P * j:P * j + P], out_w[:, m, :],
                                           start=(m == 0), stop=(m == ND - 1))
                        mm.then_inc(out_mm, 1)

                with pe.Fori(0, B) as b:
                    project(chunk_of(b))
                    with pe.Fori(0, NC // B - 1) as i:
                        c = chunk_of(b, i)
                        sum_states(c)
                        project(c + 1)
                        output(c)
                    c = chunk_of(b, NC // B - 1)
                    sum_states(c)
                    output(c)


NHP = H // 2
QB = 4
NJ = TPB // QB


REACH = 60
SIDE = P // 2
assert REACH <= SIDE


def causal_windows():
    scores = [[(i, CH * c, min(CH, P * (i + 1) - CH * c), P * i - CH * c, P * (c == J), 0)
               for i in range(QB * J, QB * J + QB) for c in range(J + 1)] for J in range(NJ)]
    turned = [[(j, max(P * j - CH * J, 0), CH - max(P * j - CH * J, 0), P * (j >= QB * J), 0)
               for j in [*range(QB * J, QB * J + QB), *range(QB * J)]] for J in range(NJ)]
    return scores, turned


def band_windows():
    scores, turned = [], []
    for J in range(NJ):
        scores.append([])
        for i in range(QB * J, QB * J + QB):
            lo, hi = max(P * i - SIDE, 0), min(P * i + P + SIDE, L)
            scores[J].append((i, lo, hi - lo, 0, hi - lo, lo - P * (i - 1)))
        turned.append([])
        for j in range(max(QB * J - 1, 0), min(QB * J + QB, TPB - 1) + 1):
            lo, hi = max(P * j - SIDE, CH * J), min(P * j + P + SIDE, CH * J + CH)
            turned[J].append((j, lo - CH * J, hi - lo, hi - lo, lo - P * (j - 1)))
    return scores, turned


INVS = 4
GAPS = ((0,), (1,), (2, 3))


def plan_attention(scores, turned, mixes, per, lead):
    blocks = [(g, J) for J in range(NJ) for g in range(2)]
    order, uses, maxes, turns = [], 0, 0, 0

    def put(action):
        nonlocal uses, maxes
        if action[0] == "max":
            order.append(("max", maxes, *action[1:]))
            maxes += 1
        elif action[0] == "parts":
            order.append(action)
        elif action[0] == "inv":
            order.append(("inv", uses - 1, *action[1:]))
        else:
            order.append((action[0], uses, *action[1:]))
            uses += 1

    def spread_out(actions, slots, lo, hi):
        for i, action in enumerate(actions):
            slots[lo + (hi - lo) * i // len(actions)].append(action)

    def maxima(q):
        return [("max", q, hh, w) for w in scores[blocks[q][1]]
                for hh in range(0, 4, per)]

    def tail(q):
        return [("den", q)] + [("inv", q, i) for i in range(INVS)] + [("mix", q)] * mixes + \
            [("out", q, 0), ("out", q, 1)]

    for action in maxima(0) + [("parts", 0), ("rows", 0, 0), ("rows", 0, 1)]:
        put(action)
    for q in range(len(blocks)):
        windows = turned[blocks[q][1]]
        slots = [[] for _ in range(4 * len(windows))]
        end = len(slots)
        if q:
            spread_out(tail(q - 1), slots, 1, end - 2)
        if q + 1 < len(blocks):
            spread_out(maxima(q + 1), slots, 0, end - lead[0])
            slots[end - lead[0]].append(("parts", q + 1))
            slots[end - lead[1]].append(("rows", q + 1, 0))
            slots[end - lead[2]].append(("rows", q + 1, 1))
        for n, w in enumerate(windows):
            for gap in range(3):
                if gap < 2:
                    order.append(("turn", turns + n, q, w, gap))
                elif n:
                    order.append(("pv", turns + n - 1, q, windows[n - 1], n == 1, False))
                for slot in GAPS[gap]:
                    for action in slots[4 * n + slot]:
                        put(action)
        order.append(("pv", turns + len(windows) - 1, q, windows[-1], len(windows) == 1, True))
        turns += len(windows)
    for action in tail(len(blocks) - 1):
        put(action)
    return blocks, order, uses, maxes, turns


def two_ahead(eng, front, back):
    front(0, 0)
    front(1, 1)
    with eng.Fori(0, TPB // 2 - 1) as it:
        for u in range(2):
            front(2 * it + u + 2, u)
            back(2 * it + u, u)
    back(TPB - 2, 0)
    back(TPB - 1, 1)


def stage_attention(k, causal):
    nc, a, X, PS = k.nc, k.a, k.X, k.PS
    nk = KV // 2 if causal else NHP
    tag = "g" if causal else "w"
    nq_w, nk_w = NHP * DH, nk * DH
    qk_w, all_w = nq_w + nk_w, nq_w + 2 * nk_w
    nh = NHP + nk
    scores, turned = causal_windows() if causal else band_windows()
    per = 1 if causal else 2
    blocks, order, USES, MAXES, TURNS = plan_attention(
        scores, turned, not causal, per, (7, 4, 2) if causal else (9, 6, 3))
    NB = len(blocks)
    wide = max(w[2] for J in turned for w in J)
    windows_of = len(scores[NJ - 1]) // QB

    with ExitStack() as ctx:
        sb = k.sb(ctx)
        W, V_ = (k.WB, k.WA) if causal else (k.WA, k.WB)
        qkv_w = W[:, 0:KD * 2 * all_w].rearrange("p (c s n) -> p c s n", c=KD, s=2)
        at = KD * 2 * all_w
        o_w = W[:, at:at + 4 * D].rearrange("p (g n) -> p g n", g=4)
        at += 4 * D
        if causal:
            Y = sb(tag + "_Y", [P, TPB, D], F32)
            small = sb(tag + "_small", [P, 4, CH], F32)
            rope = sb(tag + "_rope", [P, TPB, 2, DH], F32)
            gb = sb(tag + "_gb", [P, 2, KD], F32)
            qkv = sb(tag + "_qkv", [P, 2, all_w], F32)
            rot = sb(tag + "_rot", [P, nh, DH], F32)
            placed = sb(tag + "_placed", [P, nh, DH], F32)
            mask_q = sb(tag + "_mq", [P, P], BF16)
            mask_k = sb(tag + "_mk", [P, P], BF16)
        else:
            mix_w = W[:, at:at + 4 * P].rearrange("p (g n) -> p g n", g=4)
            at += 4 * P
            small = W[:, at:at + 4 * CH].rearrange("p (i n) -> p i n", i=4)
            at += 4 * CH
            qkv = W[:, at:at + 2 * all_w].rearrange("p (u n) -> p u n", u=2)
            at += 2 * all_w
            mix_now = W[:, at:at + 2 * P].rearrange("p (g n) -> p g n", g=2)
            Y = V_[:, WB_COLS - TPB * D:].rearrange("p (t d) -> p t d", t=TPB)
            bias = sb(tag + "_bias", [1, 2, all_w], F32)
            ones_row = sb(tag + "_ones", [1, P], F32)
            bfc = sb(tag + "_bfc", [P, D], F32)
            dist = sb(tag + "_dist", [P, 3, P], BF16)
            band = sb(tag + "_band", [P, 3, P], BF16)
            mask_q = mask_k = band[:, :, :].rearrange("p r n -> p (r n)")
            sig = sb(tag + "_sig", [P, 16], F32)
            last = sb(tag + "_last", [P, B, D], F32)
            last_two = sb(tag + "_last_two", [P, P], F32)
        Ot, rden, On, Om = (small[:, i, :] for i in range(4))
        spread = sb(tag + "_spread", [P, P], F32)
        hn = sb(tag + "_hn", [P, 2, D], F32)
        hT = sb(tag + "_hT", [P, 2, KD, P], F32)
        rest = sb(tag + "_rest", [P, nh, DH], F32)
        parts = sb(tag + "_parts", [P, 3, nh, DH], BF16)
        Qs = sb(tag + "_Qs", [P, 2, NHP, len(PAIRS), DH], BF16)
        Ks = sb(tag + "_Ks", [P, 2, nk, len(PAIRS), DH], BF16)
        QT = sb(tag + "_QT", [KM, NHP, L], BF16)
        KT = sb(tag + "_KT", [KM, nk, L], BF16)
        Vt = sb(tag + "_V", [P, TPB, nk, 32], F32)
        pT = sb(tag + "_pT", [P, 2, 4, wide], F32)
        mxp = sb(tag + "_mxp", [P, QB, 4, windows_of], F32)
        negm = sb(tag + "_negm", [P, 2, QB * 4], F32)
        stg = sb(tag + "_stg", [P, QB * 4, KM], BF16)
        (w_in, init, zeroed, norm_ready, centred, y_init, hn_ready, hnT, hT_ready, qkv_mm,
         qkv_out, parts_ready, qkT,
         q_out, k_out, mx, mx_read, m_parts, used, read, st, ex, pv, o_out, normed,
         x_out, stat, var_ready, std_ready, edge_mm, edge_asked, edge_told, band_ready) = k.sems(
            tag, "w_in init zeroed norm_ready centred y_init hn_ready hnT hT_ready qkv_mm "
            "qkv_out parts_ready "
            "qkT q_out k_out mx mx_read m_parts used read st ex pv o_out normed "
            "x_out stat var std edge_mm edge_asked edge_told band_ready")
        n_in = [0]

        def kmap(h):
            return h // 4 if causal else h

        with nc.Block() as block:
            @block.sync
            def _(sp):
                def load(dst, src, **kw):
                    sp.dma_start(dst, src, **kw).then_inc(w_in, 16)
                    n_in[0] += 1

                pre = "L0_attn_" if causal else "L1_attn_"
                names = ("q_w", "k_w", "v_w") if causal else ("Wq", "Wk", "Wv")
                lo = 0
                for name, w in zip(names, (nq_w, nk_w, nk_w)):
                    for s in range(2):
                        load(qkv_w[:, :, s, lo:lo + w],
                             a[pre + name][:, w * s:w * s + w].rearrange("(c p) n -> p c n", p=P))
                    lo += w
                load(spread[:, :], a["c_spread"])
                load(KT[KS:KM, :, :], a["c_ones"].rearrange("(one r) n -> one r n", one=1)
                     .broadcast_to([KM - KS, nk, L]))
                sp.wait_ge(zeroed, 1 if causal else 3)
                wo = a[pre + ("o_w" if causal else "Wfc")].rearrange("(g h d) n -> h d g n", h=4, d=DH)
                for h in range(4):
                    load(o_w[32 * h:32 * h + DH, :, :], wo[h])
                if causal:
                    load(rope[:, :, :, :], a["c_rope"])
                    for i, name in enumerate(("ln2_g", "ln2_b")):
                        load(gb[:, i, :], a[pre + name].rearrange("(c p) -> p c", p=P),
                             allow_slow_non_contiguous=True)
                    load(mask_q[:, :], a["c_mask_q"])
                    load(mask_k[:, :], a["c_mask_k"])
                else:
                    for h in range(4):
                        load(mix_w[32 * h:32 * h + DH, :, 32 * h:32 * h + DH],
                             a["L1_attn_W_o"].rearrange("(g h) d n -> h d g n", h=4)[h])
                    lo = 0
                    for name, w in zip(("bq", "bk", "bv"), (nq_w, nk_w, nk_w)):
                        load(bias[:, :, lo:lo + w],
                             a[pre + name].rearrange("(one s n) -> one s n", one=1, s=2))
                        lo += w
                    load(bfc[:, :], a["L1_attn_bfc"].rearrange("(one n) -> one n", one=1)
                         .broadcast_to([P, D]))
                    load(dist[:, :, :], a["c_dist"])
                    load(last_two[:, :], a["c_last_two"])
                    load(sig[:, 0:1], a["L1_attn_alpha"].rearrange("(one n) -> one n", one=1)
                         .broadcast_to([P, 1]))

            N_IN = n_in[0]

            @block.gpsimd
            def _(pool):
                pool.memset(o_w, 0.0).then_inc(zeroed, 1)
                if not causal:
                    pool.memset(mix_w, 0.0).then_inc(zeroed, 1)
                    pool.memset(ones_row[:, :], 1.0).then_inc(zeroed, 1)
                pool.sem_inc(normed, 1)
                pool.wait_ge(norm_ready, 1)

                def rows(s, b):
                    with pool.Fori(0, TPB // 2) as it:
                        for u in range(2):
                            t = 2 * it + u
                            pool.wait_ge(hnT, TPB * s + t + 1)
                            tile = TPB * b + t
                            if causal:
                                mean, rstd = (x[:, bass.ds(tile, 1)].broadcast_to([P, D])
                                              for x in (k.mean, k.rstd))
                                pool.tensor_tensor(hn[:, u, :], X[:, tile, :], mean, ALU.subtract)\
                                    .then_inc(centred, 1)
                                pool.wait_ge(centred, TPB * s + t + 1)
                                pool.tensor_tensor(hn[:, u, :], hn[:, u, :], rstd, ALU.mult)\
                                    .then_inc(hn_ready, 1)
                            else:
                                pool.tensor_copy(hn[:, u, :], X[:, tile, :]).then_inc(hn_ready, 1)

                dens = [x[1] for x in order if x[0] == "den"]

                def divide(s):
                    for use in dens:
                        pool.wait_ge(read, USES * s + use + 2)
                        pool.tensor_tensor(On, Ot, rden, ALU.mult).then_inc(normed, 1)

                with pool.Fori(0, B) as b:
                    rows(2 * b, b)
                    pool.wait_ge(w_in, 16 * N_IN)
                    with pool.Fori(0, TPB) as t:
                        pool.wait_ge(x_out, TPB * b + 1)
                        if causal:
                            ins = pool.tensor_copy(Y[:, t, :], X[:, TPB * b + t, :])
                        else:
                            ins = pool.tensor_tensor(Y[:, t, :], X[:, TPB * b + t, :], bfc[:, :],
                                                     ALU.add)
                        ins.then_inc(y_init, 1)
                    divide(2 * b)
                    rows(2 * b + 1, b)
                    divide(2 * b + 1)

            @block.scalar
            def _(act):
                act.sem_inc(hT_ready, 2)
                act.sem_inc(qkv_out, 2)
                act.sem_inc(q_out, 2)
                act.sem_inc(ex, 2)
                act.sem_inc(o_out, 1)
                if causal:
                    finish_norm_act(act, k, var_ready, std_ready)
                else:
                    act.wait_ge(edge_asked, 1)
                    act.activation(sig[:, 1:2], sig[:, 0:1], ACT.Exp, scale=-1.0)\
                        .then_inc(edge_told, 1)
                    act.wait_ge(edge_asked, 2)
                    act.activation(sig[:, 8:9], sig[:, 7:8], ACT.Exp, scale=-1.0)\
                        .then_inc(edge_told, 1)
                act.wait_ge(w_in, 16 * N_IN)
                act.wait_ge(init, 1)

                def front(s, t, u):
                    g = TPB * s + t
                    act.wait_ge(hnT, g + 3)
                    act.wait_ge(qkv_mm, g + 1)
                    if causal:
                        for kd in range(KD):
                            e = act.activation(hT[:, u, kd, :], PS[:, u, P * kd:P * kd + P],
                                               ACT.Identity, scale=gb[:, 0, kd:kd + 1],
                                               bias=gb[:, 1, kd:kd + 1])
                    else:
                        e = act.activation(hT[:, u, :, :].rearrange("p c n -> p (c n)"),
                                           PS[:, u, 0:D], ACT.Copy)
                    e.then_inc(hT_ready, 1)
                    act.wait_ge(qkv_mm, g + 3)
                    act.wait_ge(parts_ready, g + 1)
                    act.activation(Vt[:, t, :, 0:DH],
                                   PS[:, 2 + u, qk_w:all_w].rearrange("p (h d) -> p h d", d=DH),
                                   ACT.Copy)
                    act.activation(qkv[:, u, 0:qk_w], PS[:, 2 + u, 0:qk_w], ACT.Copy)\
                        .then_inc(qkv_out, 1)

                def back(s, t, u):
                    act.wait_ge(qkT, TPB * s + t + 3)
                    act.activation(QT[0:KS, :, bass.ds(P * t, P)],
                                   PS[0:KS, 4 + 2 * u, :].bitcast(BF16)
                                   .rearrange("p (h n) -> p h n", h=NHP), ACT.Copy)\
                        .then_inc(q_out, 1)

                def attend(s):
                    for what, *x in order:
                        if what == "turn":
                            n, q, (j, first, width, _, _), pair = x
                            act.wait_ge(st, 2 * TURNS * s + 2 * n + pair + 1)
                            if pair == 0:
                                act.wait_ge(pv, TURNS * s + n + 1)
                            act.activation(
                                pT[:, n % 2, 2 * pair:2 * pair + 2, 0:width],
                                PS[:, 2 * pair:2 * pair + 2, first:first + width],
                                ACT.Exp, scale=DH ** -0.5).then_inc(ex, 1)
                        elif what == "rows":
                            use, q, r = x
                            g, J = blocks[q]
                            act.wait_ge(used, USES * s + use + 1)
                            act.activation(
                                QT[KS:KM, 4 * g:4 * g + 4, CH * J + 2 * P * r:CH * J + 2 * P * (r + 1)]
                                .rearrange("p h (i n) -> p h i n", i=2),
                                PS[KS:KM, 7, :].bitcast(BF16)
                                .rearrange("p (i h n) -> p h i n", i=2, h=4), ACT.Copy)\
                                .then_inc(read, 1)
                        elif what == "pv" and x[-1]:
                            q = x[1]
                            act.wait_ge(pv, TURNS * s + x[0] + 3)
                            act.wait_ge(normed, NB * s + q + 1)
                            act.activation(Ot, PS[:, 6, :], ACT.Copy).then_inc(o_out, 1)
                        elif what == "mix":
                            use, q = x
                            act.wait_ge(used, USES * s + use + 1)
                            act.activation(Om, PS[:, 7, :], ACT.Copy).then_inc(read, 1)

                with act.Fori(0, B) as b:
                    act.preload_act_table(ACT.Exp)
                    with act.Fori(0, 2) as half:
                        s = 2 * b + half
                        two_ahead(act, lambda t, u: front(s, t, u), lambda t, u: back(s, t, u))
                        attend(s)
                    if not causal:
                        finish_norm_act(act, k, var_ready, std_ready, b + 1, TPB)

            def band_edge(dve, chain):
                dve.sem_inc(edge_asked, 1)
                dve.wait_ge(edge_told, 1)
                one = sig[:, 2:3]
                chain(dve.tensor_scalar(one, sig[:, 1:2], 1.0, None, ALU.add))
                chain(dve.reciprocal(sig[:, 3:4], one))
                dve.wait_ge(edge_mm, 1)
                flat = last[:, :, :].rearrange("p b d -> p (b d)")
                chain(dve.tensor_copy(flat, PS[:, 6, :]))
                chain(dve.scalar_tensor_tensor(out=flat, in0=flat, scalar=-1.0, in1=flat,
                                               op0=ALU.mult, op1=ALU.max))
                chain(dve.tensor_reduce(sig[:, 4:5], flat, AX.X, ALU.add))
                chain(dve.tensor_scalar(sig[:, 5:6], sig[:, 4:5], 1.0 / (B * D), flat[:, 0:1],
                                        ALU.mult, ALU.subtract))
                chain(dve.tensor_scalar(sig[:, 6:7], sig[:, 5:6], sig[:, 3:4], flat[:, 0:1],
                                        ALU.mult, ALU.add))
                chain(dve.tensor_copy(sig[:, 7:8], sig[:, 6:7]))
                dve.sem_inc(edge_asked, 1)
                dve.wait_ge(edge_told, 2)
                chain(dve.tensor_scalar(sig[:, 9:10], sig[:, 8:9], 1.0, None, ALU.add))
                chain(dve.reciprocal(sig[:, 10:11], sig[:, 9:10]))
                chain(dve.tensor_scalar(sig[:, 11:12], sig[:, 10:11], 96.0, 24.0, ALU.mult, ALU.add))
                dve.tensor_scalar(band[:, :, :], dist[:, :, :], sig[:, 11:12], MASKED,
                                  ALU.is_gt, ALU.mult).then_inc(band_ready, 1)

            @block.vector
            def _(dve):
                chain = Chain(dve, k.chain_v)
                chain.restart()
                dve.sem_inc(parts_ready, 2)
                dve.sem_inc(k_out, 2)
                dve.sem_inc(mx_read, 2)
                dve.sem_inc(read, 1)
                dve.sem_inc(x_out, 1)
                if causal:
                    finish_norm_dve(dve, k, chain, var_ready, std_ready)
                dve.sem_inc(norm_ready, 1)
                chain(dve.memset(Vt[:, :, :, :], 0.0))
                chain.post(dve.memset(Vt[:, :, :, DH:DH + 1], 1.0))
                chain(dve.memset(stg[:, :, :], 0.0))
                dve.sem_inc(init, 1)
                dve.wait_ge(w_in, 16 * N_IN)
                if not causal:
                    band_edge(dve, chain)

                def parts_of(s, t, u):
                    g = TPB * s + t
                    chain.restart()
                    dve.wait_ge(parts_ready, g + 2)
                    dve.wait_ge(qkv_out, g + 3)
                    out = src = qkv[:, u, 0:qk_w].rearrange("p (h d) -> p h d", d=DH)
                    if causal:
                        half = DH // 2
                        cos, sin = (rope[:, t, i, :].unsqueeze(1) for i in range(2))
                        out = placed[:, :, :]
                        chain.post(dve.tensor_tensor(rot[:, :, 0:half], src[:, :, half:DH],
                                                     sin[:, :, 0:half].broadcast_to([P, nh, half]),
                                                     ALU.mult))
                        chain.post(dve.tensor_tensor(rot[:, :, half:DH], src[:, :, 0:half],
                                                     sin[:, :, half:DH].broadcast_to([P, nh, half]),
                                                     ALU.mult))
                        chain(dve.tensor_tensor(out, src, cos.broadcast_to([P, nh, DH]), ALU.mult))
                        chain(dve.tensor_tensor(out, out, rot[:, :, :], ALU.add))
                    chain(dve.tensor_copy(parts[:, 0], out))
                    chain(dve.tensor_tensor(rest[:, :, :], out, parts[:, 0], ALU.subtract))
                    chain(dve.tensor_copy(parts[:, 1], rest[:, :, :]))
                    chain(dve.tensor_tensor(parts[:, 2], rest[:, :, :], parts[:, 1], ALU.subtract))
                    dve.wait_ge(qkT, g + 1)
                    slot = 0
                    for part, n in ((0, 3), (1, 2), (2, 1)):
                        chain.post(dve.tensor_copy(
                            Qs[:, u, :, slot:slot + n, :],
                            parts[:, part, 0:NHP, :].unsqueeze(2)
                            .broadcast_to([P, NHP, n, DH])))
                        slot += n
                    for part, slots in ((0, slice(0, 4, 3)), (1, slice(1, 5, 3)),
                                        (2, slice(2, 3, 1)), (0, slice(5, 6, 1))):
                        n = len(range(*slots.indices(6)))
                        ins = dve.tensor_copy(Ks[:, u, :, slots, :],
                                              parts[:, part, NHP:nh, :].unsqueeze(2)
                                              .broadcast_to([P, nk, n, DH]))
                        if slots.start < 5:
                            chain.post(ins)
                    chain.join()
                    ins.then_inc(parts_ready, 1)

                def keys_out(s, t, u):
                    dve.wait_ge(qkT, TPB * s + t + 3)
                    dve.tensor_scalar(KT[0:KS, :, bass.ds(P * t, P)],
                                      PS[0:KS, 5 + 2 * u, 0:nk * P // 2].bitcast(BF16)
                                      .rearrange("p (h n) -> p h n", h=nk), 1.0, None, ALU.mult)\
                        .then_inc(k_out, 1)

                def attend(s, b, half):
                    chain.restart()
                    if not causal:
                        chain(dve.tensor_scalar(mix_now, mix_w[:, bass.ds(2 * half, 2), :], 1.0,
                                                None, ALU.mult))
                    dve.wait_ge(y_init, TPB * b + TPB)
                    for what, *x in order:
                        if what == "max":
                            n, q, hh, (i, k0, width, *_) = x
                            c = k0 // CH if causal else 0
                            dve.wait_ge(mx, MAXES * s + n + 1)
                            dve.tensor_reduce(
                                mxp[:, i % QB, hh:hh + per, c],
                                PS[:, 4 + n % 2, :].rearrange("p (h n) -> p h n", h=per)
                                [:, :, 0:width], AX.X, ALU.max)\
                                .then_inc(mx_read, 1)
                            done = n
                        elif what == "parts":
                            q, = x
                            J = blocks[q][1]
                            width = J + 1 if causal else 1
                            dve.wait_ge(mx_read, MAXES * s + done + 3)
                            m, r = negm[:, 0, :], negm[:, 1, :]
                            chain(dve.tensor_reduce(
                                m, mxp[:, :, :, 0:width].rearrange("p i h c -> p (i h) c"),
                                AX.X, ALU.max, negate=True))
                            chain(dve.tensor_copy(stg[:, :, KS], m))
                            chain(dve.tensor_tensor(r, m, stg[:, :, KS], ALU.subtract))
                            chain(dve.tensor_copy(stg[:, :, KS + 1], r))
                            dve.tensor_tensor(stg[:, :, KS + 2], r, stg[:, :, KS + 1],
                                              ALU.subtract).then_inc(m_parts, 1)
                        elif what == "inv":
                            use, q, i = x
                            if i == 0:
                                dve.wait_ge(used, USES * s + use + 1)
                            part = slice(CH // INVS * i, CH // INVS * (i + 1))
                            ins = dve.reciprocal(rden[:, part], PS[:, 7, part])
                            if i == INVS - 1:
                                ins.then_inc(read, 1)
                        elif what == "out":
                            use, q, r = x
                            J = blocks[q][1]
                            dve.wait_ge(used, USES * s + use + 1)
                            dst = Y[:, QB * J + 2 * r:QB * J + 2 * r + 2, :]
                            dve.tensor_tensor(dst, dst, PS[:, 7, :]
                                              .rearrange("p (t d) -> p t d", t=2), ALU.add)\
                                .then_inc(read, 1)
                    dve.wait_ge(read, USES * s + USES + 1)

                with dve.Fori(0, B) as b:
                    with dve.Fori(0, 2) as half:
                        s = 2 * b + half
                        parts_of(s, 0, 0)
                        with dve.Fori(0, TPB // 2 - 1) as it:
                            for u in range(2):
                                parts_of(s, 2 * it + u + 1, 1 - u)
                                keys_out(s, 2 * it + u, u)
                        parts_of(s, TPB - 1, 1)
                        keys_out(s, TPB - 2, 0)
                        keys_out(s, TPB - 1, 1)
                        attend(s, b, half)
                    chain.restart()

                    def leave(t):
                        tile = TPB * b + t
                        row_stats(dve, k, tile, Y[:, t, :]).then_inc(stat, 1)
                        if causal:
                            dve.tensor_scalar(X[:, tile, :], Y[:, t, :], 1.0, None, ALU.mult)\
                                .then_inc(x_out, 1)

                    each_tile(dve, leave, TPB)
                    if not causal:
                        dve.wait_ge(stat, TPB * b + TPB)
                        finish_norm_dve(dve, k, chain, var_ready, std_ready, b + 1, TPB * b, TPB)
                        each_tile(dve, lambda t: normalised(
                            dve, k, X[:, TPB * b + t, :], TPB * b + t, Y[:, t, :])
                            .then_inc(x_out, 1), TPB)

            @block.tensor
            def _(pe):
                pe.sem_inc(hnT, 2)
                pe.sem_inc(qkv_mm, 2)
                pe.sem_inc(qkT, 2)
                pe.sem_inc(pv, 2)
                pe.wait_ge(w_in, 16 * N_IN)
                if not causal:
                    for b in range(B):
                        mm = pe.matmul(PS[:, 6, D * b:D * b + D], last_two[:, :],
                                       X[:, TPB * b + TPB - 1, :], start=(b == 0), stop=True,
                                       skip_group_check=True)
                    mm.then_inc(edge_mm, 1)

                def front(s, half, t, u):
                    g = TPB * s + t
                    pe.wait_ge(hn_ready, g + 1)
                    pe.wait_ge(hT_ready, g + 1)
                    for kd in range(KD):
                        mm = pe.transpose(PS[:, u, P * kd:P * kd + P], hn[:, u, P * kd:P * kd + P],
                                          k.ident[:, :])
                    mm.then_inc(hnT, 1)
                    pe.wait_ge(hT_ready, g + 3)
                    pe.wait_ge(qkv_out, g + 1)
                    for kd in range(KD):
                        mm = pe.matmul(PS[:, 2 + u, 0:all_w], hT[:, u, kd, :], qkv_w[:, kd, half, :],
                                       start=(kd == 0), stop=(kd == KD - 1) and causal)
                    if not causal:
                        mm = pe.matmul(PS[:, 2 + u, 0:all_w], ones_row[:, :], bias[:, half, :],
                                       start=False, stop=True)
                    mm.then_inc(qkv_mm, 1)

                def back(s, t, u):
                    g = TPB * s + t
                    pe.wait_ge(parts_ready, g + 3)
                    pe.wait_ge(q_out, g + 1)
                    pe.wait_ge(k_out, g + 1)
                    for h in range(NHP):
                        pe.transpose(PS[0:KS, 4 + 2 * u, P // 2 * h:P // 2 * (h + 1)].bitcast(BF16),
                                     Qs[:, u, h, :, :].rearrange("p s d -> p (s d)"),
                                     k.identb[:, :])
                    for h in range(nk):
                        mm = pe.transpose(
                            PS[0:KS, 5 + 2 * u, P // 2 * h:P // 2 * (h + 1)].bitcast(BF16),
                            Ks[:, u, h, :, :].rearrange("p s d -> p (s d)"), k.identb[:, :])
                    mm.then_inc(qkT, 1)

                def attend(s, half):
                    if not causal:
                        pe.wait_ge(band_ready, 1)
                    pe.wait_ge(q_out, TPB * s + TPB + 2)
                    pe.wait_ge(k_out, TPB * s + TPB + 2)
                    for what, *x in order:
                        if what == "max":
                            n, q, hh, (i, k0, width, m0, m_width, m_at) = x
                            pe.wait_ge(mx_read, MAXES * s + n + 1)
                            for at in range(per):
                                h = 4 * blocks[q][0] + hh + at
                                bank = PS[:, 4 + n % 2, CH // per * at:CH // per * (at + 1)]
                                mm = pe.matmul(bank[:, 0:width], QT[0:KS, h, P * i:P * i + P],
                                               KT[0:KS, kmap(h), k0:k0 + width],
                                               start=True, stop=not m_width, skip_group_check=True)
                                if m_width:
                                    mm = pe.matmul(bank[:, m0:m0 + m_width], k.identb[:, :],
                                                   mask_q[:, m_at:m_at + m_width],
                                                   start=False, stop=True, skip_group_check=True)
                            mm.then_inc(mx, 1)
                        elif what == "turn":
                            n, q, (j, first, width, m_width, m_at), pair = x
                            g, J = blocks[q]
                            if j == turned[J][0][0] and pair == 0:
                                rows = [y[1] for y in order if y[0] == "rows" and y[2] == q]
                                pe.wait_ge(read, USES * s + rows[-1] + 2)
                            pe.wait_ge(ex, 2 * TURNS * s + 2 * n + pair + 1)
                            for h2 in range(2):
                                h = 4 * g + 2 * pair + h2
                                bank = PS[:, 2 * pair + h2, :]
                                mm = pe.matmul(bank[:, first:first + width],
                                               KT[:, kmap(h), P * j:P * j + P],
                                               QT[:, h, CH * J + first:CH * J + first + width],
                                               start=True, stop=not m_width)
                                if m_width:
                                    mm = pe.matmul(bank[:, first:first + m_width],
                                                   k.identb[:, :], mask_k[:, m_at:m_at + m_width],
                                                   start=False, stop=True)
                            mm.then_inc(st, 1)
                        elif what == "pv":
                            n, q, (j, first, width, _, _), opens, closes = x
                            g = blocks[q][0]
                            pe.wait_ge(ex, 2 * TURNS * s + 2 * n + 4)
                            if opens:
                                pe.wait_ge(o_out, NB * s + q + 1)
                            for hh in range(4):
                                mm = pe.matmul(PS[32 * hh:32 * hh + 32, 6, first:first + width],
                                               Vt[:, j, kmap(4 * g + hh), :],
                                               pT[:, n % 2, hh, 0:width], start=opens,
                                               stop=closes, skip_group_check=True)
                            mm.then_inc(pv, 1)
                        elif what == "rows":
                            use, q, r = x
                            pe.wait_ge(m_parts, NB * s + q + 1)
                            pe.wait_ge(read, USES * s + use + 1)
                            for i in range(8):
                                mm = pe.transpose(
                                    PS[0:KM, 7, P // 2 * i:P // 2 * (i + 1)].bitcast(BF16),
                                    stg[:, 8 * r + i, :], k.identb[:, :])
                            mm.then_inc(used, 1)
                        elif what == "den":
                            use, q = x
                            pe.wait_ge(o_out, NB * s + q + 2)
                            pe.wait_ge(read, USES * s + use + 1)
                            pe.matmul(PS[:, 7, :], spread[:, :], Ot, start=True, stop=True)\
                                .then_inc(used, 1)
                        elif what == "mix":
                            use, q = x
                            pe.wait_ge(normed, NB * s + q + 2)
                            pe.wait_ge(read, USES * s + use + 1)
                            pe.matmul(PS[:, 7, :], mix_now[:, blocks[q][0], :], On, start=True,
                                      stop=True).then_inc(used, 1)
                        elif what == "out":
                            use, q, r = x
                            pe.wait_ge(normed, NB * s + q + 2)
                            pe.wait_ge(read, USES * s + use + 1)
                            src = On if causal else Om
                            for t in range(2):
                                mm = pe.matmul(PS[:, 7, D * t:D * t + D],
                                               src[:, P * (2 * r + t):P * (2 * r + t + 1)],
                                               o_w[:, 2 * half + blocks[q][0], :],
                                               start=(t == 0), stop=(t == 1),
                                               skip_group_check=True)
                            mm.then_inc(used, 1)
                    pe.wait_ge(read, USES * s + USES + 1)

                with pe.Fori(0, B) as b:
                    with pe.Fori(0, 2) as half:
                        s = 2 * b + half
                        two_ahead(pe, lambda t, u: front(s, half, t, u),
                                  lambda t, u: back(s, t, u))
                        attend(s, half)


def stage_causal_attention(k):
    stage_attention(k, True)


def stage_band_attention(k):
    stage_attention(k, False)


def stage_mlp(k, kind):
    nc, a, X, PS = k.nc, k.a, k.X, k.PS
    swiglu, expert, gelu = (kind == x for x in ("swiglu", "expert", "gelu"))
    tag = "f" if gelu else kind[0]
    with ExitStack() as ctx:
        sb = k.sb(ctx)

        def weights(arena, at, c):
            return arena[:, at:at + 2048].rearrange("p (c n) -> p c n", c=c)

        if swiglu:
            w1, w3, w2 = [weights(k.WA, 0, KD)] * 2, weights(k.WA, 2048, KD), \
                [weights(k.WA, 4096, NF)] * 2
        elif expert:
            w1, w2 = ([weights(k.WB, 4096 * u + at, c) for u in range(2)]
                      for at, c in ((0, KD), (2048, NF)))
        else:
            w1, w2 = [weights(k.WB, 0, KD)] * 2, [weights(k.WB, 2048, NF)] * 2
        if not swiglu:
            nb = E if expert else 1
            b1r = sb(tag + "_b1r", [nb * NF, P], F32)
            b1 = sb(tag + "_b1", [P, nb * NF], F32)
            b2 = sb(tag + "_b2", [1, nb, D], F32)
            ones_row = sb(tag + "_ones", [1, P], F32)
        if not gelu:
            gb = sb(tag + "_gb", [P, 2, KD], F32)
        hn = sb(tag + "_hn", [P, 2, TPC, D], F32)
        hT = sb(tag + "_hT", [P, 2, KD, CH], F32)
        G = sb(tag + "_G", [P, NF, CH], F32)
        sa = sb(tag + "_sa", [P, 2, CH], F32)
        io = sb(tag + "_io", [P, 2, TPC, D], F32)
        (w_in, b_in, b_T, ones_set, hn_ready, hnT, hT_ready, up, silu, G_ready, down, x_sum, x_out,
         var_ready, std_ready, renorm, freed, combined, stat) = k.sems(
            tag, "w_in b_in b_T ones hn_ready hnT hT_ready up silu G_ready down x_sum x_out "
            "var std renorm freed combined stat")
        w_e, rows_in = ([k.sem(f"{tag}_{n}{u}") for u in range(2)] for n in ("w_e", "rows"))
        stored = k.pool_dma_sem(tag + "_stored") if expert else k.sem(tag + "_stored")
        gathered = [k.pool_dma_sem(f"{tag}_gathered{u}") for u in range(NT // TPC)] \
            if expert else []

        def chunks(eng, body):
            for u in range(2):
                body(u, 0, u, u == 0, False)
            with eng.Fori(1, NC // 2 - 1) as it:
                for u in range(2):
                    body(2 * it + u, it, u, False, False)
            for u in range(2):
                body(NC - 2 + u, NC // 2 - 1, u, False, u == 1)

        norms = 1 if swiglu else 0

        with nc.Block() as block:
            @block.sync
            def _(sp):
                if swiglu:
                    for dst, src in ((w1[0], "L0_attn_w1"), (w3, "L0_attn_w3"),
                                     (w2[0], "L0_attn_w2")):
                        load_weight(sp, dst, a[src], w_in)
                if gelu:
                    load_weight(sp, w1[0], a["L1_ffn_w1"], w_in)
                    load_weight(sp, w2[0], a["L1_ffn_w2"], w_in)
                else:
                    for i, name in enumerate(("L0_attn_ln3_g", "L0_attn_ln3_b") if swiglu else
                                             ("L0_ffn_ln_g", "L0_ffn_ln_b")):
                        load_columns(sp, gb[:, i, :], a[name], b_in)
                if expert:
                    sp.dma_start(b1r[:, :], a["L0_ffn_b1"].rearrange("e (f p) -> (e f) p", p=P))\
                        .then_inc(b_in, 16)
                    sp.dma_start(b2[:, :, :], a["L0_ffn_b2"].rearrange("(one e) d -> one e d", one=1))\
                        .then_inc(b_in, 16)
                    w1x = a["L0_ffn_w1"].rearrange("e (c p) n -> e p c n", p=P)
                    w2x = a["L0_ffn_w2"].rearrange("e (c p) n -> e p c n", p=P)
                    rows = k.sorted.rearrange("(c j p) d -> c p j d", p=P, j=TPC)
                    with sp.Fori(0, NC // 2) as it:
                        for u in range(2):
                            c = 2 * it + u
                            sp.wait_ge(down, TPC * c + TPC)
                            sp.dma_start(w1[u], w1x[c]).then_inc(w_e[u], 16)
                            sp.dma_start(w2[u], w2x[c]).then_inc(w_e[u], 16)
                            sp.dma_start(hn[:, u, :, :], rows[c]).then_inc(rows_in[u], 16)
                if gelu:
                    sp.dma_start(b1r[:, :], a["L1_ffn_b1"].rearrange("(f p) -> f p", p=P))\
                        .then_inc(b_in, 16)
                    sp.dma_start(b2[:, 0, :], a["L1_ffn_b2"].rearrange("(one d) -> one d", one=1))\
                        .then_inc(b_in, 16)
                    o = k.out.rearrange("(c j p) d -> c p j d", p=P, j=TPC)
                    sp.sem_inc(freed, 2)
                    with sp.Fori(0, NC // 2) as it:
                        for u in range(2):
                            c = 2 * it + u
                            sp.wait_ge(renorm, TPC * c + TPC)
                            sp.dma_start(o[c], io[:, u, :, :]).then_inc(stored, 16)
                            sp.wait_ge(stored, 16 * c + 16)
                            sp.sem_inc(freed, 1)
                if swiglu:
                    x = a["L0_attn_x"].rearrange("b (c j p) d -> (b c) p j d", p=P, j=TPC)
                    with sp.Fori(0, NC // 2) as it:
                        for u in range(2):
                            c = 2 * it + u
                            sp.wait_ge(x_out, TPC * c + TPC)
                            sp.dma_start(io[:, u, :, :], x[c]).then_inc(rows_in[u], 16)

            @block.gpsimd
            def _(pool):
                if not swiglu:
                    pool.memset(ones_row[:, :], 1.0).then_inc(ones_set, 1)
                if swiglu:
                    with pool.Fori(0, NC // 2) as it:
                        for u in range(2):
                            c = 2 * it + u
                            for j in range(TPC):
                                pool.wait_ge(rows_in[u], 16 * it + 16)
                                pool.tensor_tensor(io[:, u, j, :], io[:, u, j, :],
                                                   X[:, TPC * c + j, :], ALU.add)\
                                    .then_inc(x_sum, 1)
                if expert:
                    outs = k.hidden.rearrange("(c j p) d -> c p j d", p=P, j=TPC)
                    pool.sem_inc(freed, 2)
                    with pool.Fori(0, NC // 2) as it:
                        for u in range(2):
                            c = 2 * it + u
                            pool.wait_ge(x_out, TPC * c + TPC + 8)
                            pool.dma_start(outs[c], io[:, u, :, :]).then_inc(stored, 16)
                            pool.wait_ge(stored, 16 * c + 16)
                            pool.sem_inc(freed, 1)
                    for t in range(NT):
                        if t == 0:
                            pool.wait_ge(down, TPC * NC + 8)
                            pool.wait_ge(stored, 16 * NC)
                        if t >= NT // 2:
                            pool.wait_ge(combined, t - NT // 2 + 1)
                        pool.indirect_dma_start(
                            G[:, t % 16 // 2, D * (t % 2):D * (t % 2) + D], None, k.hidden,
                            bass.IndirectOffsetOnAxis(ap=k.slots[:, t:t + 1], axis=0))\
                            .then_inc(gathered[t // TPC], 16)

            @block.scalar
            def _(act):
                act.sem_inc(silu, 2)
                if not swiglu:
                    act.sem_inc(G_ready, 2)
                if swiglu:
                    finish_norm_act(act, k, var_ready, std_ready)
                if not gelu:
                    act.wait_ge(b_in, 16 * (4 if expert else 2))
                if not swiglu:
                    act.wait_ge(b_T, 2)

                def transposed(c, u):
                    for kd in range(KD):
                        act.wait_ge(hnT, KD * c + kd + 1)
                        if gelu:
                            e = act.activation(hT[:, u, kd, :], PS[:, 4 + kd, :], ACT.Copy)
                        else:
                            e = act.activation(hT[:, u, kd, :], PS[:, 4 + kd, :], ACT.Identity,
                                               scale=gb[:, 0, kd:kd + 1], bias=gb[:, 1, kd:kd + 1])
                        e.then_inc(hT_ready, 1)

                def body(c, it, u, first, last):
                    for f in range(NF):
                        act.wait_ge(up, NF * c + f + 1)
                        if swiglu:
                            act.wait_ge(G_ready, NF * c + f + 1)
                            act.activation(sa[:, f % 2, :], PS[:, f % 2, :], ACT.Silu)\
                                .then_inc(silu, 1)
                        else:
                            at = NF * c + f if expert else f
                            act.activation(G[:, f, :], PS[:, f % 2, :],
                                           ACT.Gelu_apprx_tanh if expert else ACT.Gelu,
                                           bias=b1[:, bass.ds(at, 1)]).then_inc(G_ready, 1)
                    if not last:
                        transposed(c + 1, 1 - u)
                    if not expert and not first:
                        finish_norm_act(act, k, var_ready, std_ready, norms + c, TPC)

                transposed(0, 0)
                chunks(act, body)
                if expert:
                    finish_norm_act(act, k, var_ready, std_ready)
                else:
                    finish_norm_act(act, k, var_ready, std_ready, norms + NC, TPC)

            @block.vector
            def _(dve):
                chain = Chain(dve, k.chain_v)
                chain.restart()
                dve.sem_inc(x_out, 8)
                if swiglu:
                    dve.sem_inc(G_ready, 2)
                    finish_norm_dve(dve, k, chain, var_ready, std_ready)
                else:
                    dve.wait_ge(b_T, 1)
                    dve.tensor_copy(b1[:, :], PS[:, 7, 0:nb * NF]).then_inc(b_T, 1)

                def rows(c, u):
                    for j in range(TPC):
                        tile = TPC * c + j
                        if swiglu:
                            ins = normalised(dve, k, hn[:, u, j, :], tile)
                        else:
                            ins = dve.tensor_scalar(hn[:, u, j, :], X[:, tile, :], 1.0, None,
                                                    ALU.mult)
                        ins.then_inc(hn_ready, 1)

                def body(c, it, u, first, last):
                    for f in range(NF):
                        if swiglu:
                            dve.wait_ge(silu, NF * c + f + 3)
                            dve.tensor_tensor(G[:, f, :], sa[:, f % 2, :], PS[:, 2 + f % 2, :],
                                              ALU.mult).then_inc(G_ready, 1)
                        if f == 3 and not last and not expert:
                            rows(c + 1, 1 - u)
                    if not expert and not first:
                        renormalise(c - 1, 1 - u)
                    for j in range(TPC):
                        tile = TPC * c + j
                        src = PS[:, 6 + j % 2, 0:D]
                        dve.wait_ge(down, TPC * c + j + 9)
                        if swiglu:
                            dve.wait_ge(x_sum, TPC * c + j + 1)
                            ins = dve.tensor_tensor(X[:, tile, :], src, io[:, u, j, :], ALU.add)
                        elif expert:
                            dve.wait_ge(freed, c + 1)
                            ins = dve.tensor_copy(io[:, u, j, :], src)
                        else:
                            ins = dve.tensor_tensor(X[:, tile, :], src, X[:, tile, :], ALU.add)
                        ins.then_inc(x_out, 1)
                        if swiglu and not first:
                            row_stats(dve, k, tile - TPC)
                    if not expert:
                        dve.wait_ge(x_out, TPC * c + TPC + 8)
                        for j in range(TPC):
                            row_stats(dve, k, TPC * c + j).then_inc(stat, 1)
                        chain.restart()
                        dve.wait_ge(stat, TPC * c + TPC)
                        variances(dve, k, chain, var_ready, TPC * c, TPC)

                def renormalise(c, u):
                    chain.restart()
                    inverse_roots(dve, k, chain, std_ready, norms + c + 1, TPC * c, TPC)
                    if gelu:
                        dve.wait_ge(freed, c + 1)
                    for j in range(TPC):
                        normalised(dve, k, io[:, u, j, :] if gelu else X[:, TPC * c + j, :],
                                   TPC * c + j).then_inc(renorm, 1)
                    if swiglu:
                        dve.wait_ge(renorm, TPC * c + TPC)

                if not expert:
                    rows(0, 0)
                chunks(dve, body)
                if expert:
                    for t in range(NT):
                        dve.wait_ge(gathered[t // TPC], 16 * TPC)
                        dve.scalar_tensor_tensor(
                            out=X[:, t, :], in0=X[:, t, :], scalar=2.0,
                            in1=G[:, t % 16 // 2, D * (t % 2):D * (t % 2) + D],
                            op0=ALU.mult, op1=ALU.add).then_inc(combined, 1)
                        if t:
                            dve.wait_ge(combined, t)
                            row_stats(dve, k, t - 1).then_inc(stat, 1)
                    dve.wait_ge(combined, NT)
                    row_stats(dve, k, NT - 1).then_inc(stat, 1)
                    chain.restart()
                    dve.wait_ge(stat, NT)
                    finish_norm_dve(dve, k, chain, var_ready, std_ready)
                    each_tile(dve, lambda t: normalised(dve, k, X[:, t, :], t))
                else:
                    renormalise(NC - 1, 1)
                if swiglu:
                    with dve.Fori(NT - TPC, NT) as t:
                        row_stats(dve, k, t)
                if gelu:
                    dve.wait_ge(stored, 16 * NC)

            @block.tensor
            def _(pe):
                pe.sem_inc(down, 8)
                if not swiglu:
                    pe.wait_ge(b_in, 16 * (4 if expert else 2))
                    pe.wait_ge(ones_set, 1)
                    pe.transpose(PS[:, 7, 0:nb * NF], b1r[:, :], k.ident[0:nb * NF, 0:nb * NF])\
                        .then_inc(b_T, 1)
                    pe.wait_ge(b_T, 2)
                if not expert:
                    pe.wait_ge(w_in, 16 * (3 if swiglu else 2))

                def transpose(c, it, u):
                    if expert:
                        pe.wait_ge(rows_in[u], 16 * it + 16)
                    else:
                        pe.wait_ge(hn_ready, TPC * c + TPC)
                    for kd in range(KD):
                        for j in range(TPC):
                            mm = pe.transpose(PS[:, 4 + kd, P * j:P * j + P],
                                              hn[:, u, j, P * kd:P * kd + P], k.ident[:, :])
                        mm.then_inc(hnT, 1)

                def body(c, it, u, first, last):
                    if expert:
                        pe.wait_ge(w_e[u], 32 * it + 32)
                    pe.wait_ge(hT_ready, KD * c + KD)
                    for f in range(NF):
                        pe.wait_ge(G_ready, NF * c + f + 1)
                        if swiglu:
                            pe.wait_ge(silu, NF * c + f + 1)
                        for w, bank in ((w1[u], f % 2), (w3, 2 + f % 2)) if swiglu else \
                                ((w1[u], f % 2),):
                            for kd in range(KD):
                                mm = pe.matmul(PS[:, bank, :], w[:, kd, P * f:P * f + P],
                                               hT[:, u, kd, :], start=(kd == 0),
                                               stop=(kd == KD - 1))
                        mm.then_inc(up, 1)
                    if not last:
                        transpose(c + 1, it if u == 0 else it + 1, 1 - u)
                    pe.wait_ge(G_ready, NF * c + NF + 2)
                    for j in range(TPC):
                        pe.wait_ge(x_out, TPC * c + j + 7)
                        dst = PS[:, 6 + j % 2, 0:D]
                        for f in range(NF):
                            mm = pe.matmul(dst, G[:, f, P * j:P * j + P], w2[u][:, f, :],
                                           start=(f == 0), stop=(f == NF - 1 and swiglu))
                        if not swiglu:
                            mm = pe.matmul(dst, ones_row[:, :], b2[:, c if expert else 0, :],
                                           start=False, stop=True)
                        mm.then_inc(down, 1)

                transpose(0, 0, 0)
                chunks(pe, body)


def stage_swiglu(k):
    stage_mlp(k, "swiglu")


def stage_experts(k):
    stage_mlp(k, "expert")


def stage_final(k):
    stage_mlp(k, "gelu")


FAN = 15
STEPS = (4096, 256, 16, 1)


def stage_route(k):
    nc, a, X, PS = k.nc, k.a, k.X, k.PS
    with ExitStack() as ctx:
        sb = k.sb(ctx)
        gb = sb("r_gb", [P, 2, KD], F32)
        cent = sb("r_cent", [E, D], F32)
        centT = sb("r_centT", [P, KD, E], F32)
        hn = sb("r_hn", [P, 2, D], F32)
        hT = sb("r_hT", [P, 2, KD, P], F32)
        XN = sb("r_XN", [P, NT, D], F32)
        score = sb("r_score", [P, E, NT], F32)
        bits = sb("r_bits", [P, E, NT], U32)
        high = sb("r_high", [P, E, NT], F32)
        low = sb("r_low", [P, E, NT], F32)
        neg = sb("r_neg", [P, E, NT], F32)
        fold = sb("r_fold", [P, E, NT], F32)
        grid = sb("r_grid", [P, len(STEPS), FAN], F32)
        before = sb("r_before", [P, P], F32)
        onesb = sb("r_onesb", [P, P], BF16)
        ones = sb("r_ones", [P, NT], F32)
        left = sb("r_left", [P, NT], F32)
        slot = sb("r_slot", [P, NT], F32)
        base = sb("r_base", [P, 1], F32)
        key = sb("r_key", [P, NT], F32)
        tie = sb("r_tie", [P, NT], F32)
        sel = sb("r_sel", [P, NT], F32)
        pick = sb("r_pick", [P, NT], BF16)
        run = sb("r_run", [P, NT], F32)
        reach = sb("r_reach", [P, FAN, NT], BF16)
        count = sb("r_count", [P, FAN], BF16)
        hit = sb("r_hit", [P, FAN], F32)
        one = sb("r_one", [P, 8], F32)
        need, found, n_hit, total = (one[:, i:i + 1] for i in range(4))
        (w_in, var_ready, std_ready, c_T, hn_ready, hnT, hT_ready, sc_mm, asked, told,
         summed, ranked, slots_ready) = k.sems(
            "r", "w_in var std c_T hn_ready hnT hT_ready sc_mm asked told summed ranked slots")
        scattered = k.pool_dma_sem("r_scattered")
        ASKS = 2 * (len(STEPS) + 1) + 1

        with nc.Block() as block:
            @block.sync
            def _(sp):
                for i, name in enumerate(("L0_ffn_ln_g", "L0_ffn_ln_b")):
                    load_columns(sp, gb[:, i, :], a[name], w_in)
                for dst, src in ((cent[:, :], "L0_ffn_centroids"), (grid[:, :, :], "c_grid"),
                                 (before[:, :], "c_before")):
                    sp.dma_start(dst, a[src]).then_inc(w_in, 16)

            @block.gpsimd
            def _(pool):
                for t in range(NT):
                    if t == 0:
                        pool.wait_ge(slots_ready, 1)
                    pool.indirect_dma_start(
                        k.sorted, bass.IndirectOffsetOnAxis(ap=k.slots[:, t:t + 1], axis=0),
                        XN[:, t, :], None).then_inc(scattered, 16)
                pool.wait_ge(scattered, 16 * NT)

            @block.scalar
            def _(act):
                act.sem_inc(hT_ready, 2)
                finish_norm_act(act, k, var_ready, std_ready)
                act.wait_ge(w_in, 16 * 5)
                with act.Fori(0, NT // 2) as it:
                    for u in range(2):
                        t = 2 * it + u
                        act.wait_ge(hnT, t + 3)
                        act.wait_ge(sc_mm, t + 1)
                        for kd in range(KD):
                            e = act.activation(hT[:, u, kd, :], PS[:, u, P * kd:P * kd + P],
                                               ACT.Identity, scale=gb[:, 0, kd:kd + 1],
                                               bias=gb[:, 1, kd:kd + 1])
                        e.then_inc(hT_ready, 1)

            @block.vector
            def _(dve):
                chain = Chain(dve, k.chain_v)
                chain.restart()
                finish_norm_dve(dve, k, chain, var_ready, std_ready)
                dve.wait_ge(w_in, 16 * 5)
                dve.wait_ge(c_T, 1)
                dve.tensor_copy(centT[:, :, :], PS[:, 6, 0:KD * E].rearrange("p (c e) -> p c e", c=KD))\
                    .then_inc(c_T, 1)
                with dve.Fori(0, NT // 2) as it:
                    for u in range(2):
                        t = 2 * it + u
                        dve.wait_ge(hnT, t + 1)
                        normalised(dve, k, hn[:, u, :], t).then_inc(hn_ready, 1)
                        normalised(dve, k, XN[:, t, :], t)
                dve.wait_ge(sc_mm, NT + 2)
                every = (slice(None),) * 3
                chain.restart()
                chain(dve.tensor_copy(score[every],
                                      PS[:, 2, 0:E * NT].rearrange("p (t e) -> p e t", e=E)))
                raw = score[:, :, :].bitcast(U32)
                chain(dve.tensor_scalar(bits[every], raw, 16, None, ALU.logical_shift_right))
                chain(dve.tensor_copy(high[every], bits[every]))
                chain(dve.tensor_scalar(bits[every], raw, 0xFFFF, None, ALU.bitwise_and))
                chain.post(dve.tensor_copy(low[every], bits[every]))
                chain.post(dve.tensor_scalar(neg[every], high[every], 32768.0, None, ALU.is_ge))
                chain.post(dve.tensor_scalar(fold[every], high[every], -2.0, 32767.0, ALU.mult,
                                             ALU.add))
                chain.join()
                chain(dve.tensor_tensor(fold[every], fold[every], neg[every], ALU.mult))
                chain(dve.scalar_tensor_tensor(out=high[every], in0=high[every], scalar=32769.0,
                                               in1=fold[every], op0=ALU.add, op1=ALU.add))
                chain(dve.tensor_scalar(fold[every], low[every], -2.0, 65535.0, ALU.mult, ALU.add))
                chain(dve.tensor_tensor(fold[every], fold[every], neg[every], ALU.mult))
                chain(dve.scalar_tensor_tensor(out=low[every], in0=low[every], scalar=1.0,
                                               in1=fold[every], op0=ALU.add, op1=ALU.add))
                chain.post(dve.memset(ones[:, :], 1.0))
                chain.post(dve.memset(onesb[:, :], 1.0))
                chain.post(dve.memset(left[:, :], 1.0))
                chain.post(dve.memset(slot[:, :], 0.0))
                chain.post(dve.memset(base[:, :], -1.0))
                chain.join()

                def give_slots(turn):
                    chain(dve.tensor_tensor_scan(run[:, :], ones[:, :], sel[:, :], 0.0, ALU.mult,
                                                 ALU.add))
                    dve.tensor_copy(total, run[:, NT - 1:NT]).then_inc(summed, 1)
                    dve.wait_ge(ranked, turn)
                    chain(dve.tensor_copy(n_hit, PS[:, 4, 0:1]))
                    chain(dve.tensor_scalar(run[:, :], run[:, :], n_hit, base[:, :], ALU.add,
                                            ALU.add))
                    chain(dve.tensor_tensor(run[:, :], run[:, :], sel[:, :], ALU.mult))
                    chain.post(dve.tensor_tensor(slot[:, :], slot[:, :], run[:, :], ALU.add))
                    chain.post(dve.tensor_tensor(left[:, :], left[:, :], sel[:, :], ALU.subtract))
                    chain.post(dve.tensor_scalar(base[:, :], base[:, :], float(CAP), None, ALU.add))
                    chain.join()

                with dve.Fori(0, E - 1) as e:
                    chain.restart()
                    asks = [0]

                    def ask(ins):
                        ins.then_inc(asked, 1)
                        asks[0] += 1
                        dve.wait_ge(told, ASKS * e + asks[0])

                    def search(keys):
                        chain(dve.memset(found, 1.0))
                        for i, step in enumerate(STEPS):
                            chain(dve.scalar_tensor_tensor(
                                out=reach[:, :, :],
                                in0=keys.unsqueeze(1).broadcast_to([P, FAN, NT]), scalar=found,
                                in1=grid[:, i, :].unsqueeze(2).broadcast_to([P, FAN, NT]),
                                op0=ALU.subtract, op1=ALU.is_ge))
                            with nc.allow_low_precision(reason="counts up to 32 are exact"):
                                ask(dve.tensor_reduce(count[:, :], reach[:, :, :], AX.X, ALU.add))
                            chain(dve.tensor_scalar(hit[:, :], PS[:, 0, 0:FAN], need, None,
                                                    ALU.is_ge))
                            chain(dve.tensor_reduce(n_hit, hit[:, :], AX.X, ALU.add))
                            chain(dve.scalar_tensor_tensor(
                                out=found, in0=n_hit, scalar=float(step), in1=found,
                                op0=ALU.mult, op1=ALU.add))

                    def take_above(keys):
                        chain(dve.tensor_scalar(run[:, :], keys, found, None, ALU.is_gt))
                        chain.post(dve.tensor_tensor(sel[:, :], sel[:, :], run[:, :], ALU.add))
                        ask(dve.tensor_copy(pick[:, :], run[:, :]))
                        chain(dve.tensor_reduce(total, PS[:, 1, 0:NT], AX.X, ALU.add))
                        chain(dve.tensor_tensor(need, need, total, ALU.subtract))

                    chain.post(dve.memset(need, float(CAP)))
                    chain.post(dve.memset(sel[:, :], 0.0))
                    chain(dve.tensor_tensor(key[:, :], high[:, e, :], left[:, :], ALU.mult))
                    search(key[:, :])
                    take_above(key[:, :])
                    chain(dve.tensor_scalar(tie[:, :], key[:, :], found, None, ALU.is_equal))
                    chain(dve.tensor_tensor(key[:, :], low[:, e, :], tie[:, :], ALU.mult))
                    search(key[:, :])
                    take_above(key[:, :])
                    chain(dve.tensor_scalar(tie[:, :], key[:, :], found, None, ALU.is_equal))
                    ask(dve.tensor_copy(pick[:, :], tie[:, :]))
                    chain(dve.tensor_tensor_scan(run[:, :], ones[:, :], PS[:, 1, 0:NT], 0.0,
                                                 ALU.mult, ALU.add))
                    chain(dve.tensor_tensor(run[:, :], run[:, :], PS[:, 1, 0:NT], ALU.subtract))
                    chain(dve.tensor_tensor(run[:, :], run[:, :], PS[:, 3, 0:NT], ALU.add))
                    chain(dve.tensor_scalar(run[:, :], run[:, :], need, None, ALU.is_lt))
                    chain(dve.tensor_tensor(run[:, :], run[:, :], tie[:, :], ALU.mult))
                    chain(dve.tensor_tensor(sel[:, :], sel[:, :], run[:, :], ALU.add))
                    give_slots(e + 1)
                    assert asks[0] == ASKS, asks
                chain.restart()
                chain(dve.tensor_scalar(sel[:, :], left[:, :], 1.0, None, ALU.mult))
                give_slots(E)
                dve.tensor_copy(k.slots[:, :], slot[:, :]).then_inc(slots_ready, 1)

            @block.tensor
            def _(pe):
                pe.sem_inc(hnT, 2)
                pe.sem_inc(sc_mm, 2)
                pe.wait_ge(w_in, 16 * 5)
                for kd in range(KD):
                    mm = pe.transpose(PS[:, 6, E * kd:E * kd + E], cent[:, P * kd:P * kd + P],
                                      k.ident[0:E, 0:E])
                mm.then_inc(c_T, 1)
                pe.wait_ge(c_T, 2)

                def turn_rows(t, u):
                    pe.wait_ge(hn_ready, t + 1)
                    pe.wait_ge(hT_ready, t + 1)
                    for kd in range(KD):
                        mm = pe.transpose(PS[:, u, P * kd:P * kd + P],
                                          hn[:, u, P * kd:P * kd + P], k.ident[:, :])
                    mm.then_inc(hnT, 1)

                def scores(t, u):
                    pe.wait_ge(hT_ready, t + 3)
                    for kd in range(KD):
                        mm = pe.matmul(PS[:, 2, bass.ds(E * t, E)], hT[:, u, kd, :],
                                       centT[:, kd, :], start=(kd == 0), stop=(kd == KD - 1),
                                       skip_group_check=True)
                    mm.then_inc(sc_mm, 1)

                turn_rows(0, 0)
                with pe.Fori(0, NT // 2 - 1) as it:
                    for u in range(2):
                        turn_rows(2 * it + u + 1, 1 - u)
                        scores(2 * it + u, u)
                turn_rows(NT - 1, 1)
                scores(NT - 2, 0)
                scores(NT - 1, 1)

                def taken_before(turn):
                    pe.wait_ge(summed, turn)
                    pe.matmul(PS[:, 4, 0:1], before[:, :], total, start=True, stop=True)\
                        .then_inc(ranked, 1)

                with pe.Fori(0, E - 1) as e:
                    asks = [0]

                    def tell(bank, ones_or_before, what):
                        asks[0] += 1
                        pe.wait_ge(asked, ASKS * e + asks[0])
                        pe.matmul(bank, ones_or_before, what, start=True, stop=True)\
                            .then_inc(told, 1)

                    for _ in range(2):
                        for _ in STEPS:
                            tell(PS[:, 0, 0:FAN], onesb[:, :], count[:, :])
                        tell(PS[:, 1, 0:NT], onesb[:, :], pick[:, :])
                    pe.wait_ge(asked, ASKS * e + ASKS)
                    pe.matmul(PS[:, 1, 0:NT], onesb[:, :], pick[:, :], start=True, stop=True)
                    pe.matmul(PS[:, 3, 0:NT], before[:, :], tie[:, :], start=True, stop=True)\
                        .then_inc(told, 1)
                    taken_before(e + 1)
                taken_before(E)


def program(nc, args, out, stages):
    with ExitStack() as ctx:
        core = Core(nc, ctx, args, out)
        for stage in stages:
            stage(core)
            core.end_stage()



def constants():
    p, q = np.arange(P)[:, None], np.arange(P)[None, :]
    f32 = np.float32
    rotation = f32(1.0) / np.power(f32(10000.0), np.arange(0, DH, 2, dtype=f32) / f32(DH))
    angle = np.arange(L, dtype=f32)[:, None] * rotation
    cos, sin = np.cos(angle), np.sin(angle)
    rope = np.stack([np.concatenate([cos, cos], 1), np.concatenate([-sin, sin], 1)], 1)
    last_two = np.zeros((P, P), f32)
    last_two[P - 1], last_two[P - 2] = 1, -1
    tile = (np.arange(3) - 1)[None, :, None]
    wide = {
        "c_ident": np.eye(P),
        "c_spread": p == DH + 32 * (q // 32),
        "c_rope": rope.reshape(TPB, P, 2, DH).transpose(1, 0, 2, 3),
        "c_last_two": last_two,
        "c_grid": np.broadcast_to(np.outer(STEPS, np.arange(1, FAN + 1)), (P, len(STEPS), FAN)),
        "c_before": p < q,
    }
    narrow = {
        "c_identb": np.eye(P),
        "c_ones": np.ones((1, L)),
        "c_mask_q": np.where(q > p, MASKED, 0),
        "c_mask_k": np.where(q < p, MASKED, 0),
        "c_dist": np.minimum(2 * np.abs(P * tile + q[:, None, :] - p[:, :, None]), 2 * P),
    }
    out = {n: np.ascontiguousarray(v, dtype=f32) for n, v in wide.items()}
    out.update((n, np.ascontiguousarray(v.astype(np.dtype("bfloat16")))) for n, v in narrow.items())
    return out


STAGES = (stage_mamba, stage_causal_attention, stage_swiglu, stage_route, stage_experts,
          stage_band_attention, stage_final)


def kernel(**inputs):
    import concourse.bacc as _bacc
    from concourse.bass_utils import run_bass_kernel_spmd as _run

    nc = _bacc.Bacc("TRN2", target_bir_lowering=False, num_devices=1)
    arrays, args = {}, {}
    for name, value in {**inputs, **constants()}.items():
        v = np.ascontiguousarray(value)
        v = v.reshape(v.shape or (1,))
        arrays[f"in_{name}"] = v
        args[name] = nc.dram_tensor(f"in_{name}", v.shape, mybir.dt.from_np(v.dtype),
                                    kind="ExternalInput").ap()
    out = nc.dram_tensor("out", (T, D), F32, kind="ExternalOutput").ap()
    program(nc, args, out, STAGES)
    r = _run(nc, [arrays], core_ids=[0])
    return r.results[0]["out"].reshape(B, L, D)
```
